# Optimizing a Trainium2 kernel written in Bass

```python
import numpy as np
import jax
import jax.numpy as jnp

def _softmax(x, axis=-1):
    return jax.nn.softmax(x, axis=axis)

def _gelu(x):
    return jax.nn.gelu(x, approximate=True)

def _silu(x):
    return jax.nn.silu(x)

def _sigmoid(x):
    return jax.nn.sigmoid(x)

def _layernorm(x, axis=-1, eps=1e-05):
    m = jnp.mean(x, axis=axis, keepdims=True)
    v = jnp.var(x, axis=axis, keepdims=True)
    return (x - m) / jnp.sqrt(v + eps)

def _scatter_add(tgt, idx, src, axis=0):
    return tgt.at[idx].add(src)

def _segment_sum(src, seg, n):
    return jax.ops.segment_sum(src, seg, n)
kernel_name = 'mk_prb_d4_jaxref_r8_529f4b'

def setup_inputs(seed: int=0):
    np.random.seed(seed)
    _w = jnp.asarray

    def _L0_attn_setup():
        import jax, jax.numpy as jnp
        import numpy as np
        N, L, D, A, F, B = (4, 512, 128, 128, 512, 8)
        EPS_LN = 1e-06
        EPS_Z = 1e-06

        def _layernorm(x, scale, bias):
            m = jnp.mean(x, axis=-1, keepdims=True)
            v = jnp.mean(jnp.square(x - m), axis=-1, keepdims=True)
            return (x - m) * jax.lax.rsqrt(v + EPS_LN) * scale + bias

        def _block(x, p):
            Wq, bq, Wk, bk, Wv, bv, Wo, bo, ln1_s, ln1_b, Wf1, bf1, Wf2, bf2, ln2_s, ln2_b = p
            residual = x
            q = jnp.einsum('nld,da->nla', x, Wq) + bq
            k = jnp.einsum('nld,da->nla', x, Wk) + bk
            v = jnp.einsum('nld,da->nla', x, Wv) + bv
            Q = jax.nn.elu(q) + 1.0
            K = jax.nn.elu(k) + 1.0
            KV = jnp.einsum('nsh,nsh->nh', K, v)
            Ksum = jnp.sum(K, axis=1)
            Z = 1.0 / (Q * Ksum[:, None, :] + EPS_Z)
            V = Q * KV[:, None, :] * Z
            attn = jax.nn.gelu(jnp.einsum('nla,ad->nld', V, Wo) + bo)
            x = _layernorm(attn + residual, ln1_s, ln1_b)
            residual = x
            h = jax.nn.gelu(jnp.einsum('nld,df->nlf', x, Wf1) + bf1)
            ff = jax.nn.gelu(jnp.einsum('nlf,fd->nld', h, Wf2) + bf2)
            x = _layernorm(ff + residual, ln2_s, ln2_b)
            return (x, None)
        key = jax.random.key(seed)
        ks = jax.random.split(key, 10)
        s = 0.02
        x = jax.random.normal(ks[0], (N, L, D), dtype=jnp.float32)
        Wq = jax.random.normal(ks[1], (B, D, A), dtype=jnp.float32) * s
        Wk = jax.random.normal(ks[2], (B, D, A), dtype=jnp.float32) * s
        Wv = jax.random.normal(ks[3], (B, D, A), dtype=jnp.float32) * s
        Wo = jax.random.normal(ks[4], (B, A, D), dtype=jnp.float32) * s
        Wf1 = jax.random.normal(ks[5], (B, D, F), dtype=jnp.float32) * s
        Wf2 = jax.random.normal(ks[6], (B, F, D), dtype=jnp.float32) * s
        return {'x': x, 'Wq': Wq, 'bq': jnp.zeros((B, A), jnp.float32), 'Wk': Wk, 'bk': jnp.zeros((B, A), jnp.float32), 'Wv': Wv, 'bv': jnp.zeros((B, A), jnp.float32), 'Wo': Wo, 'bo': jnp.zeros((B, D), jnp.float32), 'ln1_s': jnp.ones((B, D), jnp.float32), 'ln1_b': jnp.zeros((B, D), jnp.float32), 'Wf1': Wf1, 'bf1': jnp.zeros((B, F), jnp.float32), 'Wf2': Wf2, 'bf2': jnp.zeros((B, D), jnp.float32), 'ln2_s': jnp.ones((B, D), jnp.float32), 'ln2_b': jnp.zeros((B, D), jnp.float32)}
    _L0_attn_in = _L0_attn_setup()

    def _L0_ffn_setup():
        import jax, jax.numpy as jnp
        import numpy as np
        NHEAD = 16
        NUM_GROUPS = 4
        EXPERTS_PER_GROUP = 2
        LN_EPS = 1e-05

        def _layernorm(x, g, b):
            mu = jnp.mean(x, axis=-1, keepdims=True)
            var = jnp.mean(jnp.square(x - mu), axis=-1, keepdims=True)
            return (x - mu) * jax.lax.rsqrt(var + LN_EPS) * g + b

        def _mha(x, wi, bi, wo, bo):
            B, S, D = x.shape
            hd = D // NHEAD
            qkv = x @ wi.T + bi
            q, k, v = jnp.split(qkv, 3, axis=-1)

            def heads(t):
                return t.reshape(B, S, NHEAD, hd).transpose(0, 2, 1, 3)
            q, k, v = (heads(q), heads(k), heads(v))
            scores = jnp.einsum('bhqd,bhkd->bhqk', q, k) / jnp.sqrt(jnp.asarray(hd, x.dtype))
            attn = jax.nn.softmax(scores, axis=-1)
            o = jnp.einsum('bhqk,bhkd->bhqd', attn, v)
            o = o.transpose(0, 2, 1, 3).reshape(B, S, D)
            return o @ wo.T + bo

        def _hier_moe(x, w_group, b_group, w_expert, b_expert, w1, b1, w2, b2):
            B, S, D = x.shape
            xt = x.reshape(B * S, D)
            T = xt.shape[0]
            E = NUM_GROUPS * EXPERTS_PER_GROUP
            gp = jax.nn.softmax(xt @ w_group + b_group, axis=-1)
            g_idx = jnp.argmax(gp, axis=-1)
            g_prob = jnp.max(gp, axis=-1)
            elog = jnp.einsum('td,gde->tge', xt, w_expert) + b_expert
            ep = jax.nn.softmax(elog, axis=-1)
            ep_sel = jnp.take_along_axis(ep, g_idx[:, None, None], axis=1)[:, 0, :]
            e_idx_local = jnp.argmax(ep_sel, axis=-1)
            e_prob = jnp.max(ep_sel, axis=-1)
            flat_e = g_idx * EXPERTS_PER_GROUP + e_idx_local
            combine = jax.nn.one_hot(flat_e, E, dtype=xt.dtype) * (g_prob * e_prob)[:, None]
            h = jax.nn.relu(jnp.einsum('td,edf->etf', xt, w1) + b1[:, None, :])
            y = jnp.einsum('etf,efd->etd', h, w2) + b2[:, None, :]
            out = jnp.einsum('te,etd->td', combine, y)
            return out.reshape(B, S, D)
        key = jax.random.key(seed)
        ks = jax.random.split(key, 8)
        B, S, D, F = (2, 128, 128, 256)
        G, Epg = (NUM_GROUPS, EXPERTS_PER_GROUP)
        E = G * Epg
        sc = lambda fan: 1.0 / np.sqrt(fan)
        return {'x': jax.random.normal(ks[0], (B, S, D), jnp.float32), 'in_proj_w': jax.random.normal(ks[1], (3 * D, D), jnp.float32) * sc(D), 'in_proj_b': jnp.zeros((3 * D,), jnp.float32), 'out_proj_w': jax.random.normal(ks[2], (D, D), jnp.float32) * sc(D), 'out_proj_b': jnp.zeros((D,), jnp.float32), 'ln1_g': jnp.ones((D,), jnp.float32), 'ln1_b': jnp.zeros((D,), jnp.float32), 'ln2_g': jnp.ones((D,), jnp.float32), 'ln2_b': jnp.zeros((D,), jnp.float32), 'w_group': jax.random.normal(ks[3], (D, G), jnp.float32) * sc(D), 'b_group': jnp.zeros((G,), jnp.float32), 'w_expert': jax.random.normal(ks[4], (G, D, Epg), jnp.float32) * sc(D), 'b_expert': jnp.zeros((G, Epg), jnp.float32), 'w1': jax.random.normal(ks[5], (E, D, F), jnp.float32) * sc(D), 'b1': jnp.zeros((E, F), jnp.float32), 'w2': jax.random.normal(ks[6], (E, F, D), jnp.float32) * sc(F), 'b2': jnp.zeros((E, D), jnp.float32)}
    _L0_ffn_in = _L0_ffn_setup()

    def _L1_attn_setup():
        import jax, jax.numpy as jnp
        import numpy as np
        B, T, D = (4, 256, 128)
        H = 4
        K = D // H
        V = D // H
        M = 64
        GATE_LOGIT_NORMALIZER = 8.0
        NORM_EPS = 1e-05

        def _swish(x):
            return x * jax.nn.sigmoid(x)

        def _gsa_recurrence(q, k, v, s, g, scale):
            b, t, h, dk = q.shape
            dv = v.shape[-1]
            m = s.shape[-1]

            def step(carry, inp):
                hk, hv = carry
                q_t, k_t, v_t, s_t, g_t = inp
                ge = jnp.exp(g_t)
                hk = hk * ge[:, :, None, :] + k_t[..., :, None] * s_t[..., None, :]
                logits = jnp.einsum('bhk,bhkm->bhm', q_t * scale, hk)
                p = jax.nn.softmax(logits, axis=-1)
                hv = hv * ge[..., :, None] + s_t[..., :, None] * v_t[..., None, :]
                o_t = jnp.einsum('bhm,bhmv->bhv', p, hv)
                return ((hk, hv), o_t)
            init = (jnp.zeros((b, h, dk, m), q.dtype), jnp.zeros((b, h, m, dv), q.dtype))
            xs = tuple((jnp.moveaxis(a, 1, 0) for a in (q, k, v, s, g)))
            _, o = jax.lax.scan(step, init, xs)
            return jnp.moveaxis(o, 0, 1)
        key = jax.random.key(seed)
        ks = jax.random.split(key, 6)
        sc = lambda n: 1.0 / np.sqrt(n)
        return {'x': jax.random.normal(ks[0], (B, T, D), jnp.float32), 'Wq': jax.random.normal(ks[1], (D, H * K), jnp.float32) * sc(D), 'Wk': jax.random.normal(ks[2], (D, H * K), jnp.float32) * sc(D), 'Wv': jax.random.normal(ks[3], (D, H * V), jnp.float32) * sc(D), 'Wf': jax.random.normal(ks[4], (D, H * M), jnp.float32) * sc(D), 'g_norm_w': jnp.ones((V,), jnp.float32), 'Wo': jax.random.normal(ks[5], (H * V, D), jnp.float32) * sc(H * V)}
    _L1_attn_in = _L1_attn_setup()

    def _L1_ffn_setup():
        import jax, jax.numpy as jnp
        import numpy as np
        HIDDEN = 128
        NUM_EXPERTS = 8
        CAPACITY_FACTOR = 1.25
        key = jax.random.key(seed)
        k_tok, k_g, k_w1, k_b1, k_w2, k_b2 = jax.random.split(key, 6)
        B, S, H, E = (4, 256, HIDDEN, NUM_EXPERTS)
        tokens = jax.random.normal(k_tok, (B, S, H), dtype=jnp.float32)
        gate_w = jax.random.normal(k_g, (E, H), dtype=jnp.float32) * 0.02
        W1 = jax.random.normal(k_w1, (E, H, H), dtype=jnp.float32) * 0.02
        b1 = jax.random.normal(k_b1, (E, H), dtype=jnp.float32) * 0.02
        W2 = jax.random.normal(k_w2, (E, H, H), dtype=jnp.float32) * 0.02
        b2 = jax.random.normal(k_b2, (E, H), dtype=jnp.float32) * 0.02
        return {'tokens': tokens, 'gate_w': gate_w, 'W1': W1, 'b1': b1, 'W2': W2, 'b2': b2}
    _L1_ffn_in = _L1_ffn_setup()

    def _L2_attn_setup():
        import jax, jax.numpy as jnp
        import numpy as np
        from jax import lax
        D_MODEL = 128
        D_STATE = 16
        D_CONV = 4
        EXPAND = 2
        D_INNER = D_MODEL * EXPAND
        BATCH = 2
        SEQ = 256

        def _forward(x, W_in, conv_w, conv_b, W_x, W_dt, b_dt, A_log, D_param, W_out):
            B, L, _ = x.shape
            xz = x @ W_in
            xc, z = jnp.split(xz, 2, axis=-1)
            xc_t = jnp.transpose(xc, (0, 2, 1))
            xc_t = lax.conv_general_dilated(xc_t, conv_w, window_strides=(1,), padding=[(D_CONV - 1, 0)], feature_group_count=D_INNER, dimension_numbers=('NCH', 'OIH', 'NCH'))
            xc_t = xc_t + conv_b[None, :, None]
            xc = jnp.transpose(xc_t, (0, 2, 1))
            xc = jax.nn.silu(xc)
            x_dbl = xc @ W_x
            dt_raw = x_dbl[..., :1]
            B_mat = x_dbl[..., 1:1 + D_STATE]
            C_mat = x_dbl[..., 1 + D_STATE:]
            dt = jax.nn.softplus(dt_raw @ W_dt + b_dt)
            A = -jnp.exp(A_log)

            def step(h, inp):
                x_t, dt_t, B_t, C_t = inp
                dA = jnp.exp(dt_t[..., None] * A)
                h = dA * h + dt_t[..., None] * B_t[:, None, :] * x_t[..., None]
                y = jnp.einsum('bds,bs->bd', h, C_t)
                return (h, y)
            xs = (jnp.moveaxis(xc, 1, 0), jnp.moveaxis(dt, 1, 0), jnp.moveaxis(B_mat, 1, 0), jnp.moveaxis(C_mat, 1, 0))
            h0 = jnp.zeros((B, D_INNER, D_STATE), dtype=x.dtype)
            _, ys = lax.scan(step, h0, xs)
            y = jnp.moveaxis(ys, 0, 1) + D_param * xc
            y = y * jax.nn.silu(z)
            return y @ W_out
        key = jax.random.key(seed)
        ks = jax.random.split(key, 9)
        s_in = 1.0 / np.sqrt(D_MODEL)
        s_x = 1.0 / np.sqrt(D_INNER)
        x = jax.random.normal(ks[0], (BATCH, SEQ, D_MODEL), dtype=jnp.float32)
        W_in = jax.random.normal(ks[1], (D_MODEL, 2 * D_INNER), dtype=jnp.float32) * s_in
        conv_w = jax.random.normal(ks[2], (D_INNER, 1, D_CONV), dtype=jnp.float32) * 0.5
        conv_b = jax.random.normal(ks[3], (D_INNER,), dtype=jnp.float32) * 0.1
        W_x = jax.random.normal(ks[4], (D_INNER, 2 * D_STATE + 1), dtype=jnp.float32) * s_x
        W_dt = jax.random.normal(ks[5], (1, D_INNER), dtype=jnp.float32)
        b_dt = jax.random.normal(ks[6], (D_INNER,), dtype=jnp.float32) * 0.1
        A_log = jnp.broadcast_to(jnp.log(jnp.arange(1, D_STATE + 1, dtype=jnp.float32)), (D_INNER, D_STATE))
        D_param = jnp.ones((D_INNER,), dtype=jnp.float32)
        W_out = jax.random.normal(ks[7], (D_INNER, D_MODEL), dtype=jnp.float32) * s_x
        return {'x': x, 'W_in': W_in, 'conv_w': conv_w, 'conv_b': conv_b, 'W_x': W_x, 'W_dt': W_dt, 'b_dt': b_dt, 'A_log': A_log, 'D_param': D_param, 'W_out': W_out}
    _L2_attn_in = _L2_attn_setup()

    def _L2_ffn_setup():
        import jax, jax.numpy as jnp
        import numpy as np
        B, S, D, E, F = (2, 128, 128, 14, 256)
        key = jax.random.key(seed)
        k0, k1, k2, k3 = jax.random.split(key, 4)
        h = jax.random.normal(k0, (B, S, D), jnp.float32)
        gate_w = jax.random.normal(k1, (E, D), jnp.float32) * 0.02
        w1 = jax.random.normal(k2, (E, D, F), jnp.float32) * (1.0 / np.sqrt(D).astype(np.float32))
        b1 = jnp.zeros((E, F), jnp.float32)
        w2 = jax.random.normal(k3, (E, F, D), jnp.float32) * (1.0 / np.sqrt(F).astype(np.float32))
        b2 = jnp.zeros((E, D), jnp.float32)
        return {'h': h, 'gate_w': gate_w, 'w1': w1, 'b1': b1, 'w2': w2, 'b2': b2}
    _L2_ffn_in = _L2_ffn_setup()

    def _L3_attn_setup():
        import jax, jax.numpy as jnp
        import numpy as np
        D_IN, HEAD_DIM = (128, 128)
        key = jax.random.key(seed)
        ks = jax.random.split(key, 9)
        s = 0.02
        return {'x': jax.random.normal(ks[0], (4, 512, D_IN), dtype=jnp.float32), 'Wq': jax.random.normal(ks[1], (HEAD_DIM, D_IN), dtype=jnp.float32) * s, 'bq': jnp.zeros((HEAD_DIM,), dtype=jnp.float32), 'Wk': jax.random.normal(ks[2], (HEAD_DIM, D_IN), dtype=jnp.float32) * s, 'bk': jnp.zeros((HEAD_DIM,), dtype=jnp.float32), 'Wv': jax.random.normal(ks[3], (HEAD_DIM, D_IN), dtype=jnp.float32) * s, 'bv': jnp.zeros((HEAD_DIM,), dtype=jnp.float32), 'Wo': jax.random.normal(ks[4], (D_IN, HEAD_DIM), dtype=jnp.float32) * s, 'bo': jnp.zeros((D_IN,), dtype=jnp.float32)}
    _L3_attn_in = _L3_attn_setup()

    def _L3_ffn_setup():
        import jax, jax.numpy as jnp
        import numpy as np
        BLOCK = 16
        _GRID = jnp.array([0.0, 0.5, 1.0, 1.5, 2.0, 3.0, 4.0, 6.0], dtype=jnp.float32)
        _MID = jnp.array([0.25, 0.75, 1.25, 1.75, 2.5, 3.5, 5.0], dtype=jnp.float32)

        def fp4_quant_dequant(x):
            shape = x.shape
            xb = x.reshape(shape[:-1] + (shape[-1] // BLOCK, BLOCK))
            scale = jnp.max(jnp.abs(xb), axis=-1, keepdims=True) / 6.0
            scale = jnp.maximum(scale, jnp.float32(1e-12))
            xn = xb / scale
            idx = jnp.searchsorted(_MID, jnp.abs(xn))
            q = _GRID[idx] * jnp.sign(xn) * scale
            return q.reshape(shape)

        def fp4_linear(x, w):
            xq = fp4_quant_dequant(x)
            wq = fp4_quant_dequant(w)
            return jnp.einsum('bsk,nk->bsn', xq, wq)
        key = jax.random.key(seed)
        k1, k2, k3, k4 = jax.random.split(key, 4)
        H, I = (128, 352)
        x = jax.random.normal(k1, (4, 512, H), dtype=jnp.float32)
        w_gate = jax.random.normal(k2, (I, H), dtype=jnp.float32) * 0.02
        w_up = jax.random.normal(k3, (I, H), dtype=jnp.float32) * 0.02
        w_down = jax.random.normal(k4, (H, I), dtype=jnp.float32) * 0.02
        return {'x': x, 'w_gate': w_gate, 'w_up': w_up, 'w_down': w_down}
    _L3_ffn_in = _L3_ffn_setup()
    _d = {'L0_attn_x': _L0_attn_in['x'], 'L0_attn_Wq': _L0_attn_in['Wq'], 'L0_attn_bq': _L0_attn_in['bq'], 'L0_attn_Wk': _L0_attn_in['Wk'], 'L0_attn_bk': _L0_attn_in['bk'], 'L0_attn_Wv': _L0_attn_in['Wv'], 'L0_attn_bv': _L0_attn_in['bv'], 'L0_attn_Wo': _L0_attn_in['Wo'], 'L0_attn_bo': _L0_attn_in['bo'], 'L0_attn_ln1_s': _L0_attn_in['ln1_s'], 'L0_attn_ln1_b': _L0_attn_in['ln1_b'], 'L0_attn_Wf1': _L0_attn_in['Wf1'], 'L0_attn_bf1': _L0_attn_in['bf1'], 'L0_attn_Wf2': _L0_attn_in['Wf2'], 'L0_attn_bf2': _L0_attn_in['bf2'], 'L0_attn_ln2_s': _L0_attn_in['ln2_s'], 'L0_attn_ln2_b': _L0_attn_in['ln2_b'], 'L0_ffn_in_proj_w': _L0_ffn_in['in_proj_w'], 'L0_ffn_in_proj_b': _L0_ffn_in['in_proj_b'], 'L0_ffn_out_proj_w': _L0_ffn_in['out_proj_w'], 'L0_ffn_out_proj_b': _L0_ffn_in['out_proj_b'], 'L0_ffn_ln1_g': _L0_ffn_in['ln1_g'], 'L0_ffn_ln1_b': _L0_ffn_in['ln1_b'], 'L0_ffn_ln2_g': _L0_ffn_in['ln2_g'], 'L0_ffn_ln2_b': _L0_ffn_in['ln2_b'], 'L0_ffn_w_group': _L0_ffn_in['w_group'], 'L0_ffn_b_group': _L0_ffn_in['b_group'], 'L0_ffn_w_expert': _L0_ffn_in['w_expert'], 'L0_ffn_b_expert': _L0_ffn_in['b_expert'], 'L0_ffn_w1': _L0_ffn_in['w1'], 'L0_ffn_b1': _L0_ffn_in['b1'], 'L0_ffn_w2': _L0_ffn_in['w2'], 'L0_ffn_b2': _L0_ffn_in['b2'], 'L1_attn_Wq': _L1_attn_in['Wq'], 'L1_attn_Wk': _L1_attn_in['Wk'], 'L1_attn_Wv': _L1_attn_in['Wv'], 'L1_attn_Wf': _L1_attn_in['Wf'], 'L1_attn_g_norm_w': _L1_attn_in['g_norm_w'], 'L1_attn_Wo': _L1_attn_in['Wo'], 'L1_ffn_gate_w': _L1_ffn_in['gate_w'], 'L1_ffn_W1': _L1_ffn_in['W1'], 'L1_ffn_b1': _L1_ffn_in['b1'], 'L1_ffn_W2': _L1_ffn_in['W2'], 'L1_ffn_b2': _L1_ffn_in['b2'], 'L2_attn_W_in': _L2_attn_in['W_in'], 'L2_attn_conv_w': _L2_attn_in['conv_w'], 'L2_attn_conv_b': _L2_attn_in['conv_b'], 'L2_attn_W_x': _L2_attn_in['W_x'], 'L2_attn_W_dt': _L2_attn_in['W_dt'], 'L2_attn_b_dt': _L2_attn_in['b_dt'], 'L2_attn_A_log': _L2_attn_in['A_log'], 'L2_attn_D_param': _L2_attn_in['D_param'], 'L2_attn_W_out': _L2_attn_in['W_out'], 'L2_ffn_gate_w': _L2_ffn_in['gate_w'], 'L2_ffn_w1': _L2_ffn_in['w1'], 'L2_ffn_b1': _L2_ffn_in['b1'], 'L2_ffn_w2': _L2_ffn_in['w2'], 'L2_ffn_b2': _L2_ffn_in['b2'], 'L3_attn_Wq': _L3_attn_in['Wq'], 'L3_attn_bq': _L3_attn_in['bq'], 'L3_attn_Wk': _L3_attn_in['Wk'], 'L3_attn_bk': _L3_attn_in['bk'], 'L3_attn_Wv': _L3_attn_in['Wv'], 'L3_attn_bv': _L3_attn_in['bv'], 'L3_attn_Wo': _L3_attn_in['Wo'], 'L3_attn_bo': _L3_attn_in['bo'], 'L3_ffn_w_gate': _L3_ffn_in['w_gate'], 'L3_ffn_w_up': _L3_ffn_in['w_up'], 'L3_ffn_w_down': _L3_ffn_in['w_down']}
    _x0 = _d['L0_attn_x']
    _d['L0_attn_x'] = jax.random.normal(jax.random.fold_in(jax.random.key(seed), 1), (2, 1024, 128), dtype=_x0.dtype)
    del _x0
    return _d

def reference(L0_attn_x, L0_attn_Wq, L0_attn_bq, L0_attn_Wk, L0_attn_bk, L0_attn_Wv, L0_attn_bv, L0_attn_Wo, L0_attn_bo, L0_attn_ln1_s, L0_attn_ln1_b, L0_attn_Wf1, L0_attn_bf1, L0_attn_Wf2, L0_attn_bf2, L0_attn_ln2_s, L0_attn_ln2_b, L0_ffn_in_proj_w, L0_ffn_in_proj_b, L0_ffn_out_proj_w, L0_ffn_out_proj_b, L0_ffn_ln1_g, L0_ffn_ln1_b, L0_ffn_ln2_g, L0_ffn_ln2_b, L0_ffn_w_group, L0_ffn_b_group, L0_ffn_w_expert, L0_ffn_b_expert, L0_ffn_w1, L0_ffn_b1, L0_ffn_w2, L0_ffn_b2, L1_attn_Wq, L1_attn_Wk, L1_attn_Wv, L1_attn_Wf, L1_attn_g_norm_w, L1_attn_Wo, L1_ffn_gate_w, L1_ffn_W1, L1_ffn_b1, L1_ffn_W2, L1_ffn_b2, L2_attn_W_in, L2_attn_conv_w, L2_attn_conv_b, L2_attn_W_x, L2_attn_W_dt, L2_attn_b_dt, L2_attn_A_log, L2_attn_D_param, L2_attn_W_out, L2_ffn_gate_w, L2_ffn_w1, L2_ffn_b1, L2_ffn_w2, L2_ffn_b2, L3_attn_Wq, L3_attn_bq, L3_attn_Wk, L3_attn_bk, L3_attn_Wv, L3_attn_bv, L3_attn_Wo, L3_attn_bo, L3_ffn_w_gate, L3_ffn_w_up, L3_ffn_w_down):

    def _L0_attn_ref(x, Wq, bq, Wk, bk, Wv, bv, Wo, bo, ln1_s, ln1_b, Wf1, bf1, Wf2, bf2, ln2_s, ln2_b):
        import jax, jax.numpy as jnp
        import numpy as np
        N, L, D, A, F, B = (4, 512, 128, 128, 512, 8)
        EPS_LN = 1e-06
        EPS_Z = 1e-06

        def _layernorm(x, scale, bias):
            m = jnp.mean(x, axis=-1, keepdims=True)
            v = jnp.mean(jnp.square(x - m), axis=-1, keepdims=True)
            return (x - m) * jax.lax.rsqrt(v + EPS_LN) * scale + bias

        def _block(x, p):
            Wq, bq, Wk, bk, Wv, bv, Wo, bo, ln1_s, ln1_b, Wf1, bf1, Wf2, bf2, ln2_s, ln2_b = p
            residual = x
            q = jnp.einsum('nld,da->nla', x, Wq) + bq
            k = jnp.einsum('nld,da->nla', x, Wk) + bk
            v = jnp.einsum('nld,da->nla', x, Wv) + bv
            Q = jax.nn.elu(q) + 1.0
            K = jax.nn.elu(k) + 1.0
            KV = jnp.einsum('nsh,nsh->nh', K, v)
            Ksum = jnp.sum(K, axis=1)
            Z = 1.0 / (Q * Ksum[:, None, :] + EPS_Z)
            V = Q * KV[:, None, :] * Z
            attn = jax.nn.gelu(jnp.einsum('nla,ad->nld', V, Wo) + bo)
            x = _layernorm(attn + residual, ln1_s, ln1_b)
            residual = x
            h = jax.nn.gelu(jnp.einsum('nld,df->nlf', x, Wf1) + bf1)
            ff = jax.nn.gelu(jnp.einsum('nlf,fd->nld', h, Wf2) + bf2)
            x = _layernorm(ff + residual, ln2_s, ln2_b)
            return (x, None)
        params = (Wq, bq, Wk, bk, Wv, bv, Wo, bo, ln1_s, ln1_b, Wf1, bf1, Wf2, bf2, ln2_s, ln2_b)
        out, _ = jax.lax.scan(_block, x, params)
        return out

    def _L0_ffn_ref(x, in_proj_w, in_proj_b, out_proj_w, out_proj_b, ln1_g, ln1_b, ln2_g, ln2_b, w_group, b_group, w_expert, b_expert, w1, b1, w2, b2):
        import jax, jax.numpy as jnp
        import numpy as np
        NHEAD = 16
        NUM_GROUPS = 4
        EXPERTS_PER_GROUP = 2
        LN_EPS = 1e-05

        def _layernorm(x, g, b):
            mu = jnp.mean(x, axis=-1, keepdims=True)
            var = jnp.mean(jnp.square(x - mu), axis=-1, keepdims=True)
            return (x - mu) * jax.lax.rsqrt(var + LN_EPS) * g + b

        def _mha(x, wi, bi, wo, bo):
            B, S, D = x.shape
            hd = D // NHEAD
            qkv = x @ wi.T + bi
            q, k, v = jnp.split(qkv, 3, axis=-1)

            def heads(t):
                return t.reshape(B, S, NHEAD, hd).transpose(0, 2, 1, 3)
            q, k, v = (heads(q), heads(k), heads(v))
            scores = jnp.einsum('bhqd,bhkd->bhqk', q, k) / jnp.sqrt(jnp.asarray(hd, x.dtype))
            attn = jax.nn.softmax(scores, axis=-1)
            o = jnp.einsum('bhqk,bhkd->bhqd', attn, v)
            o = o.transpose(0, 2, 1, 3).reshape(B, S, D)
            return o @ wo.T + bo

        def _hier_moe(x, w_group, b_group, w_expert, b_expert, w1, b1, w2, b2):
            B, S, D = x.shape
            xt = x.reshape(B * S, D)
            T = xt.shape[0]
            E = NUM_GROUPS * EXPERTS_PER_GROUP
            gp = jax.nn.softmax(xt @ w_group + b_group, axis=-1)
            g_idx = jnp.argmax(gp, axis=-1)
            g_prob = jnp.max(gp, axis=-1)
            elog = jnp.einsum('td,gde->tge', xt, w_expert) + b_expert
            ep = jax.nn.softmax(elog, axis=-1)
            ep_sel = jnp.take_along_axis(ep, g_idx[:, None, None], axis=1)[:, 0, :]
            e_idx_local = jnp.argmax(ep_sel, axis=-1)
            e_prob = jnp.max(ep_sel, axis=-1)
            flat_e = g_idx * EXPERTS_PER_GROUP + e_idx_local
            combine = jax.nn.one_hot(flat_e, E, dtype=xt.dtype) * (g_prob * e_prob)[:, None]
            h = jax.nn.relu(jnp.einsum('td,edf->etf', xt, w1) + b1[:, None, :])
            y = jnp.einsum('etf,efd->etd', h, w2) + b2[:, None, :]
            out = jnp.einsum('te,etd->td', combine, y)
            return out.reshape(B, S, D)
        attn_out = _mha(x, in_proj_w, in_proj_b, out_proj_w, out_proj_b)
        x = _layernorm(x + attn_out, ln1_g, ln1_b)
        moe_out = _hier_moe(x, w_group, b_group, w_expert, b_expert, w1, b1, w2, b2)
        x = _layernorm(x + moe_out, ln2_g, ln2_b)
        return x

    def _L1_attn_ref(x, Wq, Wk, Wv, Wf, g_norm_w, Wo):
        import jax, jax.numpy as jnp
        import numpy as np
        B, T, D = (4, 256, 128)
        H = 4
        K = D // H
        V = D // H
        M = 64
        GATE_LOGIT_NORMALIZER = 8.0
        NORM_EPS = 1e-05

        def _swish(x):
            return x * jax.nn.sigmoid(x)

        def _gsa_recurrence(q, k, v, s, g, scale):
            b, t, h, dk = q.shape
            dv = v.shape[-1]
            m = s.shape[-1]

            def step(carry, inp):
                hk, hv = carry
                q_t, k_t, v_t, s_t, g_t = inp
                ge = jnp.exp(g_t)
                hk = hk * ge[:, :, None, :] + k_t[..., :, None] * s_t[..., None, :]
                logits = jnp.einsum('bhk,bhkm->bhm', q_t * scale, hk)
                p = jax.nn.softmax(logits, axis=-1)
                hv = hv * ge[..., :, None] + s_t[..., :, None] * v_t[..., None, :]
                o_t = jnp.einsum('bhm,bhmv->bhv', p, hv)
                return ((hk, hv), o_t)
            init = (jnp.zeros((b, h, dk, m), q.dtype), jnp.zeros((b, h, m, dv), q.dtype))
            xs = tuple((jnp.moveaxis(a, 1, 0) for a in (q, k, v, s, g)))
            _, o = jax.lax.scan(step, init, xs)
            return jnp.moveaxis(o, 0, 1)
        b, t, d = x.shape
        q = _swish((x @ Wq).reshape(b, t, H, K))
        k = _swish((x @ Wk).reshape(b, t, H, K))
        v = (x @ Wv).reshape(b, t, H, V)
        f = jax.nn.log_sigmoid((x @ Wf).reshape(b, t, H, M)) / GATE_LOGIT_NORMALIZER
        s = 1.0 - jnp.exp(f)
        o = _gsa_recurrence(q, k, v, s, f, scale=K ** (-0.5))
        o = o * jax.lax.rsqrt(jnp.mean(o * o, axis=-1, keepdims=True) + NORM_EPS) * g_norm_w
        return o.reshape(b, t, H * V) @ Wo

    def _L1_ffn_ref(tokens, gate_w, W1, b1, W2, b2):
        import jax, jax.numpy as jnp
        import numpy as np
        HIDDEN = 128
        NUM_EXPERTS = 8
        CAPACITY_FACTOR = 1.25
        B, S, H = tokens.shape
        E = gate_w.shape[0]
        T = B * S
        x = tokens.reshape(T, H)
        logits = x @ gate_w.T
        probs = jax.nn.softmax(logits, axis=-1)
        top2_w, top2_idx = jax.lax.top_k(probs, 2)
        cap = int(CAPACITY_FACTOR * T / E)
        counts = jnp.bincount(top2_idx.reshape(-1), length=E)
        keep = (counts <= cap).astype(x.dtype)
        comb = jnp.zeros((T, E), dtype=x.dtype).at[jnp.arange(T)[:, None], top2_idx].add(top2_w)
        comb = comb * keep[None, :]
        h = jax.nn.relu(jnp.einsum('th,ehf->tef', x, W1) + b1[None, :, :])
        y = jnp.einsum('teh,ehf->tef', h, W2) + b2[None, :, :]
        out = jnp.einsum('te,tef->tf', comb, y)
        return out.reshape(B, S, H)

    def _L2_attn_ref(x, W_in, conv_w, conv_b, W_x, W_dt, b_dt, A_log, D_param, W_out):
        import jax, jax.numpy as jnp
        import numpy as np
        from jax import lax
        D_MODEL = 128
        D_STATE = 16
        D_CONV = 4
        EXPAND = 2
        D_INNER = D_MODEL * EXPAND
        BATCH = 2
        SEQ = 256

        def _forward(x, W_in, conv_w, conv_b, W_x, W_dt, b_dt, A_log, D_param, W_out):
            B, L, _ = x.shape
            xz = x @ W_in
            xc, z = jnp.split(xz, 2, axis=-1)
            xc_t = jnp.transpose(xc, (0, 2, 1))
            xc_t = lax.conv_general_dilated(xc_t, conv_w, window_strides=(1,), padding=[(D_CONV - 1, 0)], feature_group_count=D_INNER, dimension_numbers=('NCH', 'OIH', 'NCH'))
            xc_t = xc_t + conv_b[None, :, None]
            xc = jnp.transpose(xc_t, (0, 2, 1))
            xc = jax.nn.silu(xc)
            x_dbl = xc @ W_x
            dt_raw = x_dbl[..., :1]
            B_mat = x_dbl[..., 1:1 + D_STATE]
            C_mat = x_dbl[..., 1 + D_STATE:]
            dt = jax.nn.softplus(dt_raw @ W_dt + b_dt)
            A = -jnp.exp(A_log)

            def step(h, inp):
                x_t, dt_t, B_t, C_t = inp
                dA = jnp.exp(dt_t[..., None] * A)
                h = dA * h + dt_t[..., None] * B_t[:, None, :] * x_t[..., None]
                y = jnp.einsum('bds,bs->bd', h, C_t)
                return (h, y)
            xs = (jnp.moveaxis(xc, 1, 0), jnp.moveaxis(dt, 1, 0), jnp.moveaxis(B_mat, 1, 0), jnp.moveaxis(C_mat, 1, 0))
            h0 = jnp.zeros((B, D_INNER, D_STATE), dtype=x.dtype)
            _, ys = lax.scan(step, h0, xs)
            y = jnp.moveaxis(ys, 0, 1) + D_param * xc
            y = y * jax.nn.silu(z)
            return y @ W_out
        return _forward(x, W_in, conv_w, conv_b, W_x, W_dt, b_dt, A_log, D_param, W_out)

    def _L2_ffn_ref(h, gate_w, w1, b1, w2, b2):
        import jax, jax.numpy as jnp
        import numpy as np
        B, S, D, E, F = (2, 128, 128, 14, 256)
        Bb, Ss, Dd = h.shape
        x = h.reshape(Bb * Ss, Dd)
        logits = x @ gate_w.T
        probs = jax.nn.softmax(logits, axis=-1)
        top2_p, top2_i = jax.lax.top_k(probs, 2)
        w = top2_p / jnp.maximum(top2_p.sum(-1, keepdims=True), 1e-10)
        hh = jnp.einsum('nd,edf->nef', x, w1) + b1
        hh = jax.nn.gelu(hh, approximate=False)
        all_out = jnp.einsum('nef,efd->ned', hh, w2) + b2
        n = jnp.arange(x.shape[0])
        out0 = all_out[n, top2_i[:, 0]]
        out1 = all_out[n, top2_i[:, 1]]
        moe_out = w[:, 0:1] * out0 + w[:, 1:2] * out1
        result = jnp.clip(x + moe_out, -100.0, 100.0).reshape(Bb, Ss, Dd)
        return result

    def _L3_attn_ref(x, Wq, bq, Wk, bk, Wv, bv, Wo, bo):
        import jax, jax.numpy as jnp
        import numpy as np
        D_IN, HEAD_DIM = (128, 128)
        B, S, D = x.shape
        Q = jnp.einsum('bsd,hd->bsh', x, Wq) + bq
        K = jnp.einsum('bsd,hd->bsh', x, Wk) + bk
        V = jnp.einsum('bsd,hd->bsh', x, Wv) + bv
        scores = jnp.einsum('bqh,bkh->bqk', Q, K)
        causal = jnp.tril(jnp.ones((S, S), dtype=bool))
        scores = jnp.where(causal, scores, -jnp.inf)
        scale = jnp.float32(HEAD_DIM) ** (-0.5)
        attn = jax.nn.softmax(scores * scale, axis=-1)
        out = jnp.einsum('bqk,bkh->bqh', attn, V)
        return jnp.einsum('bsh,dh->bsd', out, Wo) + bo

    def _L3_ffn_ref(x, w_gate, w_up, w_down):
        import jax, jax.numpy as jnp
        import numpy as np
        BLOCK = 16
        _GRID = jnp.array([0.0, 0.5, 1.0, 1.5, 2.0, 3.0, 4.0, 6.0], dtype=jnp.float32)
        _MID = jnp.array([0.25, 0.75, 1.25, 1.75, 2.5, 3.5, 5.0], dtype=jnp.float32)

        def fp4_quant_dequant(x):
            shape = x.shape
            xb = x.reshape(shape[:-1] + (shape[-1] // BLOCK, BLOCK))
            scale = jnp.max(jnp.abs(xb), axis=-1, keepdims=True) / 6.0
            scale = jnp.maximum(scale, jnp.float32(1e-12))
            xn = xb / scale
            idx = jnp.searchsorted(_MID, jnp.abs(xn))
            q = _GRID[idx] * jnp.sign(xn) * scale
            return q.reshape(shape)

        def fp4_linear(x, w):
            xq = fp4_quant_dequant(x)
            wq = fp4_quant_dequant(w)
            return jnp.einsum('bsk,nk->bsn', xq, wq)
        gate = fp4_linear(x, w_gate)
        y = fp4_linear(x, w_up)
        h = jax.nn.silu(gate) * y
        return fp4_linear(h, w_down)
    x = L0_attn_x
    xn = _layernorm(x, axis=-1)
    x = x + _L0_attn_ref(xn, L0_attn_Wq, L0_attn_bq, L0_attn_Wk, L0_attn_bk, L0_attn_Wv, L0_attn_bv, L0_attn_Wo, L0_attn_bo, L0_attn_ln1_s, L0_attn_ln1_b, L0_attn_Wf1, L0_attn_bf1, L0_attn_Wf2, L0_attn_bf2, L0_attn_ln2_s, L0_attn_ln2_b) + _L0_ffn_ref(xn, L0_ffn_in_proj_w, L0_ffn_in_proj_b, L0_ffn_out_proj_w, L0_ffn_out_proj_b, L0_ffn_ln1_g, L0_ffn_ln1_b, L0_ffn_ln2_g, L0_ffn_ln2_b, L0_ffn_w_group, L0_ffn_b_group, L0_ffn_w_expert, L0_ffn_b_expert, L0_ffn_w1, L0_ffn_b1, L0_ffn_w2, L0_ffn_b2)
    xn = _layernorm(x, axis=-1)
    x = x + _L1_attn_ref(xn, L1_attn_Wq, L1_attn_Wk, L1_attn_Wv, L1_attn_Wf, L1_attn_g_norm_w, L1_attn_Wo) + _L1_ffn_ref(xn, L1_ffn_gate_w, L1_ffn_W1, L1_ffn_b1, L1_ffn_W2, L1_ffn_b2)
    xn = _layernorm(x, axis=-1)
    x = x + _L2_attn_ref(xn, L2_attn_W_in, L2_attn_conv_w, L2_attn_conv_b, L2_attn_W_x, L2_attn_W_dt, L2_attn_b_dt, L2_attn_A_log, L2_attn_D_param, L2_attn_W_out) + _L2_ffn_ref(xn, L2_ffn_gate_w, L2_ffn_w1, L2_ffn_b1, L2_ffn_w2, L2_ffn_b2)
    xn = _layernorm(x, axis=-1)
    x = x + _L3_attn_ref(xn, L3_attn_Wq, L3_attn_bq, L3_attn_Wk, L3_attn_bk, L3_attn_Wv, L3_attn_bv, L3_attn_Wo, L3_attn_bo) + _L3_ffn_ref(xn, L3_ffn_w_gate, L3_ffn_w_up, L3_ffn_w_down)
    return x

_drawn_inputs = setup_inputs


def setup_inputs(seed=0):
    import zlib

    import numpy as np

    out = dict(_drawn_inputs(seed))
    spreads = {'L0_attn_bq': (0.0, 2.0),
     'L0_attn_bk': (0.0, 0.8),
     'L0_attn_bv': (0.0, 0.296),
     'L0_attn_bo': (0.0, 0.1),
     'L0_attn_ln1_s': (1.0, 0.2),
     'L0_attn_ln1_b': (0.0, 0.1),
     'L0_attn_bf1': (0.0, 0.326),
     'L0_attn_bf2': (0.0, 0.1),
     'L0_attn_ln2_s': (1.0, 0.2),
     'L0_attn_ln2_b': (0.0, 0.1),
     'L0_ffn_in_proj_b': (0.0, 0.1),
     'L0_ffn_out_proj_b': (0.0, 0.1),
     'L0_ffn_ln1_g': (1.0, 0.2),
     'L0_ffn_ln1_b': (0.0, 0.1),
     'L0_ffn_ln2_g': (1.0, 0.2),
     'L0_ffn_ln2_b': (0.0, 0.1),
     'L0_ffn_b_group': (0.0, 0.1),
     'L0_ffn_b_expert': (0.0, 0.593),
     'L0_ffn_b1': (0.0, 0.502),
     'L0_ffn_b2': (0.0, 0.36),
     'L1_attn_g_norm_w': (1.0, 0.2),
     'L2_attn_D_param': (1.0, 0.6),
     'L2_ffn_b1': (0.0, 0.689),
     'L2_ffn_b2': (0.0, 0.453),
     'L3_attn_bq': (0.0, 0.8),
     'L3_attn_bk': (0.0, 2.0),
     'L3_attn_bv': (0.0, 0.8),
     'L3_attn_bo': (0.0, 0.343)}
    factors = {'L0_attn_Wq': 64.0,
     'L0_attn_Wk': 8.0,
     'L0_attn_Wv': 2.981,
     'L1_attn_Wq': 7.653,
     'L1_attn_Wk': 7.719,
     'L2_attn_conv_b': 2.778,
     'L2_attn_b_dt': 6.989,
     'L2_attn_A_log': 2.724,
     'L3_attn_Wq': 8.0,
     'L3_attn_Wk': 8.0,
     'L3_attn_Wv': 8.0,
     'L3_attn_Wo': 8.0,
     'L3_ffn_w_gate': 8.0,
     'L3_ffn_w_up': 8.0,
     'L3_ffn_w_down': 8.0}
    for name, (base, spread) in spreads.items():
        noise = np.random.default_rng([zlib.crc32(name.encode()), seed]).standard_normal(out[name].shape)
        drawn = base * np.exp(spread * noise) if base else spread * noise
        out[name] = jnp.asarray(drawn.astype(out[name].dtype))
    for name, factor in factors.items():
        out[name] = (out[name] * factor).astype(out[name].dtype)
    return out
```

```python
from contextlib import ExitStack, contextmanager

import concourse.bass as bass
from concourse import mybir

F32 = mybir.dt.float32
BF16 = mybir.dt.bfloat16
ALU = mybir.AluOpType
ACT = mybir.ActivationFunctionType
AX = mybir.AxisListType

P = 128
D = 128
HALVES = 2
T = 1024
N = HALVES * T
BANK = 512
BOTH = range(HALVES)


class Steps:

    def __init__(self, base, text, rounds):
        lead, loop, tail = text.split("|") if "|" in text else ("", text, "")
        self.lead, self.loop, self.tail = lead.split(), loop.split(), tail.split()
        self.base, self.rounds = base, rounds

    def value(self, name, i=0):
        if name in self.lead:
            return self.base + self.lead.index(name) + 1
        first = self.base + len(self.lead)
        if name in self.loop:
            return i * len(self.loop) + (first + self.loop.index(name) + 1)
        return first + self.rounds * len(self.loop) + self.tail.index(name) + 1

    def before(self, name, i):
        return i * len(self.loop) + (self.value(name) - len(self.loop))

    @property
    def end(self):
        return self.base + len(self.lead) + self.rounds * len(self.loop) + len(self.tail)


class Core:

    def __init__(self, nc, ctx):
        self.nc, self.ctx, self.taken = nc, ctx, []
        self.pe_done = [self.sem(f"pe_done{h}") for h in BOTH]
        self.act_done = [self.sem(f"act_done{h}") for h in BOTH]
        self.dve_done = [self.sem(f"dve_done{h}") for h in BOTH]
        self.pool_done = [self.sem(f"pool_done{h}") for h in BOTH]
        self.at = [0, 0, 0, 0]
        self.quad = [ctx.enter_context(nc.psum_tensor(f"quad{h}", [P, 2 * T], F32)) for h in BOTH]
        self.slot = [[self.quad[h][:, k * T:(k + 1) * T] for k in range(2)] for h in BOTH]
        self.x = self.sb("x", [P, N])
        self.xn = self.sb("xn", [P, N])
        self.mean_w = self.sb("mean_w", [P, P])
        self.centre_w = self.sb("centre_w", [P, P])
        self.eps = {1e-6: self.sb("eps6", [P, 1]), 1e-5: self.sb("eps5", [P, 1])}
        self.ident = self.sb("ident", [P, P])
        self.one = self.sb("one", [P, 1])
        self.cen_all, self.sq_all = self.sb("cen_all", [P, N]), self.sb("sq_all", [P, N])
        self.cen = [half(self.cen_all, h) for h in BOTH]
        self.sq = [half(self.sq_all, h) for h in BOTH]

    def sb(self, name, shape, dt=F32, ctx=None):
        return (ctx or self.ctx).enter_context(self.nc.sbuf_tensor(name, shape, dt))

    def sem(self, name):
        self.taken.append(self.nc.alloc_semaphore(name))
        return self.taken[-1]

    @contextmanager
    def own_semaphores(self):
        outer, self.taken = self.taken, []
        yield
        self.nc.clear_and_free_semaphores(self.taken)
        self.nc.all_engine_barrier()
        self.taken = outer

    def begin(self, pe="", act="", dve="", pool="", rounds=1):
        steps = [Steps(at, names, rounds) for at, names in zip(self.at, (pe, act, dve, pool))]
        self.at = [s.end for s in steps]
        return steps


def half(t, h):
    return t[:, h * T:(h + 1) * T]


def product(nc, out, pairs):
    for c in range(0, out.shape[-1], BANK):
        for n, (lhsT, rhs) in enumerate(pairs):
            last = nc.tensor.matmul(out[:, c:c + BANK], lhsT, rhs[:, c:c + BANK],
                                    start=(n == 0), stop=(n == len(pairs) - 1))
    return last


def norms_pe(core, pe, items, S, ready=None):
    nc, (spe, sact, sdve, _) = core.nc, S
    for h, src, s, i, pre in items:
        if ready:
            ready(h)
        product(nc, core.slot[h][s[0]], [(core.centre_w[:, :], src)]).then_inc(core.pe_done[h], 1)
    for h, src, s, i, pre in items:
        pe.wait_ge(core.act_done[h], sact.value(pre + "square", i))
        product(nc, core.slot[h][s[1]], [(core.mean_w[:, :], core.sq[h])]).then_inc(core.pe_done[h], 1)


def norms_act(core, act, items, eps, S):
    nc, (spe, sact, sdve, _) = core.nc, S
    for h, src, s, i, pre in items:
        act.wait_ge(core.pe_done[h], spe.value(pre + "centre", i))
        nc.scalar.activation(core.sq[h], core.slot[h][s[0]], ACT.Square).then_inc(core.act_done[h], 1)
    for h, src, s, i, pre in items:
        act.wait_ge(core.pe_done[h], spe.value(pre + "var", i))
        nc.scalar.activation(core.sq[h], core.slot[h][s[1]], ACT.Ln, bias=core.eps[eps][:, :]).then_inc(core.act_done[h], 1)
    for h, src, s, i, pre in items:
        act.wait_ge(core.act_done[h], sact.value(pre + "log", i))
        nc.scalar.activation(core.sq[h], core.sq[h], ACT.Exp, scale=-0.5).then_inc(core.act_done[h], 1)


def norm_pe(core, pe, streams, src, s, S, ready=None):
    norms_pe(core, pe, [(h, src(h), s, 0, "") for h in streams], S, ready)


def norm_act(core, act, streams, eps, s, S):
    norms_act(core, act, [(h, None, s, 0, "") for h in streams], eps, S)


def norm_dve(core, dve, h, out, s, S, i=0, pre=""):
    nc, (spe, sact, sdve, _) = core.nc, S
    dve.wait_ge(core.act_done[h], sact.value(pre + "rstd", i))
    nc.vector.tensor_tensor(out, core.slot[h][s[0]], core.sq[h], ALU.mult).then_inc(core.dve_done[h], 1)


def start(core, x_in):
    nc = core.nc
    S = spe, sact, sdve, spool = core.begin("centre var", "square log rstd", "scaled",
                                            "zero eps6 eps5 one mean_w ident centre_w")
    x_landed = core.sem("x_landed")
    with nc.Block() as block:
        @block.sync
        def _(sp):
            sp.dma_start(core.x[:, :], x_in).then_inc(x_landed, 16)

        @block.gpsimd
        def _(pool):
            for h in BOTH:
                nc.gpsimd.memset(core.ident[:, :], 0.0).then_inc(core.pool_done[h], 1)
                nc.gpsimd.memset(core.eps[1e-6][:, :], 1e-6).then_inc(core.pool_done[h], 1)
                nc.gpsimd.memset(core.eps[1e-5][:, :], 1e-5).then_inc(core.pool_done[h], 1)
                nc.gpsimd.memset(core.one[:, :], 1.0).then_inc(core.pool_done[h], 1)
                nc.gpsimd.memset(core.mean_w[:, :], 1.0 / D).then_inc(core.pool_done[h], 1)
                pool.wait_ge(core.pool_done[h], spool.value("mean_w"))
                nc.gpsimd.affine_select(out=core.ident[:, :], in_=core.ident[:, :], compare_op=ALU.not_equal,
                                        fill=1.0, base=0, pattern=[[-1, P]], channel_multiplier=1
                                        ).then_inc(core.pool_done[h], 1)
                pool.wait_ge(core.pool_done[h], spool.value("ident"))
                nc.gpsimd.tensor_tensor(core.centre_w[:, :], core.ident[:, :], core.mean_w[:, :], ALU.subtract).then_inc(core.pool_done[h], 1)
                pool.wait_ge(core.pool_done[h], spool.value("centre_w"))

        @block.tensor
        def _(pe):
            pe.wait_ge(x_landed, 16)
            pe.wait_ge(core.pool_done[1], spool.value("centre_w"))
            norm_pe(core, pe, BOTH, lambda h: half(core.x, h), (0, 1), S)

        @block.scalar
        def _(act):
            norm_act(core, act, BOTH, 1e-5, (0, 1), S)

        @block.vector
        def _(dve):
            for h in BOTH:
                norm_dve(core, dve, h, half(core.xn, h), (0, 1), S)


def residual_norm(core):
    nc = core.nc
    S = spe, sact, sdve, spool = core.begin("centre var", "square log rstd", "scaled", "")
    with nc.Block() as block:
        @block.tensor
        def _(pe):
            norm_pe(core, pe, BOTH, lambda h: half(core.x, h), (0, 1), S)

        @block.scalar
        def _(act):
            norm_act(core, act, BOTH, 1e-5, (0, 1), S)

        @block.vector
        def _(dve):
            for h in BOTH:
                norm_dve(core, dve, h, half(core.xn, h), (0, 1), S)


STREAMS = 4
TS = N // STREAMS
EVERY = range(STREAMS)


class Streams:

    def __init__(self, core):
        self.nc, self.mean_w, self.centre_w, self.eps = core.nc, core.mean_w, core.centre_w, core.eps
        self.slot = [[core.slot[s // 2][s % 2][:, k * TS:(k + 1) * TS] for k in range(2)] for s in EVERY]
        self.pe_done, self.act_done, self.dve_done, self.pool_done = (
            [core.sem(f"{e}_stream{s}") for s in EVERY] for e in ("pe", "act", "dve", "pool"))
        self.cen = [core.cen_all[:, s * TS:(s + 1) * TS] for s in EVERY]
        self.sq = [core.sq_all[:, s * TS:(s + 1) * TS] for s in EVERY]


def linear_blocks(core, w_att, w_f1, w_f2, cols):
    nc = core.nc
    B = w_att.shape[0]
    FT = w_f1.shape[2] // P
    BQ, BK, BV, BO, L1S, L1B, L2S, L2B, BF2, BF1 = range(10)
    VECTORS = BF1 + FT
    FIRST, SECOND = (0, 1), (2, 3)
    NONE = ()
    st = Streams(core)
    S = spe, sact, sdve, spool = [Steps(0, text, B) for text in (
        "| q k v o n1centre n1var f0 f1 f2 f3 ff n2centre n2var |",
        "| relu_q exp_q relu_k exp_k gelu_o n1square n1log n1rstd h0 h1 h2 h3 gelu_ff n2square n2log n2rstd |",
        "enter | less_k K less_q Q kv total den recip mix n1scaled n1affine n2scaled n2affine |",
        "| res1 res2 | join")]
    att_landed, f1_landed, f2_landed, cols_landed, cols_ready = (
        core.sem(n) for n in ("att_landed", "f1_landed", "f2_landed", "cols_landed", "cols_ready"))
    with ExitStack() as ctx:
        sb = lambda name, shape, dt=F32: core.sb(name, shape, dt, ctx)
        per_stream = lambda name, *shape: [sb(f"{name}{s}", [P, *shape]) for s in EVERY]
        wa = sb("wa", [P, 4 * D])
        wf1 = sb("wf1", [P, FT * P])
        wf2 = sb("wf2", [P, FT, D])
        col = sb("col", [P, B, VECTORS])
        near = sb("near", [P, 2, VECTORS])
        cur, q, k = per_stream("cur", TS), per_stream("q", TS), per_stream("k", TS)
        mq, mk = per_stream("mq", TS), per_stream("mk", TS)
        hid = per_stream("hid", FT, TS)
        sums = per_stream("sums", 2)
        totals = per_stream("totals", 2)

        def segments(engine, segment, enter=None, leave=None):
            fixed = lambda i: lambda c: col[:, i, c:c + 1]
            now, ahead = (lambda c: near[:, 0, c:c + 1]), (lambda c: near[:, 1, c:c + 1])
            segment(FIRST, 0, fixed(0), NONE, 0, None)
            with engine.Fori(0, B - 1) as i:
                if enter:
                    enter(i)
                segment(SECOND, i, now, FIRST, i, now)
                segment(FIRST, i + 1, ahead, SECOND, i, now)
                if leave:
                    leave(i)
            segment(SECOND, B - 1, fixed(B - 1), FIRST, B - 1, fixed(B - 1))
            segment(NONE, 0, None, SECOND, B - 1, fixed(B - 1))

        def norms(att, i, net, j):
            return ([(s, k[s][:, :], (1, 0), j, "n2") for s in net] + [(s, k[s][:, :], (0, 1), i, "n1") for s in att])

        with nc.Block() as block:
            @block.sync
            def _(sp):
                sp.dma_start(col[:, :, :], cols).then_inc(cols_landed, 16)
                sp.dma_start(wa[:, :], w_att[0]).then_inc(att_landed, 16)
                sp.dma_start(wf1[:, :], w_f1[0]).then_inc(f1_landed, 16)
                sp.dma_start(wf2[:, :, :], w_f2[0]).then_inc(f2_landed, 16)
                with sp.Fori(0, B - 1) as i:
                    sp.wait_ge(st.pe_done[SECOND[1]], spe.value("o", i))
                    sp.dma_start(wa[:, :], w_att[i + 1]).then_inc(att_landed, 16)
                    sp.wait_ge(st.pe_done[SECOND[1]], spe.value("f3", i))
                    sp.dma_start(wf1[:, :], w_f1[i + 1]).then_inc(f1_landed, 16)
                    sp.wait_ge(st.pe_done[SECOND[1]], spe.value("ff", i))
                    sp.dma_start(wf2[:, :, :], w_f2[i + 1]).then_inc(f2_landed, 16)

            @block.tensor
            def _(pe):
                done = st.pe_done

                def segment(att, i, _ca, net, j, _cn):
                    if att:
                        pe.wait_ge(att_landed, i * 16 + 16)
                    for s in att:
                        pe.wait_ge(st.dve_done[s], sdve.before("n2affine", i))
                        product(nc, st.slot[s][0], [(wa[:, 0:D], cur[s][:, :])]).then_inc(done[s], 1)
                        product(nc, st.slot[s][1], [(wa[:, D:2 * D], cur[s][:, :])]).then_inc(done[s], 1)
                    if net:
                        pe.wait_ge(f1_landed, j * 16 + 16)
                    for f in range(FT):
                        for s in net:
                            if f == 0:
                                pe.wait_ge(st.dve_done[s], sdve.value("n1affine", j))
                            if f >= 2:
                                pe.wait_ge(st.act_done[s], sact.value(f"h{f - 2}", j))
                            product(nc, st.slot[s][f % 2], [(wf1[:, f * P:(f + 1) * P], q[s][:, :])]).then_inc(done[s], 1)
                        if f == 1:
                            for s in att:
                                pe.wait_ge(st.act_done[s], sact.value("exp_q", i))
                                product(nc, st.slot[s][0], [(wa[:, 2 * D:3 * D], cur[s][:, :])]).then_inc(done[s], 1)
                    if net:
                        pe.wait_ge(f2_landed, j * 16 + 16)
                    for s in net:
                        pe.wait_ge(st.act_done[s], sact.value(f"h{FT - 1}", j))
                        product(nc, st.slot[s][0], [(wf2[:, f, :], hid[s][:, f, :]) for f in range(FT)]).then_inc(done[s], 1)
                    for s in att:
                        pe.wait_ge(st.dve_done[s], sdve.value("mix", i))
                        product(nc, st.slot[s][1], [(wa[:, 3 * D:4 * D], mq[s][:, :])]).then_inc(done[s], 1)
                    norms_pe(st, pe, norms(att, i, net, j), S, ready=lambda s: pe.wait_ge(
                        st.pool_done[s], spool.value("res1", i) if s in att else spool.value("res2", j)))

                segments(pe, segment)

            @block.scalar
            def _(act):
                done = st.act_done
                act.wait_ge(cols_landed, 16)

                def segment(att, i, ca, net, j, cn):
                    for s in att:
                        act.wait_ge(st.pe_done[s], spe.value("q", i))
                        nc.scalar.activation(q[s][:, :], st.slot[s][0], ACT.Relu, bias=ca(BQ)).then_inc(done[s], 1)
                        nc.scalar.activation(mq[s][:, :], st.slot[s][0], ACT.Exp, bias=ca(BQ)).then_inc(done[s], 1)
                        act.wait_ge(st.pe_done[s], spe.value("k", i))
                        nc.scalar.activation(k[s][:, :], st.slot[s][1], ACT.Relu, bias=ca(BK)).then_inc(done[s], 1)
                        nc.scalar.activation(mk[s][:, :], st.slot[s][1], ACT.Exp, bias=ca(BK)).then_inc(done[s], 1)
                    for f in range(FT):
                        for s in net:
                            act.wait_ge(st.pe_done[s], spe.value(f"f{f}", j))
                            nc.scalar.activation(hid[s][:, f, :], st.slot[s][f % 2], ACT.Gelu_apprx_tanh, bias=cn(BF1 + f)).then_inc(done[s], 1)
                    for s in net:
                        act.wait_ge(st.pe_done[s], spe.value("ff", j))
                        nc.scalar.activation(mk[s][:, :], st.slot[s][0], ACT.Gelu_apprx_tanh, bias=cn(BF2)).then_inc(done[s], 1)
                    for s in att:
                        act.wait_ge(st.pe_done[s], spe.value("o", i))
                        nc.scalar.activation(mk[s][:, :], st.slot[s][1], ACT.Gelu_apprx_tanh, bias=ca(BO)).then_inc(done[s], 1)
                    norms_act(st, act, norms(att, i, net, j), 1e-6, S)

                segments(act, segment, enter=lambda i: act.wait_ge(cols_ready, i + 1))

            @block.vector
            def _(dve):
                done = st.dve_done
                for s in EVERY:
                    nc.vector.tensor_copy(cur[s][:, :], core.xn[:, s * TS:(s + 1) * TS]).then_inc(done[s], 1)
                dve.wait_ge(cols_landed, 16)

                def segment(att, i, ca, net, j, cn):
                    for s in att:
                        dve.wait_ge(st.act_done[s], sact.value("exp_k", i))
                        for n, m, t, total in (("k", mk[s], k[s], dict(accum_out=sums[s][:, 0:1])), ("q", mq[s], q[s], {})):
                            nc.vector.tensor_scalar(m[:, :], m[:, :], 1.0, -1.0, ALU.min, ALU.add).then_inc(done[s], 1)
                            dve.wait_ge(done[s], sdve.value(f"less_{n}", i))
                            nc.vector.scalar_tensor_tensor(out=t[:, :], in0=t[:, :], scalar=1.0, in1=m[:, :],
                                                           op0=ALU.add, op1=ALU.add, **total).then_inc(done[s], 1)
                    for s in att:
                        dve.wait_ge(done[s], sdve.value("Q", i))
                        dve.wait_ge(st.pe_done[s], spe.value("v", i))
                        nc.vector.scalar_tensor_tensor(out=mk[s][:, :], in0=st.slot[s][0], scalar=ca(BV), in1=k[s][:, :],
                                                       op0=ALU.add, op1=ALU.mult, accum_out=sums[s][:, 1:2]).then_inc(done[s], 1)
                    for s in att:
                        dve.wait_ge(done[s], sdve.value("kv", i))
                    for s in att:
                        nc.vector.tensor_tensor(totals[s][:, :], sums[att[0]][:, :], sums[att[1]][:, :], ALU.add).then_inc(done[s], 1)
                    for s in att:
                        dve.wait_ge(done[s], sdve.value("total", i))
                        nc.vector.tensor_scalar(mk[s][:, :], q[s][:, :], totals[s][:, 0:1], 1e-6, ALU.mult, ALU.add).then_inc(done[s], 1)
                        dve.wait_ge(done[s], sdve.value("den", i))
                        nc.vector.reciprocal(mk[s][:, :], mk[s][:, :]).then_inc(done[s], 1)
                        dve.wait_ge(done[s], sdve.value("recip", i))
                        nc.vector.scalar_tensor_tensor(out=mq[s][:, :], in0=q[s][:, :], scalar=totals[s][:, 1:2], in1=mk[s][:, :],
                                                       op0=ALU.mult, op1=ALU.mult).then_inc(done[s], 1)
                    for s in net:
                        norm_dve(st, dve, s, st.cen[s], (1, 0), S, j, "n2")
                        dve.wait_ge(done[s], sdve.value("n2scaled", j))
                        nc.vector.tensor_scalar(cur[s][:, :], st.cen[s], cn(L2S), cn(L2B), ALU.mult, ALU.add).then_inc(done[s], 1)
                    for s in att:
                        norm_dve(st, dve, s, st.cen[s], (0, 1), S, i, "n1")
                        dve.wait_ge(done[s], sdve.value("n1scaled", i))
                        nc.vector.tensor_scalar(q[s][:, :], st.cen[s], ca(L1S), ca(L1B), ALU.mult, ALU.add).then_inc(done[s], 1)

                def enter(i):
                    nc.vector.tensor_copy(near[:, :, :], col[:, bass.ds(i, 2), :]).then_inc(cols_ready, 1)
                    dve.wait_ge(cols_ready, i + 1)

                def leave(i):
                    for s in FIRST:
                        dve.wait_ge(done[s], sdve.value("n1affine", i + 1))
                    for s in SECOND:
                        dve.wait_ge(done[s], sdve.value("n2affine", i))

                segments(dve, segment, enter, leave)

            @block.gpsimd
            def _(pool):
                done = st.pool_done

                def segment(att, i, _ca, net, j, _cn):
                    for s in net:
                        pool.wait_ge(st.act_done[s], sact.value("gelu_ff", j))
                        nc.gpsimd.tensor_tensor(k[s][:, :], mk[s][:, :], q[s][:, :], ALU.add).then_inc(done[s], 1)
                    for s in att:
                        pool.wait_ge(st.act_done[s], sact.value("gelu_o", i))
                        nc.gpsimd.tensor_tensor(k[s][:, :], mk[s][:, :], cur[s][:, :], ALU.add).then_inc(done[s], 1)

                segments(pool, segment)
                for s in EVERY:
                    pool.wait_ge(st.dve_done[s], sdve.value("n2affine", B - 1))
                    x = core.x[:, s * TS:(s + 1) * TS]
                    nc.gpsimd.tensor_tensor(x, x, cur[s][:, :], ALU.add).then_inc(done[s], 1)


HEADS, HD = 16, 8
GROUPS, GH = 4, 4
KT = T // P
TERMS = 6
Q_PARTS, K_PARTS = (0, 0, 1, 0, 2, 1), (0, 1, 0, 2, 0, 1)
ROWS = TERMS * HD


def attention_inputs(core, w_qk, w_v, cols, v_bias, q_dram, k_dram, v_dram):
    nc = core.nc
    S = spe, sact, sdve, spool = core.begin(
        "q k v", "q k", "q0 qr0 q1 qr1 q2 k0 kr0 k1 kr1 k2 v", "")
    att_w, stacked = core.sem("att_w"), core.sem("stacked")
    with ExitStack() as ctx:
        sb = lambda name, shape, dt=F32: core.sb(name, shape, dt, ctx)
        wqk = sb("wqk", [P, 2 * D])
        wv = sb("wv", [P, D])
        col = sb("colqk", [P, 2])
        vb = sb("vb", [P, D])
        full = [[sb(f"full{h}{i}", [P, T]) for i in range(2)] for h in BOTH]
        part = [[[sb(f"part{h}{i}{n}", [P, T], BF16) for n in range(3)] for i in range(2)] for h in BOTH]
        v = [sb(f"v{h}", [P, KT, D]) for h in BOTH]
        with nc.Block() as block:
            @block.sync
            def _(sp):
                sp.dma_start(wqk[:, :], w_qk).then_inc(att_w, 16)
                sp.dma_start(col[:, :], cols).then_inc(att_w, 16)
                sp.dma_start(wv[:, :], w_v).then_inc(att_w, 16)
                sp.dma_start(vb[:, :], v_bias.partition_broadcast(P)).then_inc(att_w, 16)
                for h in BOTH:
                    for i, (dram, parts, n) in enumerate(((q_dram, Q_PARTS, "q"), (k_dram, K_PARTS, "k"))):
                        sp.wait_ge(core.dve_done[h], sdve.value(f"{n}2"))
                        rows = dram[h].rearrange("g j (t d) x -> t (g j) d x", d=HD)
                        for t, p in enumerate(parts):
                            sp.dma_start(rows[t], part[h][i][p][:, :]).then_inc(stacked, 16)
                    sp.wait_ge(core.dve_done[h], sdve.value("v"))
                    for g in range(GROUPS):
                        sp.dma_start(v_dram[h, g], v[h][:, :, g * GH * HD:(g + 1) * GH * HD]).then_inc(stacked, 16)
                sp.wait_ge(stacked, HALVES * (2 * TERMS + GROUPS) * 16)

            @block.tensor
            def _(pe):
                pe.wait_ge(att_w, 64)
                for h in BOTH:
                    x = half(core.xn, h)
                    product(nc, core.slot[h][0], [(wqk[:, 0:D], x)]).then_inc(core.pe_done[h], 1)
                    product(nc, core.slot[h][1], [(wqk[:, D:2 * D], x)]).then_inc(core.pe_done[h], 1)
                for h in BOTH:
                    x = half(core.xn, h)
                    pe.wait_ge(core.act_done[h], sact.value("q"))
                    for t in range(KT):
                        last = nc.tensor.matmul(core.slot[h][0][:, t * D:(t + 1) * D], x[:, t * P:(t + 1) * P], wv[:, :],
                                                start=(t % 4 == 0), stop=(t % 4 == 3), skip_group_check=True)
                    last.then_inc(core.pe_done[h], 1)

            @block.scalar
            def _(act):
                act.wait_ge(att_w, 64)
                for h in BOTH:
                    for i, n in enumerate("qk"):
                        act.wait_ge(core.pe_done[h], spe.value(n))
                        nc.scalar.activation(full[h][i][:, :], core.slot[h][i][:, :], ACT.Identity,
                                             bias=col[:, i:i + 1]).then_inc(core.act_done[h], 1)

            @block.vector
            def _(dve):
                dve.wait_ge(att_w, 64)
                for h in BOTH:
                    done = core.dve_done[h]
                    for i, n in enumerate("qk"):
                        f, p = full[h][i], part[h][i]
                        dve.wait_ge(core.act_done[h], sact.value(n))
                        nc.vector.tensor_copy(p[0][:, :], f[:, :]).then_inc(done, 1)
                        for m in range(2):
                            dve.wait_ge(done, sdve.value(f"{n}{m}"))
                            nc.vector.tensor_tensor(f[:, :], f[:, :], p[m][:, :], ALU.subtract).then_inc(done, 1)
                            dve.wait_ge(done, sdve.value(f"{n}r{m}"))
                            nc.vector.tensor_copy(p[m + 1][:, :], f[:, :]).then_inc(done, 1)
                    dve.wait_ge(core.pe_done[h], spe.value("v"))
                    nc.vector.tensor_tensor(v[h][:, :, :], core.slot[h][0].rearrange("p (t d) -> p t d", d=D),
                                            vb[:, :].rearrange("p (a d) -> p a d", a=1).to_broadcast([P, KT, D]),
                                            ALU.add).then_inc(done, 1)


def attention(core, q_dram, k_dram, v_dram, mixed):
    nc = core.nc
    scale = float(HD) ** -0.5
    UNITS = GH * KT
    SEARCH = 3
    MAXES = 2 * UNITS
    RING = MAXES + 4
    sem = core.sem
    ones_set, ones_landed, stack_landed, v_landed = sem("ones_set"), sem("ones_landed"), [sem(f"stack_landed{h}") for h in BOTH], [sem(f"v_landed{h}") for h in BOTH]
    rows_cleared = sem("rows_cleared")
    scores_ready, weights_ready, weights_used = sem("scores_ready"), sem("weights_ready"), sem("weights_used")
    bank_ready, bank_free, maxima_found, maxima_landed = sem("bank_ready"), sem("bank_free"), sem("maxima_found"), sem("maxima_landed")
    sums_copied, sums_inverted, heads_done = sem("sums_copied"), sem("sums_inverted"), sem("heads_done")
    READY, COPIED = 2, 1
    with ExitStack() as ctx:
        sb = lambda name, shape, dt=F32: core.sb(name, shape, dt, ctx)
        qs = [sb(f"qs{h}", [P, GH, T], BF16) for h in BOTH]
        ks = [sb(f"ks{h}", [P, GH, T], BF16) for h in BOTH]
        zeros = sb("zeros", [GH, T], BF16)
        vg = [sb(f"vg{h}", [P, KT, GH, 32]) for h in BOTH]
        ones = sb("ones", [GH, T], BF16)
        spread = sb("spread", [P, P])
        weights = sb("weights", [P, 2, GH, T])
        best = sb("best", [P, UNITS, 2])
        neg = sb("neg", [P, UNITS])
        negb = [sb(f"negb{i}", [UNITS // 2, P], BF16) for i in range(2)]
        raw = sb("raw", [P, T])
        inv = sb("inv", [P, T])
        score = [core.quad[0][:, i * T:(i + 1) * T] for i in range(2)]
        out = core.quad[1][:, 0:T]
        bank = [core.quad[1][:, T + i * BANK:T + (i + 1) * BANK] for i in range(2)]

        def use(n, k):
            return k + 2 if isinstance(n, int) and n < 0 else n * RING + (RING + k)

        with nc.Block() as block:
            @block.sync
            def _(sp):
                sp.wait_ge(ones_set, 7)
                sp.wait_ge(rows_cleared, 2 * HALVES)
                for h in BOTH:
                    sp.dma_start(ks[h][ROWS:ROWS + 1, :, :], ones[:, :]).then_inc(ones_landed, 16)

                def load(h, g):
                    sp.dma_start(qs[h][ROWS:ROWS + 1, :, :], zeros[:, :]).then_inc(stack_landed[h], 16)
                    sp.dma_start(qs[h][0:ROWS, :, :], q_dram[h, g].rearrange("j r t -> r j t")).then_inc(stack_landed[h], 16)
                    sp.dma_start(ks[h][0:ROWS, :, :], k_dram[h, g].rearrange("j r t -> r j t")).then_inc(stack_landed[h], 16)
                    sp.dma_start(vg[h][:, :, :, 0:HD].rearrange("p t j d -> p (t j) d"),
                                 v_dram[h, g].rearrange("p t (j d) -> p (t j) d", d=HD)).then_inc(v_landed[h], 16)

                def maxima_rows(n, h):
                    for i in range(2):
                        sp.wait_ge(bank_free, use(n - 1, MAXES + i + 1))
                        for j in range(2):
                            sp.dma_start(qs[h][ROWS:ROWS + 1, 2 * i + j, :], negb[i][j * KT:(j + 1) * KT, :]).then_inc(maxima_landed, 16)

                load(0, 0)
                load(1, 0)
                maxima_rows(0, 0)

                def turn(n, h, g, more):
                    if h == 0 or more:
                        maxima_rows(n + 1, 1 - h)
                    if more:
                        sp.wait_ge(weights_used, n * KT + KT)
                        load(h, g + 1)

                with sp.Fori(0, GROUPS - 1) as g:
                    for h in BOTH:
                        turn(g * 2 + h, h, g, True)
                for h in BOTH:
                    turn(2 * GROUPS - 2 + h, h, GROUPS - 1, False)

            @block.gpsimd
            def _(pool):
                nc.gpsimd.memset(ones[:, :], 1.0).then_inc(ones_set, 1)
                nc.gpsimd.memset(zeros[:, :], 0.0).then_inc(ones_set, 1)
                nc.gpsimd.memset(spread[:, :], 0.0).then_inc(ones_set, 1)
                for h in BOTH:
                    nc.gpsimd.memset(vg[h][:, :, :, HD:32], 0.0).then_inc(ones_set, 1)
                pool.wait_ge(ones_set, 5)
                for h in BOTH:
                    nc.gpsimd.memset(vg[h][:, :, :, HD:HD + 1], 1.0).then_inc(ones_set, 1)
                nc.gpsimd.affine_select(out=spread[:, :].rearrange("p (j c) -> p j c", c=32),
                                        in_=spread[:, :].rearrange("p (j c) -> p j c", c=32),
                                        compare_op=ALU.not_equal, fill=1.0, base=-HD,
                                        pattern=[[-32, GH], [0, 32]], channel_multiplier=1).then_inc(ones_set, 1)

            @block.tensor
            def _(pe):
                pe.wait_ge(ones_set, 8)
                pe.wait_ge(ones_landed, 32)
                pe.sem_inc(bank_ready, 2)

                def maxima(n, h, g, lo, hi):
                    for k in range(lo, hi):
                        j, qt, c = k // (2 * KT), k // 2 % KT, k % 2
                        if k == 0:
                            pe.wait_ge(stack_landed[h], g * 48 + 48)
                        pe.wait_ge(bank_free, use(n - 1, k - 1))
                        nc.tensor.matmul(bank[k % 2], qs[h][:, j, qt * P:(qt + 1) * P], ks[h][:, j, c * BANK:(c + 1) * BANK],
                                         start=True, stop=True).then_inc(bank_ready, 1)

                def turned(n):
                    for i in range(2):
                        pe.wait_ge(bank_free, use(n - 1, MAXES + i - 1))
                        pe.wait_ge(maxima_found, n + 1)
                        nc.tensor.transpose(bank[i][0:UNITS // 2, 0:P], neg[:, i * UNITS // 2:(i + 1) * UNITS // 2],
                                            core.ident[:, :]).then_inc(bank_ready, 1)

                def scores(n, h, kt, j):
                    if kt == 0 and j == 0:
                        pe.wait_ge(maxima_landed, n * 64 + 64)
                    pe.wait_ge(weights_ready, n * UNITS + (kt * GH + j - 2 + 1 + READY))
                    for c in range(2):
                        last = nc.tensor.matmul(score[j % 2][:, c * BANK:(c + 1) * BANK], ks[h][:, j, kt * P:(kt + 1) * P],
                                                qs[h][:, j, c * BANK:(c + 1) * BANK], start=True, stop=True)
                    last.then_inc(scores_ready, 1)

                def weighted(n, h, g, kt, c):
                    if kt == 0 and c == 0:
                        pe.wait_ge(v_landed[h], g * 16 + 16)
                        pe.wait_ge(sums_copied, n + COPIED)
                    if c == 0:
                        pe.wait_ge(weights_ready, n * UNITS + (kt * GH + GH + READY))
                    for j in range(GH):
                        last = nc.tensor.matmul(out[32 * j:32 * j + 32, c * BANK:(c + 1) * BANK], vg[h][:, kt, j, :],
                                                weights[:, kt % 2, j, c * BANK:(c + 1) * BANK], start=(kt == 0), stop=(kt == KT - 1))
                    if c == 1:
                        last.then_inc(weights_used, 1)

                def sums(n, first):
                    pe.wait_ge(sums_copied, n + 1 + COPIED)
                    for c in range(2):
                        pe.wait_ge(bank_free, use(n, first + c - 1))
                        nc.tensor.matmul(bank[c], spread[:, :], raw[:, c * BANK:(c + 1) * BANK], start=True, stop=True).then_inc(bank_ready, 1)

                def turn(n, h, g, more):
                    ahead = h == 0 or more
                    g2 = g if h == 0 else g + 1
                    searched = 0
                    for kt in range(KT):
                        for j in range(GH):
                            scores(n, h, kt, j)
                            if kt and j % 2:
                                weighted(n, h, g, kt - 1, j // 2)
                            if ahead and kt:
                                upto = min(((kt - 1) * GH + j + 1) * SEARCH, MAXES)
                                maxima(n + 1, 1 - h, g2, searched, upto)
                                searched = upto
                        if ahead and kt == KT - 1:
                            turned(n + 1)
                    for c in range(2):
                        weighted(n, h, g, KT - 1, c)
                    sums(n, MAXES + 2 if ahead else 0)

                maxima(0, 0, 0, 0, MAXES)
                turned(0)
                with pe.Fori(0, GROUPS - 1) as g:
                    for h in BOTH:
                        turn(g * 2 + h, h, g, True)
                for h in BOTH:
                    turn(2 * GROUPS - 2 + h, h, GROUPS - 1, False)

            @block.scalar
            def _(act):
                act.sem_inc(weights_ready, READY)

                def turn(n):
                    for kt in range(KT):
                        act.wait_ge(weights_used, n * KT + kt - 1) if not isinstance(n, int) or n * KT + kt - 1 > 0 else None
                        for j in range(GH):
                            act.wait_ge(scores_ready, n * UNITS + (kt * GH + j + 1))
                            nc.scalar.activation(weights[:, kt % 2, j, :], score[j % 2], ACT.Exp, scale=scale).then_inc(weights_ready, 1)

                turn(0)
                with act.Fori(1, 2 * GROUPS) as n:
                    turn(n)

            @block.vector
            def _(dve):
                for h in BOTH:
                    for stack in (qs, ks):
                        nc.vector.memset(stack[h][:, :, :], 0.0).then_inc(rows_cleared, 1)
                dve.sem_inc(bank_free, 2)
                dve.sem_inc(sums_copied, COPIED)

                def maxima(n, h):
                    dve.wait_ge(maxima_found, n) if not isinstance(n, int) or n else None
                    for k in range(MAXES):
                        dve.wait_ge(bank_ready, use(n - 1, k + 1))
                        nc.vector.tensor_reduce(best[:, k // 2, k % 2:k % 2 + 1], bank[k % 2], AX.X, ALU.max).then_inc(bank_free, 1)
                    dve.wait_ge(bank_free, use(n - 1, MAXES))
                    nc.vector.tensor_reduce(neg[:, :], best[:, :, :], AX.X, ALU.max, negate=True).then_inc(maxima_found, 1)
                    if not isinstance(n, int) or n:
                        dve.wait_ge(maxima_landed, n * 64)
                    for i in range(2):
                        dve.wait_ge(bank_ready, use(n - 1, MAXES + i + 1))
                        nc.vector.tensor_copy(negb[i][:, :], bank[i][0:UNITS // 2, 0:P]).then_inc(bank_free, 1)

                def turn(n, h, g, more):
                    ahead = h == 0 or more
                    if ahead:
                        maxima(n + 1, 1 - h)
                    first = MAXES + 2 if ahead else 0
                    dve.wait_ge(weights_used, n * KT + KT)
                    if not isinstance(n, int) or n:
                        dve.wait_ge(heads_done, n)
                    nc.vector.tensor_copy(raw[:, :], out).then_inc(sums_copied, 1)
                    for c in range(2):
                        dve.wait_ge(bank_ready, use(n, first + c + 1))
                        nc.vector.reciprocal(inv[:, c * BANK:(c + 1) * BANK], bank[c]).then_inc(bank_free, 1)
                    dve.wait_ge(bank_free, use(n, first + 2))
                    dve.wait_ge(sums_copied, n + 1 + COPIED)
                    at = mixed[h][:, g, :] if isinstance(g, int) else mixed[h][:, bass.ds(g, 1), :].rearrange("p a t -> p (a t)")
                    nc.vector.tensor_tensor(at, raw[:, :], inv[:, :], ALU.mult).then_inc(heads_done, 1)

                maxima(0, 0)
                with dve.Fori(0, GROUPS - 1) as g:
                    for h in BOTH:
                        turn(g * 2 + h, h, g, True)
                for h in BOTH:
                    turn(2 * GROUPS - 2 + h, h, GROUPS - 1, False)


def attention_output(core, w_out, cols, mixed, x1):
    nc = core.nc
    S = spe, sact, sdve, spool = core.begin("o centre var", "square log rstd", "res scaled affine", "w_zero")
    out_w, cols_landed = core.sem("out_w"), core.sem("out_cols")
    with ExitStack() as ctx:
        sb = lambda name, shape, dt=F32: core.sb(name, shape, dt, ctx)
        w = sb("wout", [P, GROUPS, D])
        col = sb("colout", [P, 3])
        res = [sb(f"res{h}", [P, T]) for h in BOTH]
        with nc.Block() as block:
            @block.sync
            def _(sp):
                sp.dma_start(col[:, :], cols).then_inc(cols_landed, 16)
                sp.wait_ge(core.pool_done[1], spool.value("w_zero"))
                for j in range(GH):
                    sp.dma_start(w[32 * j:32 * j + HD, :, :], w_out[j]).then_inc(out_w, 16)

            @block.gpsimd
            def _(pool):
                for h in BOTH:
                    if h:
                        pool.wait_ge(core.pool_done[0], spool.value("w_zero"))
                    nc.gpsimd.memset(w[:, :, :], 0.0).then_inc(core.pool_done[h], 1)

            @block.tensor
            def _(pe):
                pe.wait_ge(out_w, GH * 16)
                for h in BOTH:
                    product(nc, core.slot[h][0], [(w[:, g, :], mixed[h][:, g, :]) for g in range(GROUPS)]).then_inc(core.pe_done[h], 1)
                norm_pe(core, pe, BOTH, lambda h: res[h][:, :], (0, 1), S,
                        ready=lambda h: pe.wait_ge(core.dve_done[h], sdve.value("res")))

            @block.scalar
            def _(act):
                norm_act(core, act, BOTH, 1e-5, (0, 1), S)

            @block.vector
            def _(dve):
                dve.wait_ge(cols_landed, 16)
                for h in BOTH:
                    dve.wait_ge(core.pe_done[h], spe.value("o"))
                    nc.vector.scalar_tensor_tensor(out=res[h][:, :], in0=core.slot[h][0], scalar=col[:, 0:1], in1=half(core.xn, h),
                                                   op0=ALU.add, op1=ALU.add).then_inc(core.dve_done[h], 1)
                for h in BOTH:
                    norm_dve(core, dve, h, core.cen[h], (0, 1), S)
                    dve.wait_ge(core.dve_done[h], sdve.value("scaled"))
                    nc.vector.tensor_scalar(half(x1, h), core.cen[h], col[:, 1:2], col[:, 2:3], ALU.mult, ALU.add).then_inc(core.dve_done[h], 1)


TILES = N // P


def chained(eng, chained_steps, base=0):
    count = [base]

    def link(ins):
        count[0] += 1
        ins.then_inc(chained_steps, 1)
        eng.wait_ge(chained_steps, count[0])
    return link


def over_tiles(v, n):
    if v.shape[-1] == TILES:
        return v.rearrange("p (t a) -> p t a", a=1).to_broadcast([P, TILES, n])
    return v.rearrange("p (a n) -> p a n", a=1).to_broadcast([P, TILES, n])


def first_best(nc, link, chosen, values, count, top, late, least):
    n = values.shape[-1]
    link(nc.vector.tensor_reduce(top, values, AX.X, ALU.max))
    link(nc.vector.tensor_tensor(late, values, over_tiles(top, n), ALU.is_lt))
    link(nc.vector.scalar_tensor_tensor(out=late, in0=late, scalar=100.0, in1=over_tiles(count, n), op0=ALU.mult, op1=ALU.add))
    link(nc.vector.tensor_reduce(least, late, AX.X, ALU.min))
    link(nc.vector.tensor_tensor(chosen, late, over_tiles(least, n), ALU.is_equal))


def route(core, name, src, w_router, b_router, kind, E, comb_dram, cap=None):
    nc = core.nc
    EP = 8 if E <= 8 else 16
    R = w_router.shape[1]
    BLOCKS = TILES * EP // P
    w_landed, b_landed, set_up, logits_ready = (core.sem(f"{name}_{n}") for n in ("w_landed", "b_landed", "set_up", "logits_ready"))
    steps, shifted, exps_ready = (core.sem(f"{name}_{n}") for n in ("steps", "shifted", "exps_ready"))
    counted, counts_ready, comb_ready, turned, turned_copied, stored = (
        core.sem(f"{name}_{n}") for n in ("counted", "counts_ready", "comb_ready", "turned", "turned_copied", "stored"))
    with ExitStack() as ctx:
        sb = lambda n, shape, dt=F32: core.sb(f"{name}_{n}", shape, dt, ctx)
        w = sb("w", [P, R])
        b = sb("b", [P, R])
        logits = sb("logits", [P, TILES, R])
        exps = sb("exps", [P, TILES, R])
        comb = sb("comb", [P, TILES, EP])
        count = sb("count", [P, EP])
        one_hot, two_hot, late = (sb(n, [P, TILES, 16]) for n in ("one_hot", "two_hot", "late"))
        top, least, total, scale = (sb(n, [P, TILES]) for n in ("top", "least", "total", "scale"))
        pairs = [sb(f"pairs{i}", [P, TILES, 4]) for i in range(4)]
        load = sb("load", [P, EP])
        turned_comb = sb("turned_comb", [P, BLOCKS, P])
        psum = core.quad[0][:, 0:TILES * R].rearrange("p (t r) -> p t r", r=R)
        with nc.Block() as block:
            @block.sync
            def _(sp):
                sp.dma_start(w[:, :], w_router).then_inc(w_landed, 16)
                if b_router is not None:
                    sp.dma_start(b[:, :], b_router.partition_broadcast(P)).then_inc(b_landed, 16)
                sp.wait_ge(turned_copied, 1)
                rows = comb_dram.rearrange("e (b t p) -> b t e p", b=BLOCKS, p=P)
                for i in range(BLOCKS):
                    sp.dma_start(rows[i], turned_comb[:, i, :]).then_inc(stored, 16)
                sp.wait_ge(stored, 16 * BLOCKS)

            @block.gpsimd
            def _(pool):
                nc.gpsimd.iota(count[:, :], pattern=[[1, EP]], base=0, channel_multiplier=0,
                               allow_small_or_imprecise_dtypes=True).then_inc(set_up, 1)
                nc.gpsimd.memset(comb[:, :, :], 0.0).then_inc(set_up, 1)

            @block.tensor
            def _(pe):
                pe.wait_ge(w_landed, 16)
                for t in range(TILES):
                    last = nc.tensor.matmul(psum[:, t, :], src[:, t * P:(t + 1) * P], w[:, :], start=(t == 0),
                                            stop=(t == TILES - 1), skip_group_check=True)
                last.then_inc(logits_ready, 1)
                if kind == "capped":
                    pe.wait_ge(counted, 1)
                    nc.tensor.matmul(core.quad[1][:, 0:EP], core.mean_w[:, :], load[:, :], start=True, stop=True).then_inc(counts_ready, 1)
                pe.wait_ge(comb_ready, 1)
                for i in range(BLOCKS):
                    n = TILES // BLOCKS
                    last = nc.tensor.transpose(core.quad[0][:, i * P:(i + 1) * P],
                                               comb[:, i * n:(i + 1) * n, :].rearrange("p t e -> p (t e)"), core.ident[:, :])
                last.then_inc(turned, 1)

            @block.scalar
            def _(act):
                act.wait_ge(shifted, 1)
                nc.scalar.activation(exps[:, :, :], exps[:, :, :], ACT.Exp).then_inc(exps_ready, 1)

            @block.vector
            def _(dve):
                link = chained(dve, steps)
                dve.wait_ge(set_up, 2)
                dve.wait_ge(logits_ready, 1)
                if b_router is None:
                    link(nc.vector.tensor_copy(logits[:, :, :], psum))
                else:
                    dve.wait_ge(b_landed, 16)
                    link(nc.vector.tensor_tensor(logits[:, :, :], psum, over_tiles(b[:, :], R), ALU.add))
                if kind == "groups":
                    G = R - E
                    group, expert = logits[:, :, 0:G], logits[:, :, G:R]
                    first, second = (expert.rearrange("p t (g e) -> p t g e", e=2)[:, :, :, e] for e in range(2))
                    better, lesser, group_w, pair_w = (p[:, :, :] for p in pairs)
                    first_best(nc, link, one_hot[:, :, 0:G], group, count[:, 0:G], top[:, :], late[:, :, 0:G], least[:, :])
                    link(nc.vector.tensor_tensor(exps[:, :, 0:G], group, over_tiles(top[:, :], G), ALU.subtract))
                    link(nc.vector.tensor_tensor(better, first, second, ALU.max))
                    for e, v in enumerate((first, second)):
                        out = exps[:, :, G:R].rearrange("p t (g e) -> p t g e", e=2)[:, :, :, e]
                        last = nc.vector.tensor_tensor(out, v, better, ALU.subtract)
                        if e == 0:
                            link(last)
                    last.then_inc(shifted, 1)
                    dve.wait_ge(exps_ready, 1)
                    e_first, e_second = (exps[:, :, G:R].rearrange("p t (g e) -> p t g e", e=2)[:, :, :, e] for e in range(2))
                    link(nc.vector.tensor_reduce(total[:, :], exps[:, :, 0:G], AX.X, ALU.add))
                    link(nc.vector.reciprocal(scale[:, :], total[:, :]))
                    link(nc.vector.tensor_tensor(lesser, e_first, e_second, ALU.add))
                    link(nc.vector.reciprocal(pair_w, lesser))
                    link(nc.vector.tensor_tensor(group_w, one_hot[:, :, 0:G], over_tiles(scale[:, :], G), ALU.mult))
                    link(nc.vector.tensor_tensor(pair_w, pair_w, group_w, ALU.mult))
                    link(nc.vector.tensor_tensor(lesser, first, second, ALU.is_ge))
                    out = comb[:, :, :].rearrange("p t (g e) -> p t g e", e=2)
                    link(nc.vector.tensor_tensor(out[:, :, :, 0], pair_w, lesser, ALU.mult))
                    nc.vector.tensor_tensor(out[:, :, :, 1], pair_w, out[:, :, :, 0], ALU.subtract).then_inc(comb_ready, 1)
                else:
                    one, two = one_hot[:, :, 0:E], two_hot[:, :, 0:E]
                    first_best(nc, link, one, logits[:, :, :], count[:, 0:E], top[:, :], late[:, :, 0:E], least[:, :])
                    nc.vector.tensor_tensor(exps[:, :, :], logits[:, :, :], over_tiles(top[:, :], E), ALU.subtract).then_inc(shifted, 1)
                    dve.wait_ge(shifted, 1)
                    link(nc.vector.scalar_tensor_tensor(out=logits[:, :, :], in0=one, scalar=-1e30, in1=logits[:, :, :],
                                                        op0=ALU.mult, op1=ALU.add))
                    first_best(nc, link, two, logits[:, :, :], count[:, 0:E], top[:, :], late[:, :, 0:E], least[:, :])
                    link(nc.vector.tensor_tensor(one, one, two, ALU.add))
                    dve.wait_ge(exps_ready, 1)
                    link(nc.vector.tensor_reduce(total[:, :], exps[:, :, :], AX.X, ALU.add))
                    link(nc.vector.reciprocal(scale[:, :], total[:, :]))
                    link(nc.vector.tensor_tensor(exps[:, :, :], exps[:, :, :], over_tiles(scale[:, :], E), ALU.mult))
                    out = comb[:, :, 0:E]
                    if kind == "capped":
                        nc.vector.tensor_reduce(load[:, :], one.rearrange("p t e -> p e t"), AX.X, ALU.add).then_inc(counted, 1)
                        link(nc.vector.tensor_tensor(exps[:, :, :], exps[:, :, :], one, ALU.mult))
                        dve.wait_ge(counts_ready, 1)
                        link(nc.vector.tensor_scalar(late[:, 0, 0:E], core.quad[1][:, 0:E], cap / P, None, ALU.is_le))
                        nc.vector.tensor_tensor(out, exps[:, :, :], over_tiles(late[:, 0, 0:E], E), ALU.mult).then_inc(comb_ready, 1)
                    else:
                        link(nc.vector.tensor_tensor(exps[:, :, :], exps[:, :, :], one, ALU.mult))
                        link(nc.vector.tensor_reduce(total[:, :], exps[:, :, :], AX.X, ALU.add))
                        link(nc.vector.tensor_scalar(total[:, :], total[:, :], 1e-10, None, ALU.max))
                        link(nc.vector.reciprocal(scale[:, :], total[:, :]))
                        nc.vector.tensor_tensor(out, exps[:, :, :], over_tiles(scale[:, :], E), ALU.mult).then_inc(comb_ready, 1)
                dve.wait_ge(turned, 1)
                nc.vector.tensor_copy(turned_comb[:, :, :], core.quad[0][:, 0:BLOCKS * P].rearrange("p (b t) -> p b t", t=P)
                                      ).then_inc(turned_copied, 1)


def experts(core, name, src, w1, w2, b2, comb_dram, func):
    nc = core.nc
    E, FT = w1.shape[0], w2.shape[2]
    F = FT * P
    free_slots = 2
    b2_landed, w_landed, comb_landed = core.sem(f"{name}_b2_landed"), [core.sem(f"{name}_w_landed{p}") for p in range(2)], [core.sem(f"{name}_comb_landed{p}") for p in range(2)]
    hidden_ready, hidden_read, weighted, summed = (core.sem(f"{name}_{n}") for n in ("hidden_ready", "hidden_read", "weighted", "summed"))
    with ExitStack() as ctx:
        sb = lambda n, shape, dt=F32: core.sb(f"{name}_{n}", shape, dt, ctx)
        w1s = [sb(f"w1s{p}", [P, F + FT]) for p in range(2)]
        w2s = [sb(f"w2s{p}", [P, FT, D]) for p in range(2)]
        cs = [sb(f"cs{p}", [P, N]) for p in range(2)]
        b2s = sb("b2s", [E, D])
        comb = sb("comb_t", [E, N])
        hid = [[sb(f"hid{p}{h}", [P, FT, T]) for h in BOTH] for p in range(2)]
        ring = core.slot[0]
        with nc.Block() as block:
            @block.sync
            def _(sp):
                def load(e, p):
                    sp.dma_start(w1s[p][:, :], w1[e]).then_inc(w_landed[p], 16)
                    sp.dma_start(w2s[p][:, :, :], w2[e]).then_inc(w_landed[p], 16)
                    sp.dma_start(cs[p][:, :], comb_dram[e].partition_broadcast(P)).then_inc(comb_landed[p], 16)
                sp.dma_start(b2s[:, :], b2).then_inc(b2_landed, 16)
                sp.dma_start(comb[:, :], comb_dram[0:E, :]).then_inc(b2_landed, 16)
                load(0, 0)
                load(1, 1)
                with sp.Fori(0, E // 2 - 1) as i:
                    for p in range(2):
                        sp.wait_ge(summed, i * 4 + (2 * p + 2))
                        load(i * 2 + (p + 2), p)

            @block.tensor
            def _(pe):
                pe.wait_ge(b2_landed, 32)
                for h in BOTH:
                    for c in range(0, T, BANK):
                        nc.tensor.matmul(core.slot[1][h][:, c:c + BANK], b2s[:, :], comb[:, h * T + c:h * T + c + BANK],
                                         start=True, stop=False, skip_group_check=True)

                def hidden(i, p, h):
                    if h == 0:
                        pe.wait_ge(w_landed[p], i * 32 + 32)
                    for f in range(FT):
                        u = (2 * p + h) * FT + f
                        pe.wait_ge(hidden_read, i * (4 * FT) + (u - 1 + free_slots))
                        product(nc, ring[u % 2], [(w1s[p][:, f * P:(f + 1) * P], half(src, h))]).then_inc(hidden_ready, 1)

                def add_up(i, p, h):
                    pe.wait_ge(weighted, i * (4 * FT) + ((2 * p + h) * FT + FT))
                    for c in range(0, T, BANK):
                        for f in range(FT):
                            last = nc.tensor.matmul(core.slot[1][h][:, c:c + BANK], w2s[p][:, f, :], hid[p][h][:, f, c:c + BANK],
                                                    start=False, stop=False, skip_group_check=True)
                    last.then_inc(summed, 1)

                def pair(i, first):
                    for p in range(2):
                        for h in BOTH:
                            hidden(i, p, h)
                            if p or h:
                                add_up(i, (2 * p + h - 1) // 2, 1 - h)
                            elif not first:
                                add_up(i - 1, 1, 1)
                pe.sem_inc(hidden_read, free_slots)
                pair(0, True)
                with pe.Fori(1, E // 2) as i:
                    pair(i, False)
                add_up(E // 2 - 1, 1, 1)

            @block.scalar
            def _(act):
                def pair(i):
                    for p in range(2):
                        for h in BOTH:
                            if not isinstance(i, int):
                                act.wait_ge(summed, i * 4 + (2 * p + h + 1 - 4))
                            for f in range(FT):
                                act.wait_ge(hidden_ready, i * (4 * FT) + ((2 * p + h) * FT + f + 1))
                                nc.scalar.activation(hid[p][h][:, f, :], ring[((2 * p + h) * FT + f) % 2], func,
                                                     bias=w1s[p][:, F + f:F + f + 1]).then_inc(hidden_read, 1)
                pair(0)
                with act.Fori(1, E // 2) as i:
                    pair(i)

            @block.vector
            def _(dve):
                with dve.Fori(0, E // 2) as i:
                    for p in range(2):
                        dve.wait_ge(comb_landed[p], i * 16 + 16)
                        for h in BOTH:
                            for f in range(FT):
                                dve.wait_ge(hidden_read, i * (4 * FT) + ((2 * p + h) * FT + f + 1 + free_slots))
                                nc.vector.tensor_tensor(hid[p][h][:, f, :], hid[p][h][:, f, :], half(cs[p], h), ALU.mult).then_inc(weighted, 1)


def layer_0_output(core, cols, x1):
    nc = core.nc
    S = spe, sact, sdve, spool = core.begin("centre var", "square log rstd", "res scaled affine join", "")
    landed = core.sem("ln2_cols")
    with ExitStack() as ctx:
        col = core.sb("colln2", [P, 2], ctx=ctx)
        res = [core.sb(f"res2{h}", [P, T], ctx=ctx) for h in BOTH]
        with nc.Block() as block:
            @block.sync
            def _(sp):
                sp.dma_start(col[:, :], cols).then_inc(landed, 16)

            @block.tensor
            def _(pe):
                pe.wait_ge(core.dve_done[0], sdve.value("res"))
                pe.wait_ge(core.dve_done[1], sdve.value("res"))
                norm_pe(core, pe, BOTH, lambda h: res[h][:, :], (0, 1), S)

            @block.scalar
            def _(act):
                norm_act(core, act, BOTH, 1e-5, (0, 1), S)

            @block.vector
            def _(dve):
                dve.wait_ge(landed, 16)
                for h in BOTH:
                    nc.vector.tensor_tensor(res[h][:, :], core.slot[1][h], half(x1, h), ALU.add).then_inc(core.dve_done[h], 1)
                dve.wait_ge(core.dve_done[0], sdve.value("res"))
                for h in BOTH:
                    norm_dve(core, dve, h, core.cen[h], (0, 1), S)
                    dve.wait_ge(core.dve_done[h], sdve.value("scaled"))
                    nc.vector.tensor_scalar(core.cen[h], core.cen[h], col[:, 0:1], col[:, 1:2], ALU.mult, ALU.add).then_inc(core.dve_done[h], 1)
                    dve.wait_ge(core.dve_done[h], sdve.value("affine"))
                    nc.vector.tensor_tensor(half(core.x, h), half(core.x, h), core.cen[h], ALU.add).then_inc(core.dve_done[h], 1)


GH4, GK, GM = 4, 32, 64
CHUNK = 64
CH = T // CHUNK
HM = GH4 * GM


def slot_attention_masks(core, ctx):
    nc = core.nc
    sb = lambda n, shape: core.sb(n, shape, F32, ctx)
    m = {
        "causal": sb("m_causal", [P, P]),
        "rel": sb("m_rel", [P, P]),
        "after": sb("m_after", [P, P]),
        "first": sb("m_first", [P, P]),
        "ends": sb("m_ends", [P, 2]),
        "heads": sb("m_heads", [P, P]),
    }
    built = core.sem("masks_built")
    with nc.Block() as block:
        @block.gpsimd
        def _(pool):
            link = chained(pool, built)
            for name, v in (("causal", 1.0), ("after", 1.0), ("first", 0.0), ("ends", 1.0), ("heads", 0.0)):
                link(nc.gpsimd.memset(m[name][:, :], v))
            link(nc.gpsimd.affine_select(out=m["causal"][:, :], in_=m["causal"][:, :], compare_op=ALU.is_ge, fill=0.0,
                                         base=0, pattern=[[1, P]], channel_multiplier=-1))
            link(nc.gpsimd.affine_select(out=m["after"][:, :], in_=m["after"][:, :], compare_op=ALU.is_ge, fill=0.0,
                                         base=-1, pattern=[[-1, P]], channel_multiplier=1))
            for c in (0, CHUNK):
                link(nc.gpsimd.memset(m["first"][c:c + 32, c:c + CHUNK], 1.0))
                link(nc.gpsimd.memset(m["ends"][c + 32:c + 64, 1:2], 0.0))
            for h in range(GH4):
                link(nc.gpsimd.memset(m["heads"][32 * h:32 * h + 32, 32 * h:32 * h + 32], 1.0 / GK))
            link(nc.gpsimd.memset(m["causal"][0:CHUNK, CHUNK:P], 0.0))
            link(nc.gpsimd.memset(m["after"][CHUNK:P, 0:CHUNK], 0.0))
            link(nc.gpsimd.tensor_tensor(m["rel"][:, :], m["causal"][:, :], m["first"][:, :], ALU.subtract))
    return m


def slot_attention_half(core, half_no, w_tok, w_qk, m, out):
    nc = core.nc
    GT = KT
    name = f"g{half_no}"
    sem = lambda n: core.sem(f"{name}_{n}")
    w_landed, raw_ready, raw_copied = sem("w_landed"), sem("raw_ready"), sem("raw_copied")
    with ExitStack() as ctx:
        sb = lambda n, shape, dt=F32: core.sb(f"{name}_{n}", shape, dt, ctx)
        wt, wq = sb("wt", [P, 512]), sb("wq", [P, 2 * D])
        raw = sb("raw", [P, GT, 512])
        k_tok, f = raw[:, :, 0:D], raw[:, :, 2 * D:512]
        soft = sb("soft", [P, GT, HM])
        s = sb("s", [P, GT, HM])
        eg = sb("eg", [P, GT, HM])
        se = sb("se", [P, GT, HM])
        send = sb("send", [P, GT, HM])
        qt = sb("qt", [GK, GH4, T])
        kt = sb("kt", [GK, GH4, T])
        dS = sb("dS", [P, 2, 2, GT, 2 * GK])
        ends = sb("ends", [P, 2, 2, GT, 2])
        S = sb("S", [P, 2, CH + 1, 2 * GK])
        Skt = sb("Skt", [GK, CH, HM])
        x = half(core.xn, half_no)

        qk_ready, qk_read = sem("qk_ready"), sem("qk_read")
        abs_done, exp_done, ln_done, f_done, ef_done, s_done, silu_done = (sem(n) for n in ("abs", "exp", "ln", "f", "ef", "s", "silu"))
        D_ready, D_read, eg_done, se_done = sem("D_ready"), sem("D_read"), sem("eg_done"), sem("se_done")
        with nc.Block() as block:
            @block.sync
            def _(sp):
                sp.dma_start(wt[:, :], w_tok).then_inc(w_landed, 16)
                sp.dma_start(wq[:, :], w_qk).then_inc(w_landed, 16)

            @block.tensor
            def _(pe):
                pe.wait_ge(w_landed, 32)
                for i in range(2):
                    for t in range(4):
                        tile = 4 * i + t
                        last = nc.tensor.matmul(core.quad[i][:, t * 512:(t + 1) * 512], x[:, tile * P:(tile + 1) * P], wt[:, :],
                                                start=True, stop=True)
                    last.then_inc(raw_ready, 1)
                for u in range(2 * GH4):
                    slot = core.slot[u // 2 % 2][u % 2]
                    if u < 4:
                        pe.wait_ge(raw_copied, u // 2 + 1)
                    else:
                        pe.wait_ge(qk_read, u - 3)
                    product(nc, slot[0:GK, :], [(wq[:, u * GK:(u + 1) * GK], x)]).then_inc(qk_ready, 1)
                for i in range(2):
                    pe.wait_ge(f_done, 2)
                    pe.wait_ge(qk_read, 2 * GH4)
                    for t in range(4):
                        tile = 4 * i + t
                        nc.tensor.matmul(core.quad[i][:, t * 512:t * 512 + HM], m["rel"][:, :], f[:, tile, :],
                                         start=True, stop=True, skip_group_check=True)
                        last = nc.tensor.matmul(core.quad[i][:, t * 512 + HM:(t + 1) * 512], m["after"][:, :], f[:, tile, :],
                                                start=True, stop=True, skip_group_check=True)
                    last.then_inc(D_ready, 1)

            @block.scalar
            def _(act):
                for i in range(2):
                    act.wait_ge(raw_ready, i + 1)
                    nc.scalar.activation(raw[:, 4 * i:4 * i + 4, :], core.quad[i][:, :].rearrange("p (t x) -> p t x", x=512),
                                         ACT.Identity).then_inc(raw_copied, 1)
                for u in range(2 * GH4):
                    act.wait_ge(qk_ready, u + 1)
                    dst = (qt if u < GH4 else kt)[:, u % GH4, :]
                    nc.scalar.activation(dst, core.slot[u // 2 % 2][u % 2][0:GK, :], ACT.Silu).then_inc(qk_read, 1)
                act.wait_ge(raw_copied, 2)
                nc.scalar.activation(k_tok, k_tok, ACT.Silu).then_inc(silu_done, 1)
                nc.scalar.activation(soft[:, :, :], f, ACT.Abs).then_inc(abs_done, 1)
                act.wait_ge(abs_done, 1)
                nc.scalar.activation(soft[:, :, :], soft[:, :, :], ACT.Exp, scale=-1.0).then_inc(exp_done, 1)
                act.wait_ge(exp_done, 1)
                nc.scalar.activation(soft[:, :, :], soft[:, :, :], ACT.Ln, bias=core.one[:, :]).then_inc(ln_done, 1)
                act.wait_ge(f_done, 2)
                nc.scalar.activation(s[:, :, :], f, ACT.Exp).then_inc(ef_done, 1)
                for i in range(2):
                    act.wait_ge(D_ready, i + 1)
                    D4 = core.quad[i][:, :].rearrange("p (t x) -> p t x", x=512)
                    g = slice(4 * i, 4 * i + 4)
                    nc.scalar.activation(eg[:, g, :], D4[:, :, 0:HM], ACT.Exp).then_inc(eg_done, 1)
                    nc.scalar.activation(se[:, g, :], D4[:, :, 0:HM], ACT.Exp, scale=-1.0).then_inc(eg_done, 1)
                    nc.scalar.activation(send[:, g, :], D4[:, :, HM:512], ACT.Exp).then_inc(eg_done, 1)

            @block.vector
            def _(dve):
                dve.wait_ge(ln_done, 1)
                nc.vector.scalar_tensor_tensor(out=f, in0=f, scalar=0.0, in1=soft[:, :, :], op0=ALU.min, op1=ALU.subtract).then_inc(f_done, 1)
                dve.wait_ge(f_done, 1)
                nc.vector.tensor_scalar(f, f, 0.125, None, ALU.mult).then_inc(f_done, 1)
                dve.wait_ge(ef_done, 1)
                nc.vector.tensor_scalar(s[:, :, :], s[:, :, :], -1.0, 1.0, ALU.mult, ALU.add).then_inc(s_done, 1)
                dve.wait_ge(s_done, 1)
                for i in range(2):
                    dve.wait_ge(eg_done, 3 * i + 3)
                    g = slice(4 * i, 4 * i + 4)
                    nc.vector.tensor_tensor(se[:, g, :], se[:, g, :], s[:, g, :], ALU.mult).then_inc(se_done, 1)
                    nc.vector.tensor_tensor(send[:, g, :], send[:, g, :], s[:, g, :], ALU.mult).then_inc(se_done, 1)

        add_ready, dS_copied, ends_done, S_step, S_scaled, Skt_ready, Skt_copied = (
            sem(n) for n in ("add_ready", "dS_copied", "ends_done", "S_step", "S_scaled", "Skt_ready", "Skt_copied"))
        with nc.Block() as block:
            @block.tensor
            def _(pe):
                kv = raw[:, :, 0:2 * D].rearrange("p t (a h x) -> p t a h x", a=2, h=GH4)
                for par in range(2):
                    rows = slice(CHUNK * par, CHUNK * par + CHUNK)
                    for j in range(2):
                        for t in range(GT):
                            at = j * T + par * 512 + t * 64
                            for h2 in range(2):
                                h = 2 * j + h2
                                last = nc.tensor.matmul(core.quad[0][64 * h2:64 * h2 + 64, at:at + 64],
                                                        send[rows, t, h * GM:(h + 1) * GM], kv[rows, t, :, h, :],
                                                        start=True, stop=True, skip_group_check=True)
                last.then_inc(add_ready, 1)
                for par in range(2):
                    rows = slice(CHUNK * par, CHUNK * par + CHUNK)
                    for j in range(2):
                        for t in range(GT):
                            at = par * 512 + (j * GT + t) * 2
                            last = nc.tensor.matmul(core.quad[1][:, at:at + 2], f[rows, t, j * P:(j + 1) * P], m["ends"][rows, :],
                                                    start=True, stop=True, skip_group_check=True)
                last.then_inc(add_ready, 1)
                pe.wait_ge(S_scaled, 2)
                for i in range(2):
                    if i == 0:
                        pe.wait_ge(dS_copied, 1)
                    else:
                        pe.wait_ge(ends_done, 2)
                    for c in range(8):
                        for j in range(2):
                            last = nc.tensor.transpose(core.quad[i][0:GK, (2 * c + j) * P:(2 * c + j + 1) * P],
                                                       S[:, j, 8 * i + c, 0:GK], core.ident[:, :])
                    last.then_inc(Skt_ready, 1)

            @block.scalar
            def _(act):
                act.wait_ge(add_ready, 1)
                nc.scalar.activation(dS[:, :, :, :, :].rearrange("p j a t x -> p (j a t x)"), core.quad[0][:, :], ACT.Identity).then_inc(dS_copied, 1)
                act.wait_ge(add_ready, 2)
                for par in range(2):
                    nc.scalar.activation(ends[:, par, :, :, :].rearrange("p j t e -> p (j t e)"),
                                         core.quad[1][:, par * 512:par * 512 + 4 * GT], ACT.Exp).then_inc(ends_done, 1)
                for i in range(2):
                    act.wait_ge(Skt_ready, i + 1)
                    nc.scalar.activation(Skt[:, 8 * i:8 * i + 8, :].rearrange("p c x -> p (c x)"), core.quad[i][0:GK, :], ACT.Identity).then_inc(Skt_copied, 1)

            @block.vector
            def _(dve):
                nc.vector.memset(S[:, :, 0, :], 0.0).then_inc(S_step, 2)
                dve.wait_ge(dS_copied, 1)
                dve.wait_ge(ends_done, 2)
                for c in range(CH):
                    dve.wait_ge(S_step, 2 * c + 2)
                    for j in range(2):
                        nc.vector.scalar_tensor_tensor(out=S[:, j, c + 1, :], in0=S[:, j, c, :], scalar=ends[:, c % 2, j, c // 2, 0:1],
                                                       in1=dS[:, j, c % 2, c // 2, :], op0=ALU.mult, op1=ALU.add).then_inc(S_step, 1)
                dve.wait_ge(S_step, 2 * CH + 2)
                for j in range(2):
                    for par in range(2):
                        at = S[:, j, 0:CH, :].rearrange("p (t a) x -> p a t x", a=2)[:, par]
                        last = nc.vector.tensor_tensor(at, at, ends[:, par, j, :, 1:2].to_broadcast([P, GT, 2 * GK]), ALU.mult)
                    last.then_inc(S_scaled, 1)

        ST = spe, sact, sdve, spool = core.begin("A logits turned B out", "soft turned out",
                                                 "A eg max sub sum recip scaled P B", "", GT // 2)
        with ExitStack() as inner:
            sb2 = lambda n, shape: core.sb(f"{name}_{n}", shape, F32, inner)
            Am = [sb2(f"Am{p}", [P, GH4, P]) for p in range(2)]
            lg = [sb2(f"lg{p}", [P, GH4, GM]) for p in range(2)]
            st = [sb2(f"st{p}", [P, 3, GH4]) for p in range(2)]
            turned = [sb2(f"turned{p}", [P, 4, P]) for p in range(2)]
            with nc.Block() as block:
                bank = [[core.quad[p][:, b * 512:(b + 1) * 512] for b in range(4)] for p in range(2)]
                heads = lambda v: v.rearrange("p (h t) -> p h t", h=GH4)

                @block.tensor
                def _(pe):
                    for i in range(GT // 2):
                        for p in range(2):
                            t = 2 * i + p
                            if i:
                                pe.wait_ge(core.act_done[p], sact.value("out", i - 1))
                            for h in range(GH4):
                                last = nc.tensor.matmul(bank[p][0][:, h * P:(h + 1) * P], kt[:, h, t * P:(t + 1) * P],
                                                        qt[:, h, t * P:(t + 1) * P], start=True, stop=True, skip_group_check=True)
                            last.then_inc(core.pe_done[p], 1)
                        for p in range(2):
                            t = 2 * i + p
                            pe.wait_ge(core.dve_done[p], sdve.value("A", i))
                            for h in range(GH4):
                                L = bank[p][1][:, h * GM:(h + 1) * GM]
                                nc.tensor.matmul(L, Am[p][:, h, :], se[:, t, h * GM:(h + 1) * GM], start=True, stop=False, skip_group_check=True)
                                for c in range(2):
                                    last = nc.tensor.matmul(bank[p][1][64 * c:64 * c + 64, h * GM:(h + 1) * GM],
                                                            qt[:, h, t * P + 64 * c:t * P + 64 * c + 64],
                                                            Skt[:, 2 * t + c, h * GM:(h + 1) * GM],
                                                            start=False, stop=True, skip_group_check=True)
                            last.then_inc(core.pe_done[p], 1)
                        for p in range(2):
                            t = 2 * i + p
                            for j in range(2):
                                nc.tensor.transpose(bank[p][2][:, (2 + j) * P:(3 + j) * P], se[:, t, j * P:(j + 1) * P], core.ident[:, :])
                            pe.wait_ge(core.dve_done[p], sdve.value("P", i))
                            for j in range(2):
                                last = nc.tensor.transpose(bank[p][2][:, j * P:(j + 1) * P],
                                                           lg[p][:, 2 * j:2 * j + 2, :].rearrange("p h m -> p (h m)"), core.ident[:, :])
                            last.then_inc(core.pe_done[p], 1)
                        for p in range(2):
                            pe.wait_ge(core.act_done[p], sact.value("turned", i))
                            for h2 in range(2):
                                for j in range(2):
                                    rows = slice(64 * h2, 64 * h2 + 64)
                                    last = nc.tensor.matmul(bank[p][3 * h2][:, j * P:(j + 1) * P], turned[p][rows, 2 + j, :],
                                                            turned[p][rows, j, :], start=True, stop=True, skip_group_check=True)
                            last.then_inc(core.pe_done[p], 1)
                        for p in range(2):
                            t = 2 * i + p
                            pe.wait_ge(core.dve_done[p], sdve.value("B", i))
                            for h in range(GH4):
                                j, h2 = h // 2, h % 2
                                o = bank[p][1][32 * h:32 * h + 32, 256:384]
                                nc.tensor.matmul(o, raw[:, t, D + h * GK:D + (h + 1) * GK], Am[p][:, h, :], start=True, stop=False, skip_group_check=True)
                                for c in range(2):
                                    last = nc.tensor.matmul(o[:, 64 * c:64 * c + 64], S[64 * h2:64 * h2 + 64, j, 2 * t + c, GK:2 * GK],
                                                            turned[p][64 * h2:64 * h2 + 64, j, 64 * c:64 * c + 64],
                                                            start=False, stop=True, skip_group_check=True)
                            last.then_inc(core.pe_done[p], 1)

                @block.scalar
                def _(act):
                    for i in range(GT // 2):
                        for p in range(2):
                            act.wait_ge(core.dve_done[p], sdve.value("sub", i))
                            nc.scalar.activation(lg[p][:, :, :], lg[p][:, :, :], ACT.Exp, scale=float(GK) ** -0.5).then_inc(core.act_done[p], 1)
                        for p in range(2):
                            act.wait_ge(core.pe_done[p], spe.value("turned", i))
                            nc.scalar.activation(turned[p][:, :, :], heads(bank[p][2]), ACT.Identity).then_inc(core.act_done[p], 1)
                        for p in range(2):
                            t = 2 * i + p
                            act.wait_ge(core.pe_done[p], spe.value("out", i))
                            nc.scalar.activation(out[:, t * P:(t + 1) * P], bank[p][1][:, 256:384], ACT.Identity).then_inc(core.act_done[p], 1)

                @block.vector
                def _(dve):
                    over_slots = lambda v: v.rearrange("p (h a) -> p h a", a=1).to_broadcast([P, GH4, GM])
                    causal = m["causal"][:, :].rearrange("p (a t) -> p a t", a=1)
                    for i in range(GT // 2):
                        for p in range(2):
                            dve.wait_ge(core.pe_done[p], spe.value("A", i))
                            nc.vector.tensor_tensor(Am[p][:, :, :], heads(bank[p][0]), causal.to_broadcast([P, GH4, P]), ALU.mult).then_inc(core.dve_done[p], 1)
                        for p in range(2):
                            t = 2 * i + p
                            done = core.dve_done[p]
                            dve.wait_ge(core.pe_done[p], spe.value("logits", i))
                            nc.vector.tensor_tensor(lg[p][:, :, :], bank[p][1][:, 0:HM].rearrange("p (h m) -> p h m", h=GH4),
                                                    eg[:, t, :].rearrange("p (h m) -> p h m", h=GH4), ALU.mult).then_inc(done, 1)
                            dve.wait_ge(done, sdve.value("eg", i))
                            nc.vector.tensor_reduce(st[p][:, 0, :], lg[p][:, :, :], AX.X, ALU.max).then_inc(done, 1)
                            dve.wait_ge(done, sdve.value("max", i))
                            nc.vector.tensor_tensor(lg[p][:, :, :], lg[p][:, :, :], over_slots(st[p][:, 0, :]), ALU.subtract).then_inc(done, 1)
                        for p in range(2):
                            t = 2 * i + p
                            done = core.dve_done[p]
                            dve.wait_ge(core.act_done[p], sact.value("soft", i))
                            nc.vector.tensor_reduce(st[p][:, 1, :], lg[p][:, :, :], AX.X, ALU.add).then_inc(done, 1)
                            dve.wait_ge(done, sdve.value("sum", i))
                            nc.vector.reciprocal(st[p][:, 2, :], st[p][:, 1, :]).then_inc(done, 1)
                            dve.wait_ge(done, sdve.value("recip", i))
                            nc.vector.tensor_tensor(lg[p][:, :, :], lg[p][:, :, :], over_slots(st[p][:, 2, :]), ALU.mult).then_inc(done, 1)
                            dve.wait_ge(done, sdve.value("scaled", i))
                            nc.vector.tensor_tensor(lg[p][:, :, :], lg[p][:, :, :], eg[:, t, :].rearrange("p (h m) -> p h m", h=GH4), ALU.mult).then_inc(done, 1)
                        for p in range(2):
                            dve.wait_ge(core.pe_done[p], spe.value("B", i))
                            for h2 in range(2):
                                last = nc.vector.tensor_tensor(
                                    Am[p][:, :, :].rearrange("p (j b) t -> p b j t", b=2)[:, h2],
                                    bank[p][3 * h2][:, 0:2 * P].rearrange("p (j t) -> p j t", j=2),
                                    causal.to_broadcast([P, 2, P]), ALU.mult)
                            last.then_inc(core.dve_done[p], 1)


def slot_attention(core, a):
    nc = core.nc
    with ExitStack() as ctx:
        m = slot_attention_masks(core, ctx)
        o = [core.sb(f"slot_out{h}", [P, T], ctx=ctx) for h in BOTH]
        wo, gain = core.sb("g_wo", [P, D], ctx=ctx), core.sb("g_gain", [P, 1], ctx=ctx)
        for h in BOTH:
            slot_attention_half(core, h, a["A1_tok"], a["A1_qk"], m, o[h])
        landed = core.sem("g_wo_landed")
        S = spe, sact, sdve, spool = core.begin("mean out", "square log rstd", "scaled join", "")
        with nc.Block() as block:
            @block.sync
            def _(sp):
                sp.dma_start(wo[:, :], a["A1_wo"]).then_inc(landed, 16)
                for h in range(GH4):
                    sp.dma_start(gain[32 * h:32 * h + 32, :], a["A1_gain"]).then_inc(landed, 16)

            @block.tensor
            def _(pe):
                for h in BOTH:
                    pe.wait_ge(core.act_done[h], sact.value("square"))
                    product(nc, core.slot[h][0], [(m["heads"][:, :], core.sq[h])]).then_inc(core.pe_done[h], 1)
                pe.wait_ge(landed, 16 * (1 + GH4))
                for h in BOTH:
                    pe.wait_ge(core.dve_done[h], sdve.value("scaled"))
                    product(nc, core.slot[h][1], [(wo[:, :], core.cen[h])]).then_inc(core.pe_done[h], 1)

            @block.scalar
            def _(act):
                for h in BOTH:
                    nc.scalar.activation(core.sq[h], o[h][:, :], ACT.Square).then_inc(core.act_done[h], 1)
                for h in BOTH:
                    act.wait_ge(core.pe_done[h], spe.value("mean"))
                    nc.scalar.activation(core.sq[h], core.slot[h][0], ACT.Ln, bias=core.eps[1e-5][:, :]).then_inc(core.act_done[h], 1)
                    act.wait_ge(core.act_done[h], sact.value("log"))
                    nc.scalar.activation(core.sq[h], core.sq[h], ACT.Exp, scale=-0.5).then_inc(core.act_done[h], 1)

            @block.vector
            def _(dve):
                dve.wait_ge(landed, 16 * (1 + GH4))
                for h in BOTH:
                    dve.wait_ge(core.act_done[h], sact.value("rstd"))
                    nc.vector.scalar_tensor_tensor(out=core.cen[h], in0=o[h][:, :], scalar=gain[:, :], in1=core.sq[h],
                                                   op0=ALU.mult, op1=ALU.mult).then_inc(core.dve_done[h], 1)
                for h in BOTH:
                    dve.wait_ge(core.pe_done[h], spe.value("out"))
                    nc.vector.tensor_tensor(half(core.x, h), half(core.x, h), core.slot[h][1], ALU.add).then_inc(core.dve_done[h], 1)


NS, CONV = 16, 4
DD = 2
XR = 2 * NS + 1


def state_space(core, a, scratch):
    nc = core.nc
    sem = lambda n: core.sem(f"ss_{n}")
    xd_dram = scratch("xd_dram", (HALVES, XR, T))
    with ExitStack() as ctx:
        sb = lambda n, shape, ctx=ctx: core.sb(f"ss_{n}", shape, F32, ctx)
        w_in, w_x, w_dt, w_out = sb("w_in", [P, 4 * P]), sb("w_x", [P, DD, XR]), sb("w_dt", [1, DD * P]), sb("w_out", [P, DD, D])
        cols = sb("cols", [P, DD, CONV + 3])
        TAP, CB, BDT, DP = 0, CONV, CONV + 1, CONV + 2
        neg_a = sb("neg_a", [P, DD, NS])
        diag = sb("diag", [P, DD, P])
        pick = sb("pick", [XR, NS, P])
        xdbl = [sb(f"xdbl{h}", [XR, T]) for h in BOTH]
        both = lambda n: [[sb(f"{n}{h}{d}", [P, T]) for d in range(DD)] for h in BOTH]
        xc, zs, dt, u = both("xc"), both("zs"), both("dt"), both("u")
        w_landed, built, xz_ready, xz_read, conv_done, silu_done, a_done, a_neg, diag_done = (sem(n) for n in (
            "w_landed", "built", "xz_ready", "xz_read", "conv_done", "silu_done", "a_done", "a_neg", "diag_done"))
        xd_ready, xd_copied, xd_stored, dt_ready, dt_lin, dt_abs, dt_exp, dt_ln, dt_done, u_done = (sem(n) for n in (
            "xd_ready", "xd_copied", "xd_stored", "dt_ready", "dt_lin", "dt_abs", "dt_exp", "dt_ln", "dt_done", "u_done"))
        every = [(h, d) for h in BOTH for d in range(DD)]
        with ExitStack() as inner:
            xpad = [[sb(f"xpad{h}{d}", [P, T + CONV - 1], inner) for d in range(DD)] for h in BOTH]
            with nc.Block() as block:
                @block.sync
                def _(sp):
                    for t, n in ((w_in[:, :], "A2_in"), (w_x[:, :, :], "A2_x"), (w_dt[:, :], "A2_dt"), (w_out[:, :, :], "A2_out"),
                                 (cols[:, :, :], "A2_cols"), (neg_a[:, :, :], "A2_A")):
                        sp.dma_start(t, a[n]).then_inc(w_landed, 16)
                    for h in BOTH:
                        sp.wait_ge(xd_copied, h + 1)
                        sp.dma_start(xd_dram[h], xdbl[h][:, :]).then_inc(xd_stored, 16)
                    sp.wait_ge(xd_stored, 32)

                @block.gpsimd
                def _(pool):
                    link = chained(pool, built)
                    for h, d in every:
                        link(nc.gpsimd.memset(xpad[h][d][:, 0:CONV - 1], 0.0))
                    link(nc.gpsimd.memset(pick[:, :, :], 0.0))
                    link(nc.gpsimd.affine_select(out=pick[:, :, :], in_=pick[:, :, :], compare_op=ALU.not_equal, fill=1.0,
                                                 base=-(1 + NS), pattern=[[-1, NS], [0, P]], channel_multiplier=1))

                @block.tensor
                def _(pe):
                    pe.wait_ge(w_landed, 96)
                    n = 0
                    for i in range(4):
                        for h in BOTH:
                            if n >= 4:
                                pe.wait_ge(xz_read, n - 3)
                            product(nc, core.slot[n // 2 % 2][n % 2], [(w_in[:, i * P:(i + 1) * P], half(core.xn, h))]).then_inc(xz_ready, 1)
                            n += 1
                    for h in BOTH:
                        pe.wait_ge(xz_read, 7 + h)
                        pe.wait_ge(silu_done, 2 * h + 2)
                        product(nc, core.slot[1][h][0:XR, :], [(w_x[:, d, :], xc[h][d][:, :]) for d in range(DD)]).then_inc(xd_ready, 1)
                    pe.wait_ge(xz_read, 8)
                    for n, (h, d) in enumerate(every):
                        pe.wait_ge(xd_copied, h + 1)
                        if n >= 2:
                            pe.wait_ge(dt_lin, n - 1)
                        product(nc, core.slot[0][n % 2], [(w_dt[:, d * P:(d + 1) * P], xdbl[h][0:1, :])]).then_inc(dt_ready, 1)

                @block.scalar
                def _(act):
                    act.wait_ge(w_landed, 96)
                    n = 0
                    for i in range(4):
                        for h in BOTH:
                            act.wait_ge(xz_ready, n + 1)
                            slot = core.slot[n // 2 % 2][n % 2]
                            if i < DD:
                                nc.scalar.activation(xpad[h][i][:, CONV - 1:], slot, ACT.Identity).then_inc(xz_read, 1)
                            else:
                                nc.scalar.activation(zs[h][i - DD][:, :], slot, ACT.Silu).then_inc(xz_read, 1)
                            n += 1
                    for n, (h, d) in enumerate(every):
                        act.wait_ge(conv_done, CONV * n + CONV)
                        nc.scalar.activation(xc[h][d][:, :], xc[h][d][:, :], ACT.Silu).then_inc(silu_done, 1)
                    for h in BOTH:
                        act.wait_ge(xd_ready, h + 1)
                        nc.scalar.activation(xdbl[h][:, :], core.slot[1][h][0:XR, :], ACT.Identity).then_inc(xd_copied, 1)
                    nc.scalar.activation(neg_a[:, :, :], neg_a[:, :, :], ACT.Exp).then_inc(a_done, 1)
                    for n, (h, d) in enumerate(every):
                        act.wait_ge(dt_ready, n + 1)
                        nc.scalar.activation(dt[h][d][:, :], core.slot[0][n % 2], ACT.Identity, bias=cols[:, d, BDT:BDT + 1]).then_inc(dt_lin, 1)
                    for n, (h, d) in enumerate(every):
                        act.wait_ge(dt_lin, n + 1)
                        nc.scalar.activation(u[h][d][:, :], dt[h][d][:, :], ACT.Abs).then_inc(dt_abs, 1)
                    for n, (h, d) in enumerate(every):
                        act.wait_ge(dt_abs, n + 1)
                        nc.scalar.activation(u[h][d][:, :], u[h][d][:, :], ACT.Exp, scale=-1.0).then_inc(dt_exp, 1)
                    for n, (h, d) in enumerate(every):
                        act.wait_ge(dt_exp, n + 1)
                        nc.scalar.activation(u[h][d][:, :], u[h][d][:, :], ACT.Ln, bias=core.one[:, :]).then_inc(dt_ln, 1)

                @block.vector
                def _(dve):
                    dve.wait_ge(w_landed, 96)
                    dve.wait_ge(built, 4)
                    for d in range(DD):
                        nc.vector.tensor_scalar(diag[:, d, :], core.ident[:, :], cols[:, d, DP:DP + 1], None, ALU.mult).then_inc(diag_done, 1)
                    for n, (h, d) in enumerate(every):
                        x = xpad[h][d]
                        dve.wait_ge(xz_read, 2 * d + h + 1)
                        nc.vector.tensor_scalar(xc[h][d][:, :], x[:, 0:T], cols[:, d, 0:1], cols[:, d, CB:CB + 1],
                                                ALU.mult, ALU.add).then_inc(conv_done, 1)
                        for k in range(1, CONV):
                            dve.wait_ge(conv_done, CONV * n + k)
                            nc.vector.scalar_tensor_tensor(out=xc[h][d][:, :], in0=x[:, k:k + T], scalar=cols[:, d, k:k + 1],
                                                           in1=xc[h][d][:, :], op0=ALU.mult, op1=ALU.add).then_inc(conv_done, 1)
                    dve.wait_ge(a_done, 1)
                    nc.vector.tensor_scalar(neg_a[:, :, :], neg_a[:, :, :], -1.0, None, ALU.mult).then_inc(a_neg, 1)
                    for n, (h, d) in enumerate(every):
                        dve.wait_ge(dt_ln, n + 1)
                        nc.vector.scalar_tensor_tensor(out=dt[h][d][:, :], in0=dt[h][d][:, :], scalar=0.0, in1=u[h][d][:, :],
                                                       op0=ALU.max, op1=ALU.add).then_inc(dt_done, 1)
                        dve.wait_ge(dt_done, n + 1)
                        dve.wait_ge(silu_done, n + 1)
                        nc.vector.tensor_tensor(u[h][d][:, :], dt[h][d][:, :], xc[h][d][:, :], ALU.mult).then_inc(u_done, 1)

        RING = 4
        b_landed = [sem(f"b_landed{i}") for i in range(2)]
        da_ready, dbx_ready, scanned, c_ready, hc_ready, summed, y_gated, o_ready, joined = (sem(n) for n in (
            "da_ready", "dbx_ready", "scanned", "c_ready", "hc_ready", "summed", "y_gated", "o_ready", "joined"))
        turns = [(h, s, d) for h in BOTH for s in range(NS) for d in range(DD)]
        with ExitStack() as inner:
            bs = [sb(f"bs{i}", [P, T], inner) for i in range(2)]
            da = [sb(f"da{i}", [P, T], inner) for i in range(RING)]
            st = [sb(f"st{i}", [P, T], inner) for i in range(RING)]
            with nc.Block() as block:
                @block.sync
                def _(sp):
                    for n in range(HALVES * NS):
                        h, s = n // NS, n % NS
                        if n >= 2:
                            sp.wait_ge(dbx_ready, DD * (n - 1))
                        sp.dma_start(bs[n % 2][:, :], xd_dram[h, 1 + s].partition_broadcast(P)).then_inc(b_landed[n % 2], 16)

                @block.scalar
                def _(act):
                    for n, (h, s, d) in enumerate(turns):
                        if n >= RING:
                            act.wait_ge(scanned, n - RING + 1)
                        nc.scalar.activation(da[n % RING][:, :], dt[h][d][:, :], ACT.Exp, scale=neg_a[:, d, s:s + 1]).then_inc(da_ready, 1)

                @block.gpsimd
                def _(pool):
                    for n, (h, s, d) in enumerate(turns):
                        pool.wait_ge(b_landed[n // DD % 2], 16 * (n // DD // 2 + 1))
                        if n >= RING:
                            pool.wait_ge(summed, n - RING + 1)
                        nc.gpsimd.tensor_tensor(st[n % RING][:, :], u[h][d][:, :], bs[n // DD % 2][:, :], ALU.mult).then_inc(dbx_ready, 1)

                @block.vector
                def _(dve):
                    def times_c(n):
                        h, s, d = turns[n]
                        dve.wait_ge(c_ready, n // DD + 1)
                        dve.wait_ge(scanned, n + 1)
                        nc.vector.tensor_tensor(st[n % RING][:, :], st[n % RING][:, :], core.slot[0][s % 2], ALU.mult).then_inc(hc_ready, 1)

                    def gate(h):
                        dve.wait_ge(summed, DD * NS * (h + 1))
                        for d in range(DD):
                            nc.vector.tensor_tensor(zs[h][d][:, :], zs[h][d][:, :], core.slot[1][d], ALU.mult).then_inc(y_gated, 1)

                    for n, (h, s, d) in enumerate(turns):
                        dve.wait_ge(da_ready, n + 1)
                        dve.wait_ge(dbx_ready, n + 1)
                        i = n % RING
                        nc.vector.tensor_tensor_scan(out=st[i][:, :], data0=da[i][:, :], data1=st[i][:, :], initial=0.0,
                                                     op0=ALU.mult, op1=ALU.add).then_inc(scanned, 1)
                        if n and n % (DD * NS):
                            times_c(n - 1)
                        if n % (DD * NS) == DD * NS - 1:
                            times_c(n)
                            gate(h)
                    for h in BOTH:
                        dve.wait_ge(o_ready, h + 1)
                        nc.vector.tensor_tensor(half(core.x, h), half(core.x, h), core.slot[0][h], ALU.add).then_inc(joined, 1)

                def add_state(pe, n):
                    h, s, d = turns[n]
                    pe.wait_ge(hc_ready, n + 1)
                    for c in range(0, T, BANK):
                        last = nc.tensor.matmul(core.slot[1][d][:, c:c + BANK], core.ident[:, :], st[n % RING][:, c:c + BANK],
                                                start=False, stop=(s == NS - 1), skip_group_check=True)
                    last.then_inc(summed, 1)

                @block.tensor
                def _(pe):
                    for n, (h, s, d) in enumerate(turns):
                        if s == 0 and d == 0:
                            if h:
                                pe.wait_ge(y_gated, DD)
                            for e in range(DD):
                                for c in range(0, T, BANK):
                                    nc.tensor.matmul(core.slot[1][e][:, c:c + BANK], diag[:, e, :], xc[h][e][:, c:c + BANK],
                                                     start=True, stop=False, skip_group_check=True)
                        if d == 0:
                            if n >= 2 * DD:
                                pe.wait_ge(hc_ready, n - DD)
                            product(nc, core.slot[0][s % 2], [(pick[:, s, :], xdbl[h][:, :])]).then_inc(c_ready, 1)
                        if n and n % (DD * NS):
                            add_state(pe, n - 1)
                        if n % (DD * NS) == DD * NS - 1:
                            add_state(pe, n)
                    for h in BOTH:
                        pe.wait_ge(y_gated, DD * (h + 1))
                        pe.wait_ge(hc_ready, len(turns))
                        product(nc, core.slot[0][h], [(w_out[:, d, :], zs[h][d][:, :]) for d in range(DD)]).then_inc(o_ready, 1)


def causal_attention(core, w_qkvo, cols):
    nc = core.nc
    QT = T // P
    scale = float(D) ** -0.5
    S = spe, sact, sdve, spool = core.begin("q k v | scores turned mixed | out", "q k v | exp turned mixed |",
                                            "| max neg recip norm | join", "", QT)
    landed, built = core.sem("ca_landed"), core.sem("ca_built")
    with ExitStack() as ctx:
        sb = lambda n, shape: core.sb(f"ca_{n}", shape, F32, ctx)
        w, col = sb("w", [P, 4 * D]), sb("col", [P, 4])
        hide = sb("hide", [P, P])
        q, k, p, pt, mixed = ([sb(f"{n}{h}", [P, T]) for h in BOTH] for n in ("q", "k", "p", "pt", "mixed"))
        v = [sb(f"v{h}", [P, QT, D]) for h in BOTH]
        st = [sb(f"st{h}", [P, 4]) for h in BOTH]
        proj = {"q": 0, "k": 1}
        with nc.Block() as block:
            @block.sync
            def _(sp):
                sp.dma_start(w[:, :], w_qkvo).then_inc(landed, 16)
                sp.dma_start(col[:, :], cols).then_inc(landed, 16)

            @block.gpsimd
            def _(pool):
                link = chained(pool, built)
                link(nc.gpsimd.memset(hide[:, :], 0.0))
                link(nc.gpsimd.affine_select(out=hide[:, :], in_=hide[:, :], compare_op=ALU.is_ge, fill=-1e30,
                                             base=0, pattern=[[-1, P]], channel_multiplier=1))

            @block.tensor
            def _(pe):
                pe.wait_ge(landed, 32)
                for h in BOTH:
                    x = half(core.xn, h)
                    product(nc, core.slot[h][0], [(w[:, 0:D], x)]).then_inc(core.pe_done[h], 1)
                    product(nc, core.slot[h][1], [(w[:, D:2 * D], x)]).then_inc(core.pe_done[h], 1)
                for h in BOTH:
                    pe.wait_ge(core.act_done[h], sact.value("q"))
                    for t in range(QT):
                        last = nc.tensor.matmul(core.slot[h][0][:, t * D:(t + 1) * D], half(core.xn, h)[:, t * P:(t + 1) * P],
                                                w[:, 2 * D:3 * D], start=True, stop=True, skip_group_check=True)
                    last.then_inc(core.pe_done[h], 1)
                pe.wait_ge(built, 2)
                for t in range(QT):
                    tile = slice(t * P, (t + 1) * P)
                    for h in BOTH:
                        pe.wait_ge(core.act_done[h], sact.value("mixed", t - 1) if t else sact.value("v"))
                        for c in range(0, (t + 1) * P, BANK):
                            end = min(c + BANK, (t + 1) * P)
                            own = end == (t + 1) * P
                            last = nc.tensor.matmul(core.slot[h][0][:, c:end], q[h][:, tile], k[h][:, c:end],
                                                    start=True, stop=not own, skip_group_check=True)
                        last = nc.tensor.matmul(core.slot[h][0][:, tile], core.ident[:, :], hide[:, :],
                                                start=False, stop=True, skip_group_check=True)
                        last.then_inc(core.pe_done[h], 1)
                    for h in BOTH:
                        pe.wait_ge(core.dve_done[h], sdve.value("norm", t))
                        for j in range(t + 1):
                            last = nc.tensor.transpose(core.slot[h][1][:, j * P:(j + 1) * P], p[h][:, j * P:(j + 1) * P], core.ident[:, :])
                        last.then_inc(core.pe_done[h], 1)
                    for h in BOTH:
                        pe.wait_ge(core.act_done[h], sact.value("turned", t))
                        for j in range(t + 1):
                            last = nc.tensor.matmul(core.slot[h][0][:, 0:P], v[h][:, j, :], pt[h][:, j * P:(j + 1) * P],
                                                    start=(j == 0), stop=(j == t), skip_group_check=True)
                        last.then_inc(core.pe_done[h], 1)
                for h in BOTH:
                    pe.wait_ge(core.act_done[h], sact.value("mixed", QT - 1))
                    product(nc, core.slot[h][1], [(w[:, 3 * D:4 * D], mixed[h][:, :])]).then_inc(core.pe_done[h], 1)

            @block.scalar
            def _(act):
                act.wait_ge(landed, 32)
                for h in BOTH:
                    for n, dst in (("q", q[h]), ("k", k[h])):
                        i = proj[n]
                        act.wait_ge(core.pe_done[h], spe.value(n))
                        nc.scalar.activation(dst[:, :], core.slot[h][i], ACT.Identity, bias=col[:, i:i + 1]).then_inc(core.act_done[h], 1)
                for h in BOTH:
                    act.wait_ge(core.pe_done[h], spe.value("v"))
                    nc.scalar.activation(v[h][:, :, :].rearrange("p t d -> p (t d)"), core.slot[h][0], ACT.Identity).then_inc(core.act_done[h], 1)
                for t in range(QT):
                    keys = slice(0, (t + 1) * P)
                    for h in BOTH:
                        act.wait_ge(core.dve_done[h], sdve.value("neg", t))
                        nc.scalar.activation(p[h][:, keys], core.slot[h][0][:, keys], ACT.Exp, bias=st[h][:, 1:2], scale=scale,
                                             accum_out=st[h][:, 2:3]).then_inc(core.act_done[h], 1)
                    for h in BOTH:
                        act.wait_ge(core.pe_done[h], spe.value("turned", t))
                        nc.scalar.activation(pt[h][:, keys], core.slot[h][1][:, keys], ACT.Identity).then_inc(core.act_done[h], 1)
                    for h in BOTH:
                        act.wait_ge(core.pe_done[h], spe.value("mixed", t))
                        nc.scalar.activation(mixed[h][:, t * P:(t + 1) * P], core.slot[h][0][:, 0:P], ACT.Identity,
                                             bias=col[:, 2:3]).then_inc(core.act_done[h], 1)

            @block.vector
            def _(dve):
                for t in range(QT):
                    keys = slice(0, (t + 1) * P)
                    for h in BOTH:
                        done = core.dve_done[h]
                        dve.wait_ge(core.pe_done[h], spe.value("scores", t))
                        nc.vector.tensor_reduce(st[h][:, 0:1], core.slot[h][0][:, keys], AX.X, ALU.max).then_inc(done, 1)
                        dve.wait_ge(done, sdve.value("max", t))
                        nc.vector.tensor_scalar(st[h][:, 1:2], st[h][:, 0:1], -scale, None, ALU.mult).then_inc(done, 1)
                    for h in BOTH:
                        done = core.dve_done[h]
                        dve.wait_ge(core.act_done[h], sact.value("exp", t))
                        nc.vector.reciprocal(st[h][:, 3:4], st[h][:, 2:3]).then_inc(done, 1)
                        dve.wait_ge(done, sdve.value("recip", t))
                        nc.vector.tensor_scalar(p[h][:, keys], p[h][:, keys], st[h][:, 3:4], None, ALU.mult).then_inc(done, 1)
                dve.wait_ge(landed, 32)
                for h in BOTH:
                    dve.wait_ge(core.pe_done[h], spe.value("out"))
                    nc.vector.scalar_tensor_tensor(out=half(core.x, h), in0=core.slot[h][1], scalar=col[:, 3:4], in1=half(core.x, h),
                                                   op0=ALU.add, op1=ALU.add).then_inc(core.dve_done[h], 1)


FB = 16
FI = 352
FT = T // P
FCH = [(c, min(P, FI - c)) for c in range(0, FI, P)]


FP4_STEPS = 14


def fp4_round(core, name, jobs):
    nc = core.nc
    abs_done, sign_done, rounded = (core.sem(f"{name}_{n}") for n in ("abs", "sign", "rounded"))
    blocks = lambda v: v.rearrange("p (b e) -> p b e", e=FB)
    with nc.Block() as block:
        @block.scalar
        def _(act):
            for j, (v, (r, u, w, sign), stat) in enumerate(jobs):
                if j >= 2:
                    act.wait_ge(rounded, FP4_STEPS * (j - 1))
                nc.scalar.activation(r, v, ACT.Abs).then_inc(abs_done, 1)
                nc.scalar.activation(sign, v, ACT.Sign).then_inc(sign_done, 1)

        @block.vector
        def _(dve):
            link = chained(dve, rounded)
            for j, (v, (r, u, w, sign), stat) in enumerate(jobs):
                scale, inv = stat[:, 0, :], stat[:, 1, :]
                spread = lambda s: s.rearrange("p (b e) -> p b e", e=1).to_broadcast([P, s.shape[-1], FB])
                dve.wait_ge(abs_done, j + 1)
                link(nc.vector.tensor_reduce(scale, blocks(r), AX.X, ALU.max))
                link(nc.vector.tensor_scalar(scale, scale, 1.0 / 6.0, 1e-12, ALU.mult, ALU.max))
                link(nc.vector.reciprocal(inv, scale))
                link(nc.vector.tensor_tensor(blocks(r), blocks(r), spread(inv), ALU.mult))
                link(nc.vector.tensor_scalar(u, r, 0.25, None, ALU.is_gt))
                for mid in (0.75, 1.25, 1.75):
                    link(nc.vector.scalar_tensor_tensor(out=u, in0=r, scalar=mid, in1=u, op0=ALU.is_gt, op1=ALU.add))
                link(nc.vector.tensor_scalar(w, r, 5.0, 2.0, ALU.is_gt, ALU.mult))
                for mid in (2.5, 3.5):
                    link(nc.vector.scalar_tensor_tensor(out=w, in0=r, scalar=mid, in1=w, op0=ALU.is_gt, op1=ALU.add))
                link(nc.vector.scalar_tensor_tensor(out=u, in0=u, scalar=0.5, in1=w, op0=ALU.mult, op1=ALU.add))
                dve.wait_ge(sign_done, j + 1)
                link(nc.vector.tensor_tensor(u, u, sign, ALU.mult))
                link(nc.vector.tensor_tensor(blocks(v), blocks(u), spread(scale), ALU.mult))


def fp4_net(core, w_gate, w_up, w_down):
    nc = core.nc
    name = "fp"
    sem = lambda n: core.sem(f"fp_{n}")
    WN = 2 * len(FCH) * P + FI
    HN = FT * FI // 2
    with ExitStack() as ctx:
        sb = lambda n, shape, ctx=ctx: core.sb(f"fp_{n}", shape, F32, ctx)
        hidden = [sb(f"hidden{h}", [P, FT, FI]) for h in BOTH]
        bufs = [sb(f"buf{i}", [P, 2 * HN]) for i in range(6)]
        stats = [sb(f"stats{i}", [P, 2, HN // FB]) for i in range(2)]
        gu_t = [sb(f"w{n}_t", [P, FI]) for n in ("gate", "up")]
        down_t = sb("wdown_t", [P, len(FCH), D])
        def job(j, values):
            n = values.shape[-1]
            return values, [b[:, j % 2 * HN:j % 2 * HN + n] for b in bufs[2:6]], stats[j % 2][:, :, 0:n // FB]

        landed, zeroed, turned, copied = sem("landed"), sem("zeroed"), sem("turned"), sem("copied")
        with ExitStack() as inner:
            raw = sb("raw", [P, WN], inner)
            x_tok = [bufs[h][:, 0:T] for h in BOTH]
            with nc.Block() as block:
                @block.gpsimd
                def _(pool):
                    for i in range(2):
                        at = (i * len(FCH) + 2) * P
                        nc.gpsimd.memset(raw[FCH[2][1]:, at:at + P], 0.0).then_inc(zeroed, 1)
                    pool.wait_ge(zeroed, 2)

                @block.sync
                def _(sp):
                    for i, w in enumerate((w_gate, w_up)):
                        for n, (c, size) in enumerate(FCH):
                            at = (i * len(FCH) + n) * P
                            sp.dma_start(raw[0:size, at:at + P], w[c:c + size, :]).then_inc(landed, 16)
                    sp.dma_start(raw[:, 2 * len(FCH) * P:], w_down).then_inc(landed, 16)
                    sp.wait_ge(landed, 16 * (2 * len(FCH) + 1))

                @block.tensor
                def _(pe):
                    for h in BOTH:
                        for t in range(FT):
                            last = nc.tensor.transpose(core.slot[h][0][:, t * P:(t + 1) * P], half(core.xn, h)[:, t * P:(t + 1) * P], core.ident[:, :])
                        last.then_inc(turned, 1)

                @block.scalar
                def _(act):
                    for h in BOTH:
                        act.wait_ge(turned, h + 1)
                        nc.scalar.activation(x_tok[h], core.slot[h][0], ACT.Identity).then_inc(copied, 1)

            fp4_round(core, "fp_in", [job(0, raw[:, :])] + [job(1 + h, x_tok[h]) for h in BOTH])

            w_turned, w_copied, gu_ready, silu_done, h_done = (sem(n) for n in ("w_turned", "w_copied", "gu_ready", "silu", "h_done"))
            xq = bufs[2]
            gate = [bufs[3 + i][:, 0:2 * FI].rearrange("p (t e) -> p t e", t=2) for i in range(2)]
            with nc.Block() as block:
                @block.tensor
                def _(pe):
                    for i in range(2):
                        for n, (c, size) in enumerate(FCH):
                            at = (i * len(FCH) + n) * P
                            last = nc.tensor.transpose(core.slot[0][0][:, i * BANK + c:i * BANK + c + size], raw[0:size, at:at + P], core.ident[0:size, 0:size])
                    last.then_inc(w_turned, 1)
                    for n, (c, size) in enumerate(FCH):
                        at = 2 * len(FCH) * P + c
                        last = nc.tensor.transpose(core.slot[0][1][0:size, n * P:(n + 1) * P], raw[:, at:at + size], core.ident[:, :])
                    last.then_inc(w_turned, 1)
                    for h in BOTH:
                        for t in range(FT):
                            last = nc.tensor.transpose(core.slot[1][h][:, t * P:(t + 1) * P], x_tok[h][:, t * P:(t + 1) * P], core.ident[:, :])
                        last.then_inc(w_turned, 1)
                    pe.wait_ge(w_copied, 5 + len(FCH) - 1)
                    for u in range(HALVES * FT // 2):
                        if u >= 2:
                            pe.wait_ge(h_done, u - 1)
                        for t in range(2):
                            at = (2 * u + t) * P
                            for i in range(2):
                                last = nc.tensor.matmul(core.slot[u % 2][i][:, t * BANK:t * BANK + FI], xq[:, at:at + P], gu_t[i][:, :], start=True, stop=True)
                        last.then_inc(gu_ready, 1)

                @block.scalar
                def _(act):
                    act.wait_ge(w_turned, 1)
                    for i in range(2):
                        nc.scalar.activation(gu_t[i][:, :], core.slot[0][0][:, i * BANK:i * BANK + FI], ACT.Identity).then_inc(w_copied, 1)
                    act.wait_ge(w_turned, 2)
                    for n, (c, size) in enumerate(FCH):
                        nc.scalar.activation(down_t[0:size, n, :], core.slot[0][1][0:size, n * P:(n + 1) * P], ACT.Identity).then_inc(w_copied, 1)
                    for h in BOTH:
                        act.wait_ge(w_turned, 3 + h)
                        nc.scalar.activation(half(xq, h), core.slot[1][h], ACT.Identity).then_inc(w_copied, 1)
                    for u in range(HALVES * FT // 2):
                        act.wait_ge(gu_ready, u + 1)
                        if u >= 2:
                            act.wait_ge(h_done, u - 1)
                        nc.scalar.activation(gate[u % 2], core.slot[u % 2][0].rearrange("p (t e) -> p t e", t=2)[:, :, 0:FI], ACT.Silu).then_inc(silu_done, 1)

                @block.vector
                def _(dve):
                    for u in range(HALVES * FT // 2):
                        h, t = divmod(2 * u, FT)
                        dve.wait_ge(silu_done, u + 1)
                        nc.vector.tensor_tensor(hidden[h][:, t:t + 2, :], gate[u % 2], core.slot[u % 2][1].rearrange("p (t e) -> p t e", t=2)[:, :, 0:FI],
                                                ALU.mult).then_inc(h_done, 1)

        fp4_round(core, "fp_hid", [job(j, hidden[j // 2][:, j % 2 * FT // 2:(j % 2 + 1) * FT // 2, :].rearrange("p t e -> p (t e)"))
                                 for j in range(4)])
        h_turned, h_copied, o_ready, joined = (sem(n) for n in ("h_turned", "h_copied", "o_ready", "joined"))
        units = [(h, n) for h in BOTH for n in range(len(FCH))]
        with nc.Block() as block:
            hid = lambda h, n: bufs[h * len(FCH) + n][:, 0:T]
            @block.tensor
            def _(pe):
                for i, (h, n) in enumerate(units):
                    c, size = FCH[n]
                    if i >= 2:
                        pe.wait_ge(h_copied, i - 1)
                    for t in range(FT):
                        last = nc.tensor.transpose(core.slot[0][i % 2][0:size, t * P:(t + 1) * P], hidden[h][:, t, c:c + size], core.ident[:, :])
                    last.then_inc(h_turned, 1)
                for h in BOTH:
                    pe.wait_ge(h_copied, len(FCH) * (h + 1))
                    product(nc, core.slot[1][h], [(down_t[0:size, n, :], hid(h, n)[0:size, :]) for n, (c, size) in enumerate(FCH)]).then_inc(o_ready, 1)

            @block.scalar
            def _(act):
                for i, (h, n) in enumerate(units):
                    size = FCH[n][1]
                    act.wait_ge(h_turned, i + 1)
                    nc.scalar.activation(hid(h, n)[0:size, :], core.slot[0][i % 2][0:size, :], ACT.Identity).then_inc(h_copied, 1)

            @block.vector
            def _(dve):
                for h in BOTH:
                    dve.wait_ge(o_ready, h + 1)
                    nc.vector.tensor_tensor(half(core.x, h), half(core.x, h), core.slot[1][h], ALU.add).then_inc(joined, 1)


def linear_branch_of_layer_0(core, a, scratch):
    with core.own_semaphores():
        linear_blocks(core, a["L0_att"], a["L0_f1"], a["L0_f2"], a["L0_cols"])


def routed_branch_of_layer_0(core, a, scratch):
    q_dram = scratch("q_dram", (HALVES, GROUPS, GH, ROWS, T), BF16)
    k_dram = scratch("k_dram", (HALVES, GROUPS, GH, ROWS, T), BF16)
    v_dram = scratch("v_dram", (HALVES, GROUPS, P, KT, GH * HD))
    with ExitStack() as ctx:
        x1 = core.sb("x1", [P, N], ctx=ctx)
        attention_inputs(core, a["F0_qk"], a["F0_v"], a["F0_qk_cols"], a["F0_v_bias"], q_dram, k_dram, v_dram)
        with ExitStack() as inner:
            mixed = [core.sb(f"mixed{h}", [P, GROUPS, T], ctx=inner) for h in BOTH]
            attention(core, q_dram, k_dram, v_dram, mixed)
            attention_output(core, a["F0_out"], a["F0_out_cols"], mixed, x1)
        comb = scratch("comb0", (8, N))
        route(core, "r0", x1, a["F0_router"], a["F0_router_b"], "groups", 8, comb)
        experts(core, "e0", x1, a["F0_w1"], a["F0_w2"], a["F0_b2"], comb, ACT.Relu)
        layer_0_output(core, a["F0_ln2"], x1)


def add_experts(core, name, clip=None):
    nc = core.nc
    joined = core.sem(f"{name}_joined")
    with nc.Block() as block:
        @block.vector
        def _(dve):
            link = chained(dve, joined)
            for h in BOTH:
                if clip is None:
                    link(nc.vector.tensor_tensor(half(core.x, h), half(core.x, h), core.slot[1][h], ALU.add))
                else:
                    link(nc.vector.tensor_tensor(core.cen[h], half(core.xn, h), core.slot[1][h], ALU.add))
                    link(nc.vector.tensor_scalar(core.cen[h], core.cen[h], clip, -clip, ALU.min, ALU.max))
                    link(nc.vector.tensor_tensor(half(core.x, h), half(core.x, h), core.cen[h], ALU.add))


def layer_1_experts(core, a, scratch):
    comb = scratch("comb1", (8, N))
    choices_cap = int(1.25 * N / 8)
    route(core, "r1", core.xn, a["F1_router"], None, "capped", 8, comb, choices_cap)
    experts(core, "e1", core.xn, a["F1_w1"], a["F1_w2"], a["F1_b2"], comb, ACT.Relu)
    add_experts(core, "e1")


def layer_2_experts(core, a, scratch):
    comb = scratch("comb2", (16, N))
    route(core, "r2", core.xn, a["F2_router"], None, "pair", 14, comb)
    experts(core, "e2", core.xn, a["F2_w1"], a["F2_w2"], a["F2_b2"], comb, ACT.Gelu)
    add_experts(core, "e2", clip=100.0)


def program(nc, a, out, scratch):
    with ExitStack() as ctx:
        core = Core(nc, ctx)
        start(core, a["x"])
        linear_branch_of_layer_0(core, a, scratch)
        routed_branch_of_layer_0(core, a, scratch)
        residual_norm(core)
        with core.own_semaphores():
            slot_attention(core, a)
        layer_1_experts(core, a, scratch)
        residual_norm(core)
        with core.own_semaphores():
            state_space(core, a, scratch)
        layer_2_experts(core, a, scratch)
        residual_norm(core)
        causal_attention(core, a["A3_w"], a["A3_cols"])
        fp4_net(core, a["F3_gate"], a["F3_up"], a["F3_down"])
        finish(core, out)


def finish(core, out):
    nc = core.nc
    stored = core.sem("stored")
    with nc.Block() as block:
        @block.sync
        def _(sp):
            sp.dma_start(out, core.x[:, :]).then_inc(stored, 16)
            sp.wait_ge(stored, 16)


def columns(np, v):
    v = np.asarray(v)
    v = v.reshape(*v.shape[:-1], v.shape[-1] // P, P)
    return np.ascontiguousarray(np.moveaxis(v, -1, 0))


def kernel(**inputs):
    import numpy as np
    import concourse.bacc as bacc
    from concourse.bass_utils import run_bass_kernel_spmd as run

    g = {n: np.asarray(v) for n, v in inputs.items()}
    lay = lambda v: np.ascontiguousarray(v)
    of = lambda prefix: lambda n: g[prefix + n]
    L0, F0, A1, F1, A2, F2, A3, F3 = (of(f"L{i}_{b}_") for i in range(4) for b in ("attn", "ffn"))
    B = L0("Wq").shape[0]
    w, b = F0("in_proj_w"), F0("in_proj_b")

    def expert_w1(w, b):
        b = b.reshape(b.shape[0], -1, P).transpose(0, 2, 1)
        return lay(np.concatenate([w, b], axis=2))

    def expert_w2(w):
        return lay(w.reshape(w.shape[0], -1, P, D).transpose(0, 2, 1, 3))

    a = {
        "x": lay(g["L0_attn_x"].reshape(N, D).T),
        "L0_att": lay(np.concatenate([L0("Wq"), L0("Wk"), L0("Wv"), L0("Wo")], axis=2)),
        "L0_f1": lay(L0("Wf1")),
        "L0_f2": expert_w2(L0("Wf2")),
        "L0_cols": lay(np.concatenate([columns(np, L0(n)) for n in
                                       ("bq", "bk", "bv", "bo", "ln1_s", "ln1_b", "ln2_s", "ln2_b", "bf2", "bf1")], axis=2)),
        "F0_qk": lay(w[:2 * D].T),
        "F0_v": lay(w[2 * D:].T),
        "F0_qk_cols": columns(np, b[:2 * D]),
        "F0_v_bias": lay(b[2 * D:]),
        "F0_out": lay(F0("out_proj_w").T.reshape(GROUPS, GH, HD, D).transpose(1, 2, 0, 3)),
        "F0_out_cols": lay(np.stack([F0("out_proj_b"), F0("ln1_g"), F0("ln1_b")], axis=1)),
        "F0_router": lay(np.concatenate([F0("w_group"), F0("w_expert").transpose(1, 0, 2).reshape(D, -1)], axis=1)),
        "F0_router_b": lay(np.concatenate([F0("b_group"), F0("b_expert").reshape(-1)])),
        "F0_w1": expert_w1(F0("w1"), F0("b1")), "F0_w2": expert_w2(F0("w2")), "F0_b2": lay(F0("b2")),
        "F0_ln2": lay(np.stack([F0("ln2_g"), F0("ln2_b")], axis=1)),
        "A1_tok": lay(np.concatenate([A1("Wk"), A1("Wv"), A1("Wf")], axis=1)),
        "A1_qk": lay(np.concatenate([A1("Wq"), A1("Wk")], axis=1)),
        "A1_gain": lay(A1("g_norm_w").reshape(-1, 1)),
        "A1_wo": lay(A1("Wo")),
        "F1_router": lay(F1("gate_w").T),
        "F1_w1": expert_w1(F1("W1"), F1("b1")), "F1_w2": expert_w2(F1("W2")), "F1_b2": lay(F1("b2")),
        "A2_in": lay(A2("W_in")),
        "A2_x": lay(A2("W_x").reshape(-1, P, XR).transpose(1, 0, 2)),
        "A2_dt": lay(A2("W_dt")),
        "A2_out": lay(A2("W_out").reshape(-1, P, D).transpose(1, 0, 2)),
        "A2_cols": lay(np.concatenate([A2("conv_w").reshape(-1, CONV)] + [A2(n).reshape(-1, 1) for n in ("conv_b", "b_dt", "D_param")],
                                      axis=1).reshape(-1, P, CONV + 3).transpose(1, 0, 2)),
        "A2_A": lay(A2("A_log").reshape(-1, P, NS).transpose(1, 0, 2)),
        "F2_router": lay(F2("gate_w").T),
        "F2_w1": expert_w1(F2("w1"), F2("b1")), "F2_w2": expert_w2(F2("w2")), "F2_b2": lay(F2("b2")),
        "A3_w": lay(np.concatenate([A3(n).T for n in ("Wq", "Wk", "Wv", "Wo")], axis=1)),
        "A3_cols": lay(np.stack([A3(n) for n in ("bq", "bk", "bv", "bo")], axis=1)),
        "F3_gate": lay(F3("w_gate")), "F3_up": lay(F3("w_up")), "F3_down": lay(F3("w_down")),
    }
    nc = bacc.Bacc("TRN2", target_bir_lowering=False, num_devices=1)
    aps = {n: nc.dram_tensor(f"in_{n}", v.shape, mybir.dt.from_np(v.dtype), kind="ExternalInput").ap() for n, v in a.items()}
    out = nc.dram_tensor("out", (D, N), F32, kind="ExternalOutput").ap()
    scratch = lambda name, shape, dt=F32: nc.dram_tensor(name, shape, dt, kind="Internal").ap()
    program(nc, aps, out, scratch)
    r = run(nc, [{f"in_{n}": v for n, v in a.items()}], core_ids=[0])
    return lay(r.results[0]["out"].T).reshape(g["L0_attn_x"].shape)
```

```python
from contextlib import ExitStack, contextmanager

import concourse.bass as bass
from concourse import mybir

F32 = mybir.dt.float32
BF16 = mybir.dt.bfloat16
ALU = mybir.AluOpType
ACT = mybir.ActivationFunctionType
AX = mybir.AxisListType

P = 128
D = 128
HALVES = 2
T = 1024
N = HALVES * T
BANK = 512
BOTH = range(HALVES)


class Steps:

    def __init__(self, base, text, rounds):
        lead, loop, tail = text.split("|") if "|" in text else ("", text, "")
        self.lead, self.loop, self.tail = lead.split(), loop.split(), tail.split()
        self.base, self.rounds = base, rounds

    def value(self, name, i=0):
        if name in self.lead:
            return self.base + self.lead.index(name) + 1
        first = self.base + len(self.lead)
        if name in self.loop:
            return i * len(self.loop) + (first + self.loop.index(name) + 1)
        return first + self.rounds * len(self.loop) + self.tail.index(name) + 1

    def before(self, name, i):
        return i * len(self.loop) + (self.value(name) - len(self.loop))

    @property
    def end(self):
        return self.base + len(self.lead) + self.rounds * len(self.loop) + len(self.tail)


class Core:

    def __init__(self, nc, ctx):
        self.nc, self.ctx, self.taken = nc, ctx, []
        self.pe_done = [self.sem(f"pe_done{h}") for h in BOTH]
        self.act_done = [self.sem(f"act_done{h}") for h in BOTH]
        self.dve_done = [self.sem(f"dve_done{h}") for h in BOTH]
        self.pool_done = [self.sem(f"pool_done{h}") for h in BOTH]
        self.at = [0, 0, 0, 0]
        self.quad = [ctx.enter_context(nc.psum_tensor(f"quad{h}", [P, 2 * T], F32)) for h in BOTH]
        self.slot = [[self.quad[h][:, k * T:(k + 1) * T] for k in range(2)] for h in BOTH]
        self.x = self.sb("x", [P, N])
        self.xn = self.sb("xn", [P, N])
        self.mean_w = self.sb("mean_w", [P, P])
        self.centre_w = self.sb("centre_w", [P, P])
        self.eps = {1e-6: self.sb("eps6", [P, 1]), 1e-5: self.sb("eps5", [P, 1])}
        self.ident = self.sb("ident", [P, P])
        self.one = self.sb("one", [P, 1])
        self.cen_all, self.sq_all = self.sb("cen_all", [P, N]), self.sb("sq_all", [P, N])
        self.cen = [half(self.cen_all, h) for h in BOTH]
        self.sq = [half(self.sq_all, h) for h in BOTH]

    def sb(self, name, shape, dt=F32, ctx=None):
        return (ctx or self.ctx).enter_context(self.nc.sbuf_tensor(name, shape, dt))

    def sem(self, name):
        self.taken.append(self.nc.alloc_semaphore(name))
        return self.taken[-1]

    @contextmanager
    def own_semaphores(self):
        outer, self.taken = self.taken, []
        yield
        self.nc.clear_and_free_semaphores(self.taken)
        self.nc.all_engine_barrier()
        self.taken = outer

    def begin(self, pe="", act="", dve="", pool="", rounds=1):
        steps = [Steps(at, names, rounds) for at, names in zip(self.at, (pe, act, dve, pool))]
        self.at = [s.end for s in steps]
        return steps


def half(t, h):
    return t[:, h * T:(h + 1) * T]


def product(nc, out, pairs):
    for c in range(0, out.shape[-1], BANK):
        for n, (lhsT, rhs) in enumerate(pairs):
            last = nc.tensor.matmul(out[:, c:c + BANK], lhsT, rhs[:, c:c + BANK],
                                    start=(n == 0), stop=(n == len(pairs) - 1))
    return last


def norms_pe(core, pe, items, S, ready=None):
    nc, (spe, sact, sdve, _) = core.nc, S
    for h, src, s, i, pre in items:
        if ready:
            ready(h)
        product(nc, core.slot[h][s[0]], [(core.centre_w[:, :], src)]).then_inc(core.pe_done[h], 1)
    for h, src, s, i, pre in items:
        pe.wait_ge(core.act_done[h], sact.value(pre + "square", i))
        product(nc, core.slot[h][s[1]], [(core.mean_w[:, :], core.sq[h])]).then_inc(core.pe_done[h], 1)


def norms_act(core, act, items, eps, S):
    nc, (spe, sact, sdve, _) = core.nc, S
    for h, src, s, i, pre in items:
        act.wait_ge(core.pe_done[h], spe.value(pre + "centre", i))
        nc.scalar.activation(core.sq[h], core.slot[h][s[0]], ACT.Square).then_inc(core.act_done[h], 1)
    for h, src, s, i, pre in items:
        act.wait_ge(core.pe_done[h], spe.value(pre + "var", i))
        nc.scalar.activation(core.sq[h], core.slot[h][s[1]], ACT.Ln, bias=core.eps[eps][:, :]).then_inc(core.act_done[h], 1)
    for h, src, s, i, pre in items:
        act.wait_ge(core.act_done[h], sact.value(pre + "log", i))
        nc.scalar.activation(core.sq[h], core.sq[h], ACT.Exp, scale=-0.5).then_inc(core.act_done[h], 1)


def norm_pe(core, pe, streams, src, s, S, ready=None):
    norms_pe(core, pe, [(h, src(h), s, 0, "") for h in streams], S, ready)


def norm_act(core, act, streams, eps, s, S):
    norms_act(core, act, [(h, None, s, 0, "") for h in streams], eps, S)


def norm_dve(core, dve, h, out, s, S, i=0, pre=""):
    nc, (spe, sact, sdve, _) = core.nc, S
    dve.wait_ge(core.act_done[h], sact.value(pre + "rstd", i))
    nc.vector.tensor_tensor(out, core.slot[h][s[0]], core.sq[h], ALU.mult).then_inc(core.dve_done[h], 1)


def start(core, x_in):
    nc = core.nc
    S = spe, sact, sdve, spool = core.begin("centre var", "square log rstd", "scaled",
                                            "zero eps6 eps5 one mean_w ident centre_w")
    x_landed = core.sem("x_landed")
    with nc.Block() as block:
        @block.sync
        def _(sp):
            sp.dma_start(core.x[:, :], x_in).then_inc(x_landed, 16)

        @block.gpsimd
        def _(pool):
            for h in BOTH:
                nc.gpsimd.memset(core.ident[:, :], 0.0).then_inc(core.pool_done[h], 1)
                nc.gpsimd.memset(core.eps[1e-6][:, :], 1e-6).then_inc(core.pool_done[h], 1)
                nc.gpsimd.memset(core.eps[1e-5][:, :], 1e-5).then_inc(core.pool_done[h], 1)
                nc.gpsimd.memset(core.one[:, :], 1.0).then_inc(core.pool_done[h], 1)
                nc.gpsimd.memset(core.mean_w[:, :], 1.0 / D).then_inc(core.pool_done[h], 1)
                pool.wait_ge(core.pool_done[h], spool.value("mean_w"))
                nc.gpsimd.affine_select(out=core.ident[:, :], in_=core.ident[:, :], compare_op=ALU.not_equal,
                                        fill=1.0, base=0, pattern=[[-1, P]], channel_multiplier=1
                                        ).then_inc(core.pool_done[h], 1)
                pool.wait_ge(core.pool_done[h], spool.value("ident"))
                nc.gpsimd.tensor_tensor(core.centre_w[:, :], core.ident[:, :], core.mean_w[:, :], ALU.subtract).then_inc(core.pool_done[h], 1)
                pool.wait_ge(core.pool_done[h], spool.value("centre_w"))

        @block.tensor
        def _(pe):
            pe.wait_ge(x_landed, 16)
            pe.wait_ge(core.pool_done[1], spool.value("centre_w"))
            norm_pe(core, pe, BOTH, lambda h: half(core.x, h), (0, 1), S)

        @block.scalar
        def _(act):
            norm_act(core, act, BOTH, 1e-5, (0, 1), S)

        @block.vector
        def _(dve):
            for h in BOTH:
                norm_dve(core, dve, h, half(core.xn, h), (0, 1), S)


def residual_norm(core):
    nc = core.nc
    S = spe, sact, sdve, spool = core.begin("centre var", "square log rstd", "scaled", "")
    with nc.Block() as block:
        @block.tensor
        def _(pe):
            norm_pe(core, pe, BOTH, lambda h: half(core.x, h), (0, 1), S)

        @block.scalar
        def _(act):
            norm_act(core, act, BOTH, 1e-5, (0, 1), S)

        @block.vector
        def _(dve):
            for h in BOTH:
                norm_dve(core, dve, h, half(core.xn, h), (0, 1), S)


STREAMS = 4
TS = N // STREAMS
EVERY = range(STREAMS)


class Streams:

    def __init__(self, core):
        self.nc, self.mean_w, self.centre_w, self.eps = core.nc, core.mean_w, core.centre_w, core.eps
        self.slot = [[core.slot[s // 2][s % 2][:, k * TS:(k + 1) * TS] for k in range(2)] for s in EVERY]
        self.pe_done, self.act_done, self.dve_done, self.pool_done = (
            [core.sem(f"{e}_stream{s}") for s in EVERY] for e in ("pe", "act", "dve", "pool"))
        self.cen = [core.cen_all[:, s * TS:(s + 1) * TS] for s in EVERY]
        self.sq = [core.sq_all[:, s * TS:(s + 1) * TS] for s in EVERY]


def linear_blocks(core, w_att, w_f1, w_f2, cols):
    nc = core.nc
    B = w_att.shape[0]
    FT = w_f1.shape[2] // P
    BQ, BK, BV, BO, L1S, L1B, L2S, L2B, BF2, BF1 = range(10)
    VECTORS = BF1 + FT
    FIRST, SECOND = (0, 1), (2, 3)
    NONE = ()
    st = Streams(core)
    S = spe, sact, sdve, spool = [Steps(0, text, B) for text in (
        "| q k v o n1centre n1var f0 f1 f2 f3 ff n2centre n2var |",
        "| relu_q exp_q relu_k exp_k gelu_o n1square n1log n1rstd h0 h1 h2 h3 gelu_ff n2square n2log n2rstd |",
        "enter | less_k K less_q Q kv total den recip mix res1 n1scaled n1affine res2 n2scaled n2affine |",
        "| | join")]
    att_landed, f1_landed, f2_landed, cols_landed, cols_ready = (
        core.sem(n) for n in ("att_landed", "f1_landed", "f2_landed", "cols_landed", "cols_ready"))
    with ExitStack() as ctx:
        sb = lambda name, shape, dt=F32: core.sb(name, shape, dt, ctx)
        per_stream = lambda name, *shape: [sb(f"{name}{s}", [P, *shape]) for s in EVERY]
        wa = sb("wa", [P, 4 * D])
        wf1 = sb("wf1", [P, FT * P])
        wf2 = sb("wf2", [P, FT, D])
        col = sb("col", [P, B, VECTORS])
        near = sb("near", [P, 2, VECTORS])
        cur, q, k = per_stream("cur", TS), per_stream("q", TS), per_stream("k", TS)
        mq, mk = per_stream("mq", TS), per_stream("mk", TS)
        hid = per_stream("hid", FT, TS)
        sums = per_stream("sums", 2)
        totals = per_stream("totals", 2)

        def segments(engine, segment, enter=None, leave=None):
            fixed = lambda i: lambda c: col[:, i, c:c + 1]
            now, ahead = (lambda c: near[:, 0, c:c + 1]), (lambda c: near[:, 1, c:c + 1])
            segment(FIRST, 0, fixed(0), NONE, 0, None)
            with engine.Fori(0, B - 1) as i:
                if enter:
                    enter(i)
                segment(SECOND, i, now, FIRST, i, now)
                segment(FIRST, i + 1, ahead, SECOND, i, now)
                if leave:
                    leave(i)
            segment(SECOND, B - 1, fixed(B - 1), FIRST, B - 1, fixed(B - 1))
            segment(NONE, 0, None, SECOND, B - 1, fixed(B - 1))

        def norms(att, i, net, j):
            return ([(s, k[s][:, :], (1, 0), j, "n2") for s in net] + [(s, k[s][:, :], (0, 1), i, "n1") for s in att])

        with nc.Block() as block:
            @block.sync
            def _(sp):
                sp.dma_start(col[:, :, :], cols).then_inc(cols_landed, 16)
                sp.dma_start(wa[:, :], w_att[0]).then_inc(att_landed, 16)
                sp.dma_start(wf1[:, :], w_f1[0]).then_inc(f1_landed, 16)
                sp.dma_start(wf2[:, :, :], w_f2[0]).then_inc(f2_landed, 16)
                with sp.Fori(0, B - 1) as i:
                    sp.wait_ge(st.pe_done[SECOND[1]], spe.value("o", i))
                    sp.dma_start(wa[:, :], w_att[i + 1]).then_inc(att_landed, 16)
                    sp.wait_ge(st.pe_done[SECOND[1]], spe.value("f3", i))
                    sp.dma_start(wf1[:, :], w_f1[i + 1]).then_inc(f1_landed, 16)
                    sp.wait_ge(st.pe_done[SECOND[1]], spe.value("ff", i))
                    sp.dma_start(wf2[:, :, :], w_f2[i + 1]).then_inc(f2_landed, 16)

            @block.tensor
            def _(pe):
                done = st.pe_done

                def segment(att, i, _ca, net, j, _cn):
                    if att:
                        pe.wait_ge(att_landed, i * 16 + 16)
                    for s in att:
                        pe.wait_ge(st.dve_done[s], sdve.before("n2affine", i))
                        product(nc, st.slot[s][0], [(wa[:, 0:D], cur[s][:, :])]).then_inc(done[s], 1)
                        product(nc, st.slot[s][1], [(wa[:, D:2 * D], cur[s][:, :])]).then_inc(done[s], 1)
                    if net:
                        pe.wait_ge(f1_landed, j * 16 + 16)
                    for f in range(FT):
                        for s in net:
                            if f == 0:
                                pe.wait_ge(st.dve_done[s], sdve.value("n1affine", j))
                            if f >= 2:
                                pe.wait_ge(st.act_done[s], sact.value(f"h{f - 2}", j))
                            product(nc, st.slot[s][f % 2], [(wf1[:, f * P:(f + 1) * P], q[s][:, :])]).then_inc(done[s], 1)
                        if f == 1:
                            for s in att:
                                pe.wait_ge(st.act_done[s], sact.value("exp_q", i))
                                product(nc, st.slot[s][0], [(wa[:, 2 * D:3 * D], cur[s][:, :])]).then_inc(done[s], 1)
                    if net:
                        pe.wait_ge(f2_landed, j * 16 + 16)
                    for s in net:
                        pe.wait_ge(st.act_done[s], sact.value(f"h{FT - 1}", j))
                        product(nc, st.slot[s][0], [(wf2[:, f, :], hid[s][:, f, :]) for f in range(FT)]).then_inc(done[s], 1)
                    for s in att:
                        pe.wait_ge(st.dve_done[s], sdve.value("mix", i))
                        product(nc, st.slot[s][1], [(wa[:, 3 * D:4 * D], mq[s][:, :])]).then_inc(done[s], 1)
                    norms_pe(st, pe, norms(att, i, net, j), S, ready=lambda s: pe.wait_ge(
                        st.dve_done[s], sdve.value("res1", i) if s in att else sdve.value("res2", j)))

                segments(pe, segment)

            @block.scalar
            def _(act):
                done = st.act_done
                act.wait_ge(cols_landed, 16)

                def segment(att, i, ca, net, j, cn):
                    for s in att:
                        act.wait_ge(st.pe_done[s], spe.value("q", i))
                        nc.scalar.activation(q[s][:, :], st.slot[s][0], ACT.Relu, bias=ca(BQ)).then_inc(done[s], 1)
                        nc.scalar.activation(mq[s][:, :], st.slot[s][0], ACT.Exp, bias=ca(BQ)).then_inc(done[s], 1)
                        act.wait_ge(st.pe_done[s], spe.value("k", i))
                        nc.scalar.activation(k[s][:, :], st.slot[s][1], ACT.Relu, bias=ca(BK)).then_inc(done[s], 1)
                        nc.scalar.activation(mk[s][:, :], st.slot[s][1], ACT.Exp, bias=ca(BK)).then_inc(done[s], 1)
                    for f in range(FT):
                        for s in net:
                            act.wait_ge(st.pe_done[s], spe.value(f"f{f}", j))
                            nc.scalar.activation(hid[s][:, f, :], st.slot[s][f % 2], ACT.Gelu_apprx_tanh, bias=cn(BF1 + f)).then_inc(done[s], 1)
                    for s in net:
                        act.wait_ge(st.pe_done[s], spe.value("ff", j))
                        nc.scalar.activation(mk[s][:, :], st.slot[s][0], ACT.Gelu_apprx_tanh, bias=cn(BF2)).then_inc(done[s], 1)
                    for s in att:
                        act.wait_ge(st.pe_done[s], spe.value("o", i))
                        nc.scalar.activation(mk[s][:, :], st.slot[s][1], ACT.Gelu_apprx_tanh, bias=ca(BO)).then_inc(done[s], 1)
                    norms_act(st, act, norms(att, i, net, j), 1e-6, S)

                segments(act, segment, enter=lambda i: act.wait_ge(cols_ready, i + 1))

            @block.vector
            def _(dve):
                done = st.dve_done
                for s in EVERY:
                    nc.vector.tensor_copy(cur[s][:, :], core.xn[:, s * TS:(s + 1) * TS]).then_inc(done[s], 1)
                dve.wait_ge(cols_landed, 16)

                def segment(att, i, ca, net, j, cn):
                    for s in att:
                        dve.wait_ge(st.act_done[s], sact.value("exp_k", i))
                        for n, m, t, total in (("k", mk[s], k[s], dict(accum_out=sums[s][:, 0:1])), ("q", mq[s], q[s], {})):
                            nc.vector.tensor_scalar(m[:, :], m[:, :], 1.0, -1.0, ALU.min, ALU.add).then_inc(done[s], 1)
                            dve.wait_ge(done[s], sdve.value(f"less_{n}", i))
                            nc.vector.scalar_tensor_tensor(out=t[:, :], in0=t[:, :], scalar=1.0, in1=m[:, :],
                                                           op0=ALU.add, op1=ALU.add, **total).then_inc(done[s], 1)
                    for s in att:
                        dve.wait_ge(done[s], sdve.value("Q", i))
                        dve.wait_ge(st.pe_done[s], spe.value("v", i))
                        nc.vector.scalar_tensor_tensor(out=mk[s][:, :], in0=st.slot[s][0], scalar=ca(BV), in1=k[s][:, :],
                                                       op0=ALU.add, op1=ALU.mult, accum_out=sums[s][:, 1:2]).then_inc(done[s], 1)
                    for s in att:
                        dve.wait_ge(done[s], sdve.value("kv", i))
                    for s in att:
                        nc.vector.tensor_tensor(totals[s][:, :], sums[att[0]][:, :], sums[att[1]][:, :], ALU.add).then_inc(done[s], 1)
                    for s in att:
                        dve.wait_ge(done[s], sdve.value("total", i))
                        nc.vector.tensor_scalar(mk[s][:, :], q[s][:, :], totals[s][:, 0:1], 1e-6, ALU.mult, ALU.add).then_inc(done[s], 1)
                        dve.wait_ge(done[s], sdve.value("den", i))
                        nc.vector.reciprocal(mk[s][:, :], mk[s][:, :]).then_inc(done[s], 1)
                        dve.wait_ge(done[s], sdve.value("recip", i))
                        nc.vector.scalar_tensor_tensor(out=mq[s][:, :], in0=q[s][:, :], scalar=totals[s][:, 1:2], in1=mk[s][:, :],
                                                       op0=ALU.mult, op1=ALU.mult).then_inc(done[s], 1)
                    for s in net:
                        dve.wait_ge(st.act_done[s], sact.value("gelu_ff", j))
                        nc.vector.tensor_tensor(k[s][:, :], mk[s][:, :], q[s][:, :], ALU.add).then_inc(done[s], 1)
                    for s in att:
                        dve.wait_ge(st.act_done[s], sact.value("gelu_o", i))
                        nc.vector.tensor_tensor(k[s][:, :], mk[s][:, :], cur[s][:, :], ALU.add).then_inc(done[s], 1)
                    for s in net:
                        norm_dve(st, dve, s, st.cen[s], (1, 0), S, j, "n2")
                        dve.wait_ge(done[s], sdve.value("n2scaled", j))
                        nc.vector.tensor_scalar(cur[s][:, :], st.cen[s], cn(L2S), cn(L2B), ALU.mult, ALU.add).then_inc(done[s], 1)
                    for s in att:
                        norm_dve(st, dve, s, st.cen[s], (0, 1), S, i, "n1")
                        dve.wait_ge(done[s], sdve.value("n1scaled", i))
                        nc.vector.tensor_scalar(q[s][:, :], st.cen[s], ca(L1S), ca(L1B), ALU.mult, ALU.add).then_inc(done[s], 1)

                def enter(i):
                    nc.vector.tensor_copy(near[:, :, :], col[:, bass.ds(i, 2), :]).then_inc(cols_ready, 1)
                    dve.wait_ge(cols_ready, i + 1)

                def leave(i):
                    for s in FIRST:
                        dve.wait_ge(done[s], sdve.value("n1affine", i + 1))
                    for s in SECOND:
                        dve.wait_ge(done[s], sdve.value("n2affine", i))

                segments(dve, segment, enter, leave)

            @block.gpsimd
            def _(pool):
                done = st.pool_done

                for s in EVERY:
                    pool.wait_ge(st.dve_done[s], sdve.value("n2affine", B - 1))
                    x = core.x[:, s * TS:(s + 1) * TS]
                    nc.gpsimd.tensor_tensor(x, x, cur[s][:, :], ALU.add).then_inc(done[s], 1)


HEADS, HD = 16, 8
GROUPS, GH = 4, 4
KT = T // P
TERMS = 6
Q_PARTS, K_PARTS = (0, 0, 1, 0, 2, 1), (0, 1, 0, 2, 0, 1)
ROWS = TERMS * HD


def attention_stacks(core, ctx):
    return [[core.sb(f"{n}s{h}", [P, GH, T], BF16, ctx) for h in BOTH] for n in "qk"]


def attention_inputs(core, w_qk, w_v, cols, v_bias, q_dram, k_dram, v_dram, stacks):
    nc = core.nc
    S = spe, sact, sdve, spool = core.begin(
        "q k v", "q k", "q0 qr0 q1 qr1 q2 k0 kr0 k1 kr1 k2 v", "")
    att_w, stacked, rows_cleared = core.sem("att_w"), core.sem("stacked"), core.sem("rows_cleared")
    with ExitStack() as ctx:
        sb = lambda name, shape, dt=F32: core.sb(name, shape, dt, ctx)
        wqk = sb("wqk", [P, 2 * D])
        wv = sb("wv", [P, D])
        col = sb("colqk", [P, 2])
        vb = sb("vb", [P, D])
        full = [[sb(f"full{h}{i}", [P, T]) for i in range(2)] for h in BOTH]
        part = [[[sb(f"part{h}{i}{n}", [P, T], BF16) for n in range(3)] for i in range(2)] for h in BOTH]
        v = [sb(f"v{h}", [P, KT, D]) for h in BOTH]
        with nc.Block() as block:
            @block.gpsimd
            def _(pool):
                for h in BOTH:
                    for stack in stacks:
                        nc.gpsimd.memset(stack[h][:, :, :], 0.0).then_inc(rows_cleared, 1)
                pool.wait_ge(rows_cleared, 2 * HALVES)

            @block.sync
            def _(sp):
                sp.dma_start(wqk[:, :], w_qk).then_inc(att_w, 16)
                sp.dma_start(col[:, :], cols).then_inc(att_w, 16)
                sp.dma_start(wv[:, :], w_v).then_inc(att_w, 16)
                sp.dma_start(vb[:, :], v_bias.partition_broadcast(P)).then_inc(att_w, 16)
                for h in BOTH:
                    for i, (dram, parts, n) in enumerate(((q_dram, Q_PARTS, "q"), (k_dram, K_PARTS, "k"))):
                        sp.wait_ge(core.dve_done[h], sdve.value(f"{n}2"))
                        rows = dram[h].rearrange("g j (t d) x -> t (g j) d x", d=HD)
                        for t, p in enumerate(parts):
                            sp.dma_start(rows[t], part[h][i][p][:, :]).then_inc(stacked, 16)
                    sp.wait_ge(core.dve_done[h], sdve.value("v"))
                    for g in range(GROUPS):
                        sp.dma_start(v_dram[h, g], v[h][:, :, g * GH * HD:(g + 1) * GH * HD]).then_inc(stacked, 16)
                sp.wait_ge(stacked, HALVES * (2 * TERMS + GROUPS) * 16)

            @block.tensor
            def _(pe):
                pe.wait_ge(att_w, 64)
                for h in BOTH:
                    x = half(core.xn, h)
                    product(nc, core.slot[h][0], [(wqk[:, 0:D], x)]).then_inc(core.pe_done[h], 1)
                    product(nc, core.slot[h][1], [(wqk[:, D:2 * D], x)]).then_inc(core.pe_done[h], 1)
                for h in BOTH:
                    x = half(core.xn, h)
                    pe.wait_ge(core.act_done[h], sact.value("q"))
                    for t in range(KT):
                        last = nc.tensor.matmul(core.slot[h][0][:, t * D:(t + 1) * D], x[:, t * P:(t + 1) * P], wv[:, :],
                                                start=(t % 4 == 0), stop=(t % 4 == 3), skip_group_check=True)
                    last.then_inc(core.pe_done[h], 1)

            @block.scalar
            def _(act):
                act.wait_ge(att_w, 64)
                for h in BOTH:
                    for i, n in enumerate("qk"):
                        act.wait_ge(core.pe_done[h], spe.value(n))
                        nc.scalar.activation(full[h][i][:, :], core.slot[h][i][:, :], ACT.Identity,
                                             bias=col[:, i:i + 1]).then_inc(core.act_done[h], 1)

            @block.vector
            def _(dve):
                dve.wait_ge(att_w, 64)
                for h in BOTH:
                    done = core.dve_done[h]
                    for i, n in enumerate("qk"):
                        f, p = full[h][i], part[h][i]
                        dve.wait_ge(core.act_done[h], sact.value(n))
                        nc.vector.tensor_copy(p[0][:, :], f[:, :]).then_inc(done, 1)
                        for m in range(2):
                            dve.wait_ge(done, sdve.value(f"{n}{m}"))
                            nc.vector.tensor_tensor(f[:, :], f[:, :], p[m][:, :], ALU.subtract).then_inc(done, 1)
                            dve.wait_ge(done, sdve.value(f"{n}r{m}"))
                            nc.vector.tensor_copy(p[m + 1][:, :], f[:, :]).then_inc(done, 1)
                    dve.wait_ge(core.pe_done[h], spe.value("v"))
                    nc.vector.tensor_tensor(v[h][:, :, :], core.slot[h][0].rearrange("p (t d) -> p t d", d=D),
                                            vb[:, :].rearrange("p (a d) -> p a d", a=1).to_broadcast([P, KT, D]),
                                            ALU.add).then_inc(done, 1)


def attention(core, q_dram, k_dram, v_dram, qs, ks, mixed):
    nc = core.nc
    scale = float(HD) ** -0.5
    UNITS = GH * KT
    SEARCHING = 6 * GH + 2
    MAXES = 2 * UNITS
    RING = MAXES + 4
    sem = core.sem
    ones_set, ones_landed, stack_landed, v_landed = sem("ones_set"), sem("ones_landed"), [sem(f"stack_landed{h}") for h in BOTH], [sem(f"v_landed{h}") for h in BOTH]
    scores_ready, weights_ready, weights_used = sem("scores_ready"), sem("weights_ready"), sem("weights_used")
    bank_ready, bank_free, maxima_found, maxima_landed = sem("bank_ready"), sem("bank_free"), sem("maxima_found"), sem("maxima_landed")
    sums_copied, sums_inverted, heads_done = sem("sums_copied"), sem("sums_inverted"), sem("heads_done")
    READY, COPIED = 2, 1
    with ExitStack() as ctx:
        sb = lambda name, shape, dt=F32: core.sb(name, shape, dt, ctx)
        zeros = sb("zeros", [GH, T], BF16)
        vg = [sb(f"vg{h}", [P, KT, GH, 32]) for h in BOTH]
        ones = sb("ones", [GH, T], BF16)
        spread = sb("spread", [P, P])
        weights = sb("weights", [P, 2, GH, T])
        best = sb("best", [P, UNITS, 2])
        neg = sb("neg", [P, UNITS])
        negb = [sb(f"negb{i}", [UNITS // 2, P], BF16) for i in range(2)]
        raw = sb("raw", [P, T])
        inv = sb("inv", [P, T])
        score = [core.quad[0][:, i * T:(i + 1) * T] for i in range(2)]
        out = core.quad[1][:, 0:T]
        bank = [core.quad[1][:, T + i * BANK:T + (i + 1) * BANK] for i in range(2)]

        def use(n, k):
            return k + 2 if isinstance(n, int) and n < 0 else n * RING + (RING + k)

        with nc.Block() as block:
            @block.sync
            def _(sp):
                sp.wait_ge(ones_set, 7)
                for h in BOTH:
                    sp.dma_start(ks[h][ROWS:ROWS + 1, :, :], ones[:, :]).then_inc(ones_landed, 16)

                def load(h, g):
                    sp.dma_start(qs[h][ROWS:ROWS + 1, :, :], zeros[:, :]).then_inc(stack_landed[h], 16)
                    sp.dma_start(qs[h][0:ROWS, :, :], q_dram[h, g].rearrange("j r t -> r j t")).then_inc(stack_landed[h], 16)
                    sp.dma_start(ks[h][0:ROWS, :, :], k_dram[h, g].rearrange("j r t -> r j t")).then_inc(stack_landed[h], 16)
                    sp.dma_start(vg[h][:, :, :, 0:HD].rearrange("p t j d -> p (t j) d"),
                                 v_dram[h, g].rearrange("p t (j d) -> p (t j) d", d=HD)).then_inc(v_landed[h], 16)

                def maxima_rows(n, h):
                    for i in range(2):
                        sp.wait_ge(bank_free, use(n - 1, MAXES + i + 1))
                        for j in range(2):
                            sp.dma_start(qs[h][ROWS:ROWS + 1, 2 * i + j, :], negb[i][j * KT:(j + 1) * KT, :]).then_inc(maxima_landed, 16)

                load(0, 0)
                load(1, 0)
                maxima_rows(0, 0)

                def turn(n, h, g, more):
                    if h == 0 or more:
                        maxima_rows(n + 1, 1 - h)
                    if more:
                        sp.wait_ge(weights_used, n * KT + KT)
                        load(h, g + 1)

                with sp.Fori(0, GROUPS - 1) as g:
                    for h in BOTH:
                        turn(g * 2 + h, h, g, True)
                for h in BOTH:
                    turn(2 * GROUPS - 2 + h, h, GROUPS - 1, False)

            @block.gpsimd
            def _(pool):
                nc.gpsimd.memset(ones[:, :], 1.0).then_inc(ones_set, 1)
                nc.gpsimd.memset(zeros[:, :], 0.0).then_inc(ones_set, 1)
                nc.gpsimd.memset(spread[:, :], 0.0).then_inc(ones_set, 1)
                for h in BOTH:
                    nc.gpsimd.memset(vg[h][:, :, :, HD:32], 0.0).then_inc(ones_set, 1)
                pool.wait_ge(ones_set, 5)
                for h in BOTH:
                    nc.gpsimd.memset(vg[h][:, :, :, HD:HD + 1], 1.0).then_inc(ones_set, 1)
                nc.gpsimd.affine_select(out=spread[:, :].rearrange("p (j c) -> p j c", c=32),
                                        in_=spread[:, :].rearrange("p (j c) -> p j c", c=32),
                                        compare_op=ALU.not_equal, fill=1.0, base=-HD,
                                        pattern=[[-32, GH], [0, 32]], channel_multiplier=1).then_inc(ones_set, 1)

            @block.tensor
            def _(pe):
                pe.wait_ge(ones_set, 8)
                pe.wait_ge(ones_landed, 32)
                pe.sem_inc(bank_ready, 2)

                def maxima(n, h, g, lo, hi):
                    for k in range(lo, hi):
                        j, qt, c = k // (2 * KT), k // 2 % KT, k % 2
                        if k == 0:
                            pe.wait_ge(stack_landed[h], g * 48 + 48)
                        pe.wait_ge(bank_free, use(n - 1, k - 1))
                        nc.tensor.matmul(bank[k % 2], qs[h][:, j, qt * P:(qt + 1) * P], ks[h][:, j, c * BANK:(c + 1) * BANK],
                                         start=True, stop=True).then_inc(bank_ready, 1)

                def turned(n):
                    for i in range(2):
                        pe.wait_ge(bank_free, use(n - 1, MAXES + i - 1))
                        pe.wait_ge(maxima_found, n + 1)
                        nc.tensor.transpose(bank[i][0:UNITS // 2, 0:P], neg[:, i * UNITS // 2:(i + 1) * UNITS // 2],
                                            core.ident[:, :]).then_inc(bank_ready, 1)

                def scores(n, h, kt, j):
                    if kt == 0 and j == 0:
                        pe.wait_ge(maxima_landed, n * 64 + 64)
                    pe.wait_ge(weights_ready, n * UNITS + (kt * GH + j - 2 + 1 + READY))
                    for c in range(2):
                        last = nc.tensor.matmul(score[j % 2][:, c * BANK:(c + 1) * BANK], ks[h][:, j, kt * P:(kt + 1) * P],
                                                qs[h][:, j, c * BANK:(c + 1) * BANK], start=True, stop=True)
                    last.then_inc(scores_ready, 1)

                def weighted(n, h, g, kt, c):
                    if kt == 0 and c == 0:
                        pe.wait_ge(v_landed[h], g * 16 + 16)
                        pe.wait_ge(sums_copied, n + COPIED)
                    if c == 0:
                        pe.wait_ge(weights_ready, n * UNITS + (kt * GH + GH + READY))
                    for j in range(GH):
                        last = nc.tensor.matmul(out[32 * j:32 * j + 32, c * BANK:(c + 1) * BANK], vg[h][:, kt, j, :],
                                                weights[:, kt % 2, j, c * BANK:(c + 1) * BANK], start=(kt == 0), stop=(kt == KT - 1))
                    if c == 1:
                        last.then_inc(weights_used, 1)

                def sums(n, first):
                    pe.wait_ge(sums_copied, n + 1 + COPIED)
                    for c in range(2):
                        pe.wait_ge(bank_free, use(n, first + c - 1))
                        nc.tensor.matmul(bank[c], spread[:, :], raw[:, c * BANK:(c + 1) * BANK], start=True, stop=True).then_inc(bank_ready, 1)

                def turn(n, h, g, more):
                    ahead = h == 0 or more
                    g2 = g if h == 0 else g + 1
                    searched = 0
                    for kt in range(KT):
                        for j in range(GH):
                            scores(n, h, kt, j)
                            if kt and j % 2:
                                weighted(n, h, g, kt - 1, j // 2)
                            if ahead and kt:
                                upto = min(((kt - 1) * GH + j + 1) * MAXES // SEARCHING, MAXES)
                                maxima(n + 1, 1 - h, g2, searched, upto)
                                searched = upto
                                if kt == KT - 1 and j == 2:
                                    turned(n + 1)
                    for c in range(2):
                        weighted(n, h, g, KT - 1, c)
                    sums(n, MAXES + 2 if ahead else 0)

                maxima(0, 0, 0, 0, MAXES)
                turned(0)
                with pe.Fori(0, GROUPS - 1) as g:
                    for h in BOTH:
                        turn(g * 2 + h, h, g, True)
                for h in BOTH:
                    turn(2 * GROUPS - 2 + h, h, GROUPS - 1, False)

            @block.scalar
            def _(act):
                act.sem_inc(weights_ready, READY)

                def turn(n):
                    for kt in range(KT):
                        act.wait_ge(weights_used, n * KT + kt - 1) if not isinstance(n, int) or n * KT + kt - 1 > 0 else None
                        for j in range(GH):
                            act.wait_ge(scores_ready, n * UNITS + (kt * GH + j + 1))
                            nc.scalar.activation(weights[:, kt % 2, j, :], score[j % 2], ACT.Exp, scale=scale).then_inc(weights_ready, 1)

                turn(0)
                with act.Fori(1, 2 * GROUPS) as n:
                    turn(n)

            @block.vector
            def _(dve):
                dve.sem_inc(bank_free, 2)
                dve.sem_inc(sums_copied, COPIED)

                def maxima(n, h):
                    dve.wait_ge(maxima_found, n) if not isinstance(n, int) or n else None
                    for k in range(MAXES):
                        dve.wait_ge(bank_ready, use(n - 1, k + 1))
                        nc.vector.tensor_reduce(best[:, k // 2, k % 2:k % 2 + 1], bank[k % 2], AX.X, ALU.max).then_inc(bank_free, 1)
                    dve.wait_ge(bank_free, use(n - 1, MAXES))
                    nc.vector.tensor_reduce(neg[:, :], best[:, :, :], AX.X, ALU.max, negate=True).then_inc(maxima_found, 1)
                    if not isinstance(n, int) or n:
                        dve.wait_ge(maxima_landed, n * 64)
                    for i in range(2):
                        dve.wait_ge(bank_ready, use(n - 1, MAXES + i + 1))
                        nc.vector.tensor_copy(negb[i][:, :], bank[i][0:UNITS // 2, 0:P]).then_inc(bank_free, 1)

                def turn(n, h, g, more):
                    ahead = h == 0 or more
                    if ahead:
                        maxima(n + 1, 1 - h)
                    first = MAXES + 2 if ahead else 0
                    dve.wait_ge(weights_used, n * KT + KT)
                    if not isinstance(n, int) or n:
                        dve.wait_ge(heads_done, n)
                    nc.vector.tensor_copy(raw[:, :], out).then_inc(sums_copied, 1)
                    for c in range(2):
                        dve.wait_ge(bank_ready, use(n, first + c + 1))
                        nc.vector.reciprocal(inv[:, c * BANK:(c + 1) * BANK], bank[c]).then_inc(bank_free, 1)
                    dve.wait_ge(bank_free, use(n, first + 2))
                    dve.wait_ge(sums_copied, n + 1 + COPIED)
                    at = mixed[h][:, g, :] if isinstance(g, int) else mixed[h][:, bass.ds(g, 1), :].rearrange("p a t -> p (a t)")
                    nc.vector.tensor_tensor(at, raw[:, :], inv[:, :], ALU.mult).then_inc(heads_done, 1)

                maxima(0, 0)
                with dve.Fori(0, GROUPS - 1) as g:
                    for h in BOTH:
                        turn(g * 2 + h, h, g, True)
                for h in BOTH:
                    turn(2 * GROUPS - 2 + h, h, GROUPS - 1, False)


def attention_output(core, w_out, cols, mixed, x1):
    nc = core.nc
    S = spe, sact, sdve, spool = core.begin("o centre var", "square log rstd", "res scaled affine", "w_zero")
    out_w, cols_landed = core.sem("out_w"), core.sem("out_cols")
    with ExitStack() as ctx:
        sb = lambda name, shape, dt=F32: core.sb(name, shape, dt, ctx)
        w = sb("wout", [P, GROUPS, D])
        col = sb("colout", [P, 3])
        res = [sb(f"res{h}", [P, T]) for h in BOTH]
        with nc.Block() as block:
            @block.sync
            def _(sp):
                sp.dma_start(col[:, :], cols).then_inc(cols_landed, 16)
                sp.wait_ge(core.pool_done[1], spool.value("w_zero"))
                for j in range(GH):
                    sp.dma_start(w[32 * j:32 * j + HD, :, :], w_out[j]).then_inc(out_w, 16)

            @block.gpsimd
            def _(pool):
                for h in BOTH:
                    if h:
                        pool.wait_ge(core.pool_done[0], spool.value("w_zero"))
                    nc.gpsimd.memset(w[:, :, :], 0.0).then_inc(core.pool_done[h], 1)

            @block.tensor
            def _(pe):
                pe.wait_ge(out_w, GH * 16)
                for h in BOTH:
                    product(nc, core.slot[h][0], [(w[:, g, :], mixed[h][:, g, :]) for g in range(GROUPS)]).then_inc(core.pe_done[h], 1)
                norm_pe(core, pe, BOTH, lambda h: res[h][:, :], (0, 1), S,
                        ready=lambda h: pe.wait_ge(core.dve_done[h], sdve.value("res")))

            @block.scalar
            def _(act):
                norm_act(core, act, BOTH, 1e-5, (0, 1), S)

            @block.vector
            def _(dve):
                dve.wait_ge(cols_landed, 16)
                for h in BOTH:
                    dve.wait_ge(core.pe_done[h], spe.value("o"))
                    nc.vector.scalar_tensor_tensor(out=res[h][:, :], in0=core.slot[h][0], scalar=col[:, 0:1], in1=half(core.xn, h),
                                                   op0=ALU.add, op1=ALU.add).then_inc(core.dve_done[h], 1)
                for h in BOTH:
                    norm_dve(core, dve, h, core.cen[h], (0, 1), S)
                    dve.wait_ge(core.dve_done[h], sdve.value("scaled"))
                    nc.vector.tensor_scalar(half(x1, h), core.cen[h], col[:, 1:2], col[:, 2:3], ALU.mult, ALU.add).then_inc(core.dve_done[h], 1)


TILES = N // P


def chained(eng, chained_steps, base=0):
    count = [base]

    def link(ins):
        count[0] += 1
        ins.then_inc(chained_steps, 1)
        eng.wait_ge(chained_steps, count[0])
    return link


def over_tiles(v, n):
    if v.shape[-1] == TILES:
        return v.rearrange("p (t a) -> p t a", a=1).to_broadcast([P, TILES, n])
    return v.rearrange("p (a n) -> p a n", a=1).to_broadcast([P, TILES, n])


def first_best(nc, link, chosen, values, count, top, late, least):
    n = values.shape[-1]
    link(nc.vector.tensor_reduce(top, values, AX.X, ALU.max))
    link(nc.vector.tensor_tensor(late, values, over_tiles(top, n), ALU.is_lt))
    link(nc.vector.scalar_tensor_tensor(out=late, in0=late, scalar=100.0, in1=over_tiles(count, n), op0=ALU.mult, op1=ALU.add))
    link(nc.vector.tensor_reduce(least, late, AX.X, ALU.min))
    link(nc.vector.tensor_tensor(chosen, late, over_tiles(least, n), ALU.is_equal))


def route(core, name, src, w_router, b_router, kind, E, comb_dram, cap=None):
    nc = core.nc
    EP = 8 if E <= 8 else 16
    R = w_router.shape[1]
    BLOCKS = TILES * EP // P
    w_landed, b_landed, set_up, logits_ready = (core.sem(f"{name}_{n}") for n in ("w_landed", "b_landed", "set_up", "logits_ready"))
    steps, shifted, exps_ready = (core.sem(f"{name}_{n}") for n in ("steps", "shifted", "exps_ready"))
    counted, counts_ready, comb_ready, turned, turned_copied, stored = (
        core.sem(f"{name}_{n}") for n in ("counted", "counts_ready", "comb_ready", "turned", "turned_copied", "stored"))
    with ExitStack() as ctx:
        sb = lambda n, shape, dt=F32: core.sb(f"{name}_{n}", shape, dt, ctx)
        w = sb("w", [P, R])
        b = sb("b", [P, R])
        logits = sb("logits", [P, TILES, R])
        exps = sb("exps", [P, TILES, R])
        comb = sb("comb", [P, TILES, EP])
        count = sb("count", [P, EP])
        one_hot, two_hot, late = (sb(n, [P, TILES, 16]) for n in ("one_hot", "two_hot", "late"))
        top, least, total, scale = (sb(n, [P, TILES]) for n in ("top", "least", "total", "scale"))
        pairs = [sb(f"pairs{i}", [P, TILES, 4]) for i in range(4)]
        load = sb("load", [P, EP])
        turned_comb = sb("turned_comb", [P, BLOCKS, P])
        psum = core.quad[0][:, 0:TILES * R].rearrange("p (t r) -> p t r", r=R)
        with nc.Block() as block:
            @block.sync
            def _(sp):
                sp.dma_start(w[:, :], w_router).then_inc(w_landed, 16)
                if b_router is not None:
                    sp.dma_start(b[:, :], b_router.partition_broadcast(P)).then_inc(b_landed, 16)
                sp.wait_ge(turned_copied, 1)
                rows = comb_dram.rearrange("e (b t p) -> b t e p", b=BLOCKS, p=P)
                for i in range(BLOCKS):
                    sp.dma_start(rows[i], turned_comb[:, i, :]).then_inc(stored, 16)
                sp.wait_ge(stored, 16 * BLOCKS)

            @block.gpsimd
            def _(pool):
                nc.gpsimd.iota(count[:, :], pattern=[[1, EP]], base=0, channel_multiplier=0,
                               allow_small_or_imprecise_dtypes=True).then_inc(set_up, 1)
                nc.gpsimd.memset(comb[:, :, :], 0.0).then_inc(set_up, 1)

            @block.tensor
            def _(pe):
                pe.wait_ge(w_landed, 16)
                for t in range(TILES):
                    last = nc.tensor.matmul(psum[:, t, :], src[:, t * P:(t + 1) * P], w[:, :], start=(t == 0),
                                            stop=(t == TILES - 1), skip_group_check=True)
                last.then_inc(logits_ready, 1)
                if kind == "capped":
                    pe.wait_ge(counted, 1)
                    nc.tensor.matmul(core.quad[1][:, 0:EP], core.mean_w[:, :], load[:, :], start=True, stop=True).then_inc(counts_ready, 1)
                pe.wait_ge(comb_ready, 1)
                for i in range(BLOCKS):
                    n = TILES // BLOCKS
                    last = nc.tensor.transpose(core.quad[0][:, i * P:(i + 1) * P],
                                               comb[:, i * n:(i + 1) * n, :].rearrange("p t e -> p (t e)"), core.ident[:, :])
                last.then_inc(turned, 1)

            @block.scalar
            def _(act):
                act.wait_ge(shifted, 1)
                nc.scalar.activation(exps[:, :, :], exps[:, :, :], ACT.Exp).then_inc(exps_ready, 1)

            @block.vector
            def _(dve):
                link = chained(dve, steps)
                dve.wait_ge(set_up, 2)
                dve.wait_ge(logits_ready, 1)
                if b_router is None:
                    link(nc.vector.tensor_copy(logits[:, :, :], psum))
                else:
                    dve.wait_ge(b_landed, 16)
                    link(nc.vector.tensor_tensor(logits[:, :, :], psum, over_tiles(b[:, :], R), ALU.add))
                if kind == "groups":
                    G = R - E
                    group, expert = logits[:, :, 0:G], logits[:, :, G:R]
                    first, second = (expert.rearrange("p t (g e) -> p t g e", e=2)[:, :, :, e] for e in range(2))
                    better, lesser, group_w, pair_w = (p[:, :, :] for p in pairs)
                    first_best(nc, link, one_hot[:, :, 0:G], group, count[:, 0:G], top[:, :], late[:, :, 0:G], least[:, :])
                    link(nc.vector.tensor_tensor(exps[:, :, 0:G], group, over_tiles(top[:, :], G), ALU.subtract))
                    link(nc.vector.tensor_tensor(better, first, second, ALU.max))
                    for e, v in enumerate((first, second)):
                        out = exps[:, :, G:R].rearrange("p t (g e) -> p t g e", e=2)[:, :, :, e]
                        last = nc.vector.tensor_tensor(out, v, better, ALU.subtract)
                        if e == 0:
                            link(last)
                    last.then_inc(shifted, 1)
                    dve.wait_ge(exps_ready, 1)
                    e_first, e_second = (exps[:, :, G:R].rearrange("p t (g e) -> p t g e", e=2)[:, :, :, e] for e in range(2))
                    link(nc.vector.tensor_reduce(total[:, :], exps[:, :, 0:G], AX.X, ALU.add))
                    link(nc.vector.reciprocal(scale[:, :], total[:, :]))
                    link(nc.vector.tensor_tensor(lesser, e_first, e_second, ALU.add))
                    link(nc.vector.reciprocal(pair_w, lesser))
                    link(nc.vector.tensor_tensor(group_w, one_hot[:, :, 0:G], over_tiles(scale[:, :], G), ALU.mult))
                    link(nc.vector.tensor_tensor(pair_w, pair_w, group_w, ALU.mult))
                    link(nc.vector.tensor_tensor(lesser, first, second, ALU.is_ge))
                    out = comb[:, :, :].rearrange("p t (g e) -> p t g e", e=2)
                    link(nc.vector.tensor_tensor(out[:, :, :, 0], pair_w, lesser, ALU.mult))
                    nc.vector.tensor_tensor(out[:, :, :, 1], pair_w, out[:, :, :, 0], ALU.subtract).then_inc(comb_ready, 1)
                else:
                    one, two = one_hot[:, :, 0:E], two_hot[:, :, 0:E]
                    first_best(nc, link, one, logits[:, :, :], count[:, 0:E], top[:, :], late[:, :, 0:E], least[:, :])
                    nc.vector.tensor_tensor(exps[:, :, :], logits[:, :, :], over_tiles(top[:, :], E), ALU.subtract).then_inc(shifted, 1)
                    dve.wait_ge(shifted, 1)
                    link(nc.vector.scalar_tensor_tensor(out=logits[:, :, :], in0=one, scalar=-1e30, in1=logits[:, :, :],
                                                        op0=ALU.mult, op1=ALU.add))
                    first_best(nc, link, two, logits[:, :, :], count[:, 0:E], top[:, :], late[:, :, 0:E], least[:, :])
                    link(nc.vector.tensor_tensor(one, one, two, ALU.add))
                    dve.wait_ge(exps_ready, 1)
                    link(nc.vector.tensor_reduce(total[:, :], exps[:, :, :], AX.X, ALU.add))
                    link(nc.vector.reciprocal(scale[:, :], total[:, :]))
                    link(nc.vector.tensor_tensor(exps[:, :, :], exps[:, :, :], over_tiles(scale[:, :], E), ALU.mult))
                    out = comb[:, :, 0:E]
                    if kind == "capped":
                        nc.vector.tensor_reduce(load[:, :], one.rearrange("p t e -> p e t"), AX.X, ALU.add).then_inc(counted, 1)
                        link(nc.vector.tensor_tensor(exps[:, :, :], exps[:, :, :], one, ALU.mult))
                        dve.wait_ge(counts_ready, 1)
                        link(nc.vector.tensor_scalar(late[:, 0, 0:E], core.quad[1][:, 0:E], cap / P, None, ALU.is_le))
                        nc.vector.tensor_tensor(out, exps[:, :, :], over_tiles(late[:, 0, 0:E], E), ALU.mult).then_inc(comb_ready, 1)
                    else:
                        link(nc.vector.tensor_tensor(exps[:, :, :], exps[:, :, :], one, ALU.mult))
                        link(nc.vector.tensor_reduce(total[:, :], exps[:, :, :], AX.X, ALU.add))
                        link(nc.vector.tensor_scalar(total[:, :], total[:, :], 1e-10, None, ALU.max))
                        link(nc.vector.reciprocal(scale[:, :], total[:, :]))
                        nc.vector.tensor_tensor(out, exps[:, :, :], over_tiles(scale[:, :], E), ALU.mult).then_inc(comb_ready, 1)
                dve.wait_ge(turned, 1)
                nc.vector.tensor_copy(turned_comb[:, :, :], core.quad[0][:, 0:BLOCKS * P].rearrange("p (b t) -> p b t", t=P)
                                      ).then_inc(turned_copied, 1)


def experts(core, name, src, w1, w2, b2, comb_dram, func):
    nc = core.nc
    E, FT = w1.shape[0], w2.shape[2]
    F = FT * P
    free_slots = 2
    b2_landed, w_landed, comb_landed = core.sem(f"{name}_b2_landed"), [core.sem(f"{name}_w_landed{p}") for p in range(2)], [core.sem(f"{name}_comb_landed{p}") for p in range(2)]
    hidden_ready, hidden_read, weighted, summed = (core.sem(f"{name}_{n}") for n in ("hidden_ready", "hidden_read", "weighted", "summed"))
    with ExitStack() as ctx:
        sb = lambda n, shape, dt=F32: core.sb(f"{name}_{n}", shape, dt, ctx)
        w1s = [sb(f"w1s{p}", [P, F + FT]) for p in range(2)]
        w2s = [sb(f"w2s{p}", [P, FT, D]) for p in range(2)]
        cs = [sb(f"cs{p}", [P, N]) for p in range(2)]
        b2s = sb("b2s", [E, D])
        comb = sb("comb_t", [E, N])
        hid = [[sb(f"hid{p}{h}", [P, FT, T]) for h in BOTH] for p in range(2)]
        ring = core.slot[0]
        with nc.Block() as block:
            @block.sync
            def _(sp):
                def load(e, p):
                    sp.dma_start(w1s[p][:, :], w1[e]).then_inc(w_landed[p], 16)
                    sp.dma_start(w2s[p][:, :, :], w2[e]).then_inc(w_landed[p], 16)
                    sp.dma_start(cs[p][:, :], comb_dram[e].partition_broadcast(P)).then_inc(comb_landed[p], 16)
                sp.dma_start(b2s[:, :], b2).then_inc(b2_landed, 16)
                sp.dma_start(comb[:, :], comb_dram[0:E, :]).then_inc(b2_landed, 16)
                load(0, 0)
                load(1, 1)
                with sp.Fori(0, E // 2 - 1) as i:
                    for p in range(2):
                        sp.wait_ge(summed, i * 4 + (2 * p + 2))
                        load(i * 2 + (p + 2), p)

            @block.tensor
            def _(pe):
                pe.wait_ge(b2_landed, 32)
                for h in BOTH:
                    for c in range(0, T, BANK):
                        nc.tensor.matmul(core.slot[1][h][:, c:c + BANK], b2s[:, :], comb[:, h * T + c:h * T + c + BANK],
                                         start=True, stop=False, skip_group_check=True)

                def hidden(i, p, h):
                    if h == 0:
                        pe.wait_ge(w_landed[p], i * 32 + 32)
                    for f in range(FT):
                        u = (2 * p + h) * FT + f
                        pe.wait_ge(hidden_read, i * (4 * FT) + (u - 1 + free_slots))
                        product(nc, ring[u % 2], [(w1s[p][:, f * P:(f + 1) * P], half(src, h))]).then_inc(hidden_ready, 1)

                def add_up(i, p, h):
                    pe.wait_ge(weighted, i * (4 * FT) + ((2 * p + h) * FT + FT))
                    for c in range(0, T, BANK):
                        for f in range(FT):
                            last = nc.tensor.matmul(core.slot[1][h][:, c:c + BANK], w2s[p][:, f, :], hid[p][h][:, f, c:c + BANK],
                                                    start=False, stop=False, skip_group_check=True)
                    last.then_inc(summed, 1)

                def pair(i, first):
                    for p in range(2):
                        for h in BOTH:
                            hidden(i, p, h)
                            if p or h:
                                add_up(i, (2 * p + h - 1) // 2, 1 - h)
                            elif not first:
                                add_up(i - 1, 1, 1)
                pe.sem_inc(hidden_read, free_slots)
                pair(0, True)
                with pe.Fori(1, E // 2) as i:
                    pair(i, False)
                add_up(E // 2 - 1, 1, 1)

            @block.scalar
            def _(act):
                def pair(i):
                    for p in range(2):
                        for h in BOTH:
                            if not isinstance(i, int):
                                act.wait_ge(summed, i * 4 + (2 * p + h + 1 - 4))
                            for f in range(FT):
                                act.wait_ge(hidden_ready, i * (4 * FT) + ((2 * p + h) * FT + f + 1))
                                nc.scalar.activation(hid[p][h][:, f, :], ring[((2 * p + h) * FT + f) % 2], func,
                                                     bias=w1s[p][:, F + f:F + f + 1]).then_inc(hidden_read, 1)
                pair(0)
                with act.Fori(1, E // 2) as i:
                    pair(i)

            @block.vector
            def _(dve):
                with dve.Fori(0, E // 2) as i:
                    for p in range(2):
                        dve.wait_ge(comb_landed[p], i * 16 + 16)
                        for h in BOTH:
                            for f in range(FT):
                                dve.wait_ge(hidden_read, i * (4 * FT) + ((2 * p + h) * FT + f + 1 + free_slots))
                                nc.vector.tensor_tensor(hid[p][h][:, f, :], hid[p][h][:, f, :], half(cs[p], h), ALU.mult).then_inc(weighted, 1)


def layer_0_output(core, cols, x1):
    nc = core.nc
    S = spe, sact, sdve, spool = core.begin("centre var", "square log rstd", "res scaled affine join", "")
    landed = core.sem("ln2_cols")
    with ExitStack() as ctx:
        col = core.sb("colln2", [P, 2], ctx=ctx)
        res = [core.sb(f"res2{h}", [P, T], ctx=ctx) for h in BOTH]
        with nc.Block() as block:
            @block.sync
            def _(sp):
                sp.dma_start(col[:, :], cols).then_inc(landed, 16)

            @block.tensor
            def _(pe):
                pe.wait_ge(core.dve_done[0], sdve.value("res"))
                pe.wait_ge(core.dve_done[1], sdve.value("res"))
                norm_pe(core, pe, BOTH, lambda h: res[h][:, :], (0, 1), S)

            @block.scalar
            def _(act):
                norm_act(core, act, BOTH, 1e-5, (0, 1), S)

            @block.vector
            def _(dve):
                dve.wait_ge(landed, 16)
                for h in BOTH:
                    nc.vector.tensor_tensor(res[h][:, :], core.slot[1][h], half(x1, h), ALU.add).then_inc(core.dve_done[h], 1)
                dve.wait_ge(core.dve_done[0], sdve.value("res"))
                for h in BOTH:
                    norm_dve(core, dve, h, core.cen[h], (0, 1), S)
                    dve.wait_ge(core.dve_done[h], sdve.value("scaled"))
                    nc.vector.tensor_scalar(core.cen[h], core.cen[h], col[:, 0:1], col[:, 1:2], ALU.mult, ALU.add).then_inc(core.dve_done[h], 1)
                    dve.wait_ge(core.dve_done[h], sdve.value("affine"))
                    nc.vector.tensor_tensor(half(core.x, h), half(core.x, h), core.cen[h], ALU.add).then_inc(core.dve_done[h], 1)


GH4, GK, GM = 4, 32, 64
CHUNK = 64
CH = T // CHUNK
HM = GH4 * GM


def slot_attention_masks(core, ctx, loads):
    nc = core.nc
    sb = lambda n, shape: core.sb(n, shape, F32, ctx)
    m = {
        "causal": sb("m_causal", [P, P]),
        "rel": sb("m_rel", [P, P]),
        "after": sb("m_after", [P, P]),
        "first": sb("m_first", [P, P]),
        "ends": sb("m_ends", [P, 2]),
        "heads": sb("m_heads", [P, P]),
    }
    built, landed = core.sem("masks_built"), core.sem("slot_weights_landed")
    with nc.Block() as block:
        @block.sync
        def _(sp):
            for to, w in loads:
                sp.dma_start(to, w).then_inc(landed, 16)
            sp.wait_ge(landed, 16 * len(loads))

        @block.gpsimd
        def _(pool):
            link = chained(pool, built)
            for name, v in (("causal", 1.0), ("after", 1.0), ("first", 0.0), ("ends", 1.0), ("heads", 0.0)):
                link(nc.gpsimd.memset(m[name][:, :], v))
            link(nc.gpsimd.affine_select(out=m["causal"][:, :], in_=m["causal"][:, :], compare_op=ALU.is_ge, fill=0.0,
                                         base=0, pattern=[[1, P]], channel_multiplier=-1))
            link(nc.gpsimd.affine_select(out=m["after"][:, :], in_=m["after"][:, :], compare_op=ALU.is_ge, fill=0.0,
                                         base=-1, pattern=[[-1, P]], channel_multiplier=1))
            for c in (0, CHUNK):
                link(nc.gpsimd.memset(m["first"][c:c + 32, c:c + CHUNK], 1.0))
                link(nc.gpsimd.memset(m["ends"][c + 32:c + 64, 1:2], 0.0))
            for h in range(GH4):
                link(nc.gpsimd.memset(m["heads"][32 * h:32 * h + 32, 32 * h:32 * h + 32], 1.0 / GK))
            link(nc.gpsimd.memset(m["causal"][0:CHUNK, CHUNK:P], 0.0))
            link(nc.gpsimd.memset(m["after"][CHUNK:P, 0:CHUNK], 0.0))
            link(nc.gpsimd.tensor_tensor(m["rel"][:, :], m["causal"][:, :], m["first"][:, :], ALU.subtract))
    return m


def slot_attention_half(core, half_no, wt, wq, m, out):
    nc = core.nc
    GT = KT
    name = f"g{half_no}"
    sem = lambda n: core.sem(f"{name}_{n}")
    raw_ready, raw_copied = sem("raw_ready"), sem("raw_copied")
    with ExitStack() as ctx:
        sb = lambda n, shape, dt=F32: core.sb(f"{name}_{n}", shape, dt, ctx)
        raw = sb("raw", [P, GT, 512])
        k_tok, f = raw[:, :, 0:D], raw[:, :, 2 * D:512]
        soft = sb("soft", [P, GT, HM])
        s = sb("s", [P, GT, HM])
        eg = sb("eg", [P, GT, HM])
        se = sb("se", [P, GT, HM])
        send = sb("send", [P, GT, HM])
        qt = sb("qt", [P, T])
        kt = sb("kt", [P, GH4, T])
        dS = sb("dS", [P, 2, 2, GT, 2 * GK])
        ends = sb("ends", [P, 2, 2, GT, 2])
        S = sb("S", [P, 2, CH + 1, 2 * GK])
        Skt = sb("Skt", [P, CH, HM])
        x = half(core.xn, half_no)

        qk_ready, qk_read = sem("qk_ready"), sem("qk_read")
        abs_done, exp_done, ln_done, f_done, ef_done, s_done, silu_done = (sem(n) for n in ("abs", "exp", "ln", "f", "ef", "s", "silu"))
        D_ready, D_read, eg_done, se_done = sem("D_ready"), sem("D_read"), sem("eg_done"), sem("se_done")
        cleared = sem("cleared")
        with nc.Block() as block:
            @block.gpsimd
            def _(pool):
                nc.gpsimd.memset(kt[:, :, :], 0.0).then_inc(cleared, 1)
                nc.gpsimd.memset(Skt[:, :, :], 0.0).then_inc(cleared, 1)

            @block.tensor
            def _(pe):
                for i in range(2):
                    for t in range(4):
                        tile = 4 * i + t
                        last = nc.tensor.matmul(core.quad[i][:, t * 512:(t + 1) * 512], x[:, tile * P:(tile + 1) * P], wt[:, :],
                                                start=True, stop=True)
                    last.then_inc(raw_ready, 1)
                pe.wait_ge(raw_copied, 1)
                for u in range(2):
                    product(nc, core.slot[0][u], [(wq[:, u * D:(u + 1) * D], x)]).then_inc(qk_ready, 1)
                for n, i in enumerate((1, 0)):
                    pe.wait_ge(f_done, 2)
                    if i:
                        pe.wait_ge(raw_copied, 2)
                    else:
                        pe.wait_ge(qk_read, 1 + GH4)
                    for t in range(4):
                        tile = 4 * i + t
                        nc.tensor.matmul(core.quad[i][:, t * 512:t * 512 + HM], m["rel"][:, :], f[:, tile, :],
                                         start=True, stop=True, skip_group_check=True)
                        last = nc.tensor.matmul(core.quad[i][:, t * 512 + HM:(t + 1) * 512], m["after"][:, :], f[:, tile, :],
                                                start=True, stop=True, skip_group_check=True)
                    last.then_inc(D_ready, 1)

            @block.scalar
            def _(act):
                for i in range(2):
                    act.wait_ge(raw_ready, i + 1)
                    nc.scalar.activation(raw[:, 4 * i:4 * i + 4, :], core.quad[i][:, :].rearrange("p (t x) -> p t x", x=512),
                                         ACT.Identity).then_inc(raw_copied, 1)
                act.wait_ge(raw_copied, 2)
                nc.scalar.activation(soft[:, :, :], f, ACT.Abs).then_inc(abs_done, 1)
                act.wait_ge(abs_done, 1)
                nc.scalar.activation(soft[:, :, :], soft[:, :, :], ACT.Exp, scale=-1.0).then_inc(exp_done, 1)
                act.wait_ge(exp_done, 1)
                nc.scalar.activation(soft[:, :, :], soft[:, :, :], ACT.Ln, bias=core.one[:, :]).then_inc(ln_done, 1)
                act.wait_ge(qk_ready, 1)
                nc.scalar.activation(qt[:, :], core.slot[0][0], ACT.Silu).then_inc(qk_read, 1)
                act.wait_ge(qk_ready, 2)
                act.wait_ge(cleared, 2)
                for h in range(GH4):
                    rows = slice(GK * h, GK * h + GK)
                    nc.scalar.activation(kt[rows, h, :], core.slot[0][1][rows, :], ACT.Silu).then_inc(qk_read, 1)
                nc.scalar.activation(k_tok, k_tok, ACT.Silu).then_inc(silu_done, 1)
                act.wait_ge(f_done, 2)
                nc.scalar.activation(s[:, :, :], f, ACT.Exp).then_inc(ef_done, 1)
                for n, i in enumerate((1, 0)):
                    act.wait_ge(D_ready, n + 1)
                    D4 = core.quad[i][:, :].rearrange("p (t x) -> p t x", x=512)
                    g = slice(4 * i, 4 * i + 4)
                    nc.scalar.activation(eg[:, g, :], D4[:, :, 0:HM], ACT.Exp).then_inc(eg_done, 1)
                    nc.scalar.activation(se[:, g, :], D4[:, :, 0:HM], ACT.Exp, scale=-1.0).then_inc(eg_done, 1)
                    nc.scalar.activation(send[:, g, :], D4[:, :, HM:512], ACT.Exp).then_inc(eg_done, 1)

            @block.vector
            def _(dve):
                dve.wait_ge(ln_done, 1)
                nc.vector.scalar_tensor_tensor(out=f, in0=f, scalar=0.0, in1=soft[:, :, :], op0=ALU.min, op1=ALU.subtract).then_inc(f_done, 1)
                dve.wait_ge(f_done, 1)
                nc.vector.tensor_scalar(f, f, 0.125, None, ALU.mult).then_inc(f_done, 1)
                dve.wait_ge(ef_done, 1)
                nc.vector.tensor_scalar(s[:, :, :], s[:, :, :], -1.0, 1.0, ALU.mult, ALU.add).then_inc(s_done, 1)
                dve.wait_ge(s_done, 1)
                for n, i in enumerate((1, 0)):
                    dve.wait_ge(eg_done, 3 * n + 3)
                    g = slice(4 * i, 4 * i + 4)
                    nc.vector.tensor_tensor(se[:, g, :], se[:, g, :], s[:, g, :], ALU.mult).then_inc(se_done, 1)
                    nc.vector.tensor_tensor(send[:, g, :], send[:, g, :], s[:, g, :], ALU.mult).then_inc(se_done, 1)

        add_ready, dS_copied, ends_done, S_step, S_scaled, Skt_ready, Skt_copied = (
            sem(n) for n in ("add_ready", "dS_copied", "ends_done", "S_step", "S_scaled", "Skt_ready", "Skt_copied"))
        with nc.Block() as block:
            @block.tensor
            def _(pe):
                kv = raw[:, :, 0:2 * D].rearrange("p t (a h x) -> p t a h x", a=2, h=GH4)
                for par in range(2):
                    rows = slice(CHUNK * par, CHUNK * par + CHUNK)
                    for j in range(2):
                        for t in range(GT):
                            at = j * T + par * 512 + t * 64
                            for h2 in range(2):
                                h = 2 * j + h2
                                last = nc.tensor.matmul(core.quad[0][64 * h2:64 * h2 + 64, at:at + 64],
                                                        send[rows, t, h * GM:(h + 1) * GM], kv[rows, t, :, h, :],
                                                        start=True, stop=True, skip_group_check=True)
                last.then_inc(add_ready, 1)
                for par in range(2):
                    rows = slice(CHUNK * par, CHUNK * par + CHUNK)
                    for j in range(2):
                        for t in range(GT):
                            at = par * 512 + (j * GT + t) * 2
                            last = nc.tensor.matmul(core.quad[1][:, at:at + 2], f[rows, t, j * P:(j + 1) * P], m["ends"][rows, :],
                                                    start=True, stop=True, skip_group_check=True)
                last.then_inc(add_ready, 1)
                pe.wait_ge(S_scaled, 2)
                pe.wait_ge(dS_copied, 1)
                pe.wait_ge(ends_done, 2)
                for h2 in range(2):
                    rows = slice(64 * h2, 64 * h2 + 64)
                    for c in range(CH):
                        for j in range(2):
                            h = 2 * j + h2
                            last = nc.tensor.matmul(core.quad[h2][GK * h:GK * h + GK, c * GM:(c + 1) * GM], S[rows, j, c, 0:GK],
                                                    core.ident[rows, rows], start=True, stop=True, skip_group_check=True)
                    last.then_inc(Skt_ready, 1)

            @block.scalar
            def _(act):
                act.wait_ge(add_ready, 1)
                nc.scalar.activation(dS[:, :, :, :, :].rearrange("p j a t x -> p (j a t x)"), core.quad[0][:, :], ACT.Identity).then_inc(dS_copied, 1)
                act.wait_ge(add_ready, 2)
                for par in range(2):
                    nc.scalar.activation(ends[:, par, :, :, :].rearrange("p j t e -> p (j t e)"),
                                         core.quad[1][:, par * 512:par * 512 + 4 * GT], ACT.Exp).then_inc(ends_done, 1)
                for h2 in range(2):
                    act.wait_ge(Skt_ready, h2 + 1)
                    for j in range(2):
                        h = 2 * j + h2
                        rows = slice(GK * h, GK * h + GK)
                        nc.scalar.activation(Skt[rows, :, h * GM:(h + 1) * GM], core.quad[h2][rows, 0:T].rearrange("p (c m) -> p c m", m=GM),
                                             ACT.Identity).then_inc(Skt_copied, 1)

            @block.vector
            def _(dve):
                nc.vector.memset(S[:, :, 0, :], 0.0).then_inc(S_step, 2)
                dve.wait_ge(dS_copied, 1)
                dve.wait_ge(ends_done, 2)
                for c in range(CH):
                    dve.wait_ge(S_step, 2 * c + 2)
                    for j in range(2):
                        nc.vector.scalar_tensor_tensor(out=S[:, j, c + 1, :], in0=S[:, j, c, :], scalar=ends[:, c % 2, j, c // 2, 0:1],
                                                       in1=dS[:, j, c % 2, c // 2, :], op0=ALU.mult, op1=ALU.add).then_inc(S_step, 1)
                dve.wait_ge(S_step, 2 * CH + 2)
                for j in range(2):
                    for par in range(2):
                        at = S[:, j, 0:CH, :].rearrange("p (t a) x -> p a t x", a=2)[:, par]
                        last = nc.vector.tensor_tensor(at, at, ends[:, par, j, :, 1:2].to_broadcast([P, GT, 2 * GK]), ALU.mult)
                    last.then_inc(S_scaled, 1)

        SIDE = 4
        spe, sact, sdve = (Steps(0, text, GT // SIDE) for text in (
            "A logits turned B out", "soft turned out", "A eg max sub sum recip scaled P B"))
        pe_done, act_done, dve_done = ([sem(f"{e}_side{p}") for p in range(SIDE)] for e in ("pe", "act", "dve"))
        with ExitStack() as inner:
            sb2 = lambda n, shape: core.sb(f"{name}_{n}", shape, F32, inner)
            Am = [sb2(f"Am{p}", [P, GH4, P]) for p in range(SIDE)]
            lg = [sb2(f"lg{p}", [P, GH4, GM]) for p in range(SIDE)]
            st = [sb2(f"st{p}", [P, 3, GH4]) for p in range(SIDE)]
            turned = [sb2(f"turned{p}", [P, 4, P]) for p in range(SIDE)]
            with nc.Block() as block:
                bank = [[core.slot[p // 2][p % 2][:, b * 512:(b + 1) * 512] for b in range(2)] for p in range(SIDE)]
                heads = lambda v: v.rearrange("p (h t) -> p h t", h=GH4)

                @block.tensor
                def _(pe):
                    for i in range(GT // SIDE):
                        for p in range(SIDE):
                            t = SIDE * i + p
                            if i:
                                pe.wait_ge(act_done[p], sact.value("out", i - 1))
                            for h in range(GH4):
                                last = nc.tensor.matmul(bank[p][0][:, h * P:(h + 1) * P], kt[:, h, t * P:(t + 1) * P],
                                                        qt[:, t * P:(t + 1) * P], start=True, stop=True, skip_group_check=True)
                            last.then_inc(pe_done[p], 1)
                        for p in range(SIDE):
                            t = SIDE * i + p
                            for c in range(2):
                                nc.tensor.matmul(bank[p][1][64 * c:64 * c + 64, 0:HM], qt[:, t * P + 64 * c:t * P + 64 * c + 64],
                                                 Skt[:, 2 * t + c, :], start=True, stop=False, skip_group_check=True)
                            pe.wait_ge(dve_done[p], sdve.value("A", i))
                            for h in range(GH4):
                                last = nc.tensor.matmul(bank[p][1][:, h * GM:(h + 1) * GM], Am[p][:, h, :], se[:, t, h * GM:(h + 1) * GM],
                                                        start=False, stop=True, skip_group_check=True)
                            last.then_inc(pe_done[p], 1)
                        for p in range(SIDE):
                            t = SIDE * i + p
                            for j in range(2):
                                nc.tensor.transpose(bank[p][0][:, (2 + j) * P:(3 + j) * P], se[:, t, j * P:(j + 1) * P], core.ident[:, :])
                            pe.wait_ge(dve_done[p], sdve.value("P", i))
                            for j in range(2):
                                last = nc.tensor.transpose(bank[p][0][:, j * P:(j + 1) * P],
                                                           lg[p][:, 2 * j:2 * j + 2, :].rearrange("p h m -> p (h m)"), core.ident[:, :])
                            last.then_inc(pe_done[p], 1)
                        for p in range(SIDE):
                            pe.wait_ge(act_done[p], sact.value("turned", i))
                            for h2 in range(2):
                                for j in range(2):
                                    rows = slice(64 * h2, 64 * h2 + 64)
                                    last = nc.tensor.matmul(bank[p][h2][:, j * P:(j + 1) * P], turned[p][rows, 2 + j, :],
                                                            turned[p][rows, j, :], start=True, stop=True, skip_group_check=True)
                            last.then_inc(pe_done[p], 1)
                        for p in range(SIDE):
                            t = SIDE * i + p
                            pe.wait_ge(dve_done[p], sdve.value("B", i))
                            for h in range(GH4):
                                j, h2 = h // 2, h % 2
                                o = bank[p][1][32 * h:32 * h + 32, 256:384]
                                nc.tensor.matmul(o, raw[:, t, D + h * GK:D + (h + 1) * GK], Am[p][:, h, :], start=True, stop=False, skip_group_check=True)
                                for c in range(2):
                                    last = nc.tensor.matmul(o[:, 64 * c:64 * c + 64], S[64 * h2:64 * h2 + 64, j, 2 * t + c, GK:2 * GK],
                                                            turned[p][64 * h2:64 * h2 + 64, j, 64 * c:64 * c + 64],
                                                            start=False, stop=True, skip_group_check=True)
                            last.then_inc(pe_done[p], 1)

                @block.scalar
                def _(act):
                    for i in range(GT // SIDE):
                        for p in range(SIDE):
                            act.wait_ge(dve_done[p], sdve.value("sub", i))
                            nc.scalar.activation(lg[p][:, :, :], lg[p][:, :, :], ACT.Exp, scale=float(GK) ** -0.5).then_inc(act_done[p], 1)
                        for p in range(SIDE):
                            act.wait_ge(pe_done[p], spe.value("turned", i))
                            nc.scalar.activation(turned[p][:, :, :], heads(bank[p][0]), ACT.Identity).then_inc(act_done[p], 1)
                        for p in range(SIDE):
                            t = SIDE * i + p
                            act.wait_ge(pe_done[p], spe.value("out", i))
                            nc.scalar.activation(out[:, t * P:(t + 1) * P], bank[p][1][:, 256:384], ACT.Identity).then_inc(act_done[p], 1)

                @block.vector
                def _(dve):
                    over_slots = lambda v: v.rearrange("p (h a) -> p h a", a=1).to_broadcast([P, GH4, GM])
                    causal = m["causal"][:, :].rearrange("p (a t) -> p a t", a=1)
                    for i in range(GT // SIDE):
                        for p in range(SIDE):
                            dve.wait_ge(pe_done[p], spe.value("A", i))
                            nc.vector.tensor_tensor(Am[p][:, :, :], heads(bank[p][0]), causal.to_broadcast([P, GH4, P]), ALU.mult).then_inc(dve_done[p], 1)
                        for p in range(SIDE):
                            t = SIDE * i + p
                            done = dve_done[p]
                            dve.wait_ge(pe_done[p], spe.value("logits", i))
                            nc.vector.tensor_tensor(lg[p][:, :, :], bank[p][1][:, 0:HM].rearrange("p (h m) -> p h m", h=GH4),
                                                    eg[:, t, :].rearrange("p (h m) -> p h m", h=GH4), ALU.mult).then_inc(done, 1)
                            dve.wait_ge(done, sdve.value("eg", i))
                            nc.vector.tensor_reduce(st[p][:, 0, :], lg[p][:, :, :], AX.X, ALU.max).then_inc(done, 1)
                            dve.wait_ge(done, sdve.value("max", i))
                            nc.vector.tensor_tensor(lg[p][:, :, :], lg[p][:, :, :], over_slots(st[p][:, 0, :]), ALU.subtract).then_inc(done, 1)
                        for p in range(SIDE):
                            t = SIDE * i + p
                            done = dve_done[p]
                            dve.wait_ge(act_done[p], sact.value("soft", i))
                            nc.vector.tensor_reduce(st[p][:, 1, :], lg[p][:, :, :], AX.X, ALU.add).then_inc(done, 1)
                            dve.wait_ge(done, sdve.value("sum", i))
                            nc.vector.reciprocal(st[p][:, 2, :], st[p][:, 1, :]).then_inc(done, 1)
                            dve.wait_ge(done, sdve.value("recip", i))
                            nc.vector.tensor_tensor(lg[p][:, :, :], lg[p][:, :, :], over_slots(st[p][:, 2, :]), ALU.mult).then_inc(done, 1)
                            dve.wait_ge(done, sdve.value("scaled", i))
                            nc.vector.tensor_tensor(lg[p][:, :, :], lg[p][:, :, :], eg[:, t, :].rearrange("p (h m) -> p h m", h=GH4), ALU.mult).then_inc(done, 1)
                        for p in range(SIDE):
                            dve.wait_ge(pe_done[p], spe.value("B", i))
                            for h2 in range(2):
                                last = nc.vector.tensor_tensor(
                                    Am[p][:, :, :].rearrange("p (j b) t -> p b j t", b=2)[:, h2],
                                    bank[p][h2][:, 0:2 * P].rearrange("p (j t) -> p j t", j=2),
                                    causal.to_broadcast([P, 2, P]), ALU.mult)
                            last.then_inc(dve_done[p], 1)


def slot_attention(core, a):
    nc = core.nc
    with ExitStack() as ctx:
        wt, wq = core.sb("g_wt", [P, 512], ctx=ctx), core.sb("g_wq", [P, 2 * D], ctx=ctx)
        m = slot_attention_masks(core, ctx, [(wt[:, :], a["A1_tok"]), (wq[:, :], a["A1_qk"])])
        o = [core.sb(f"slot_out{h}", [P, T], ctx=ctx) for h in BOTH]
        wo, gain = core.sb("g_wo", [P, D], ctx=ctx), core.sb("g_gain", [P, 1], ctx=ctx)
        for h in BOTH:
            slot_attention_half(core, h, wt, wq, m, o[h])
        landed = core.sem("g_wo_landed")
        S = spe, sact, sdve, spool = core.begin("mean out", "square log rstd", "scaled join", "")
        with nc.Block() as block:
            @block.sync
            def _(sp):
                sp.dma_start(wo[:, :], a["A1_wo"]).then_inc(landed, 16)
                for h in range(GH4):
                    sp.dma_start(gain[32 * h:32 * h + 32, :], a["A1_gain"]).then_inc(landed, 16)

            @block.tensor
            def _(pe):
                for h in BOTH:
                    pe.wait_ge(core.act_done[h], sact.value("square"))
                    product(nc, core.slot[h][0], [(m["heads"][:, :], core.sq[h])]).then_inc(core.pe_done[h], 1)
                pe.wait_ge(landed, 16 * (1 + GH4))
                for h in BOTH:
                    pe.wait_ge(core.dve_done[h], sdve.value("scaled"))
                    product(nc, core.slot[h][1], [(wo[:, :], core.cen[h])]).then_inc(core.pe_done[h], 1)

            @block.scalar
            def _(act):
                for h in BOTH:
                    nc.scalar.activation(core.sq[h], o[h][:, :], ACT.Square).then_inc(core.act_done[h], 1)
                for h in BOTH:
                    act.wait_ge(core.pe_done[h], spe.value("mean"))
                    nc.scalar.activation(core.sq[h], core.slot[h][0], ACT.Ln, bias=core.eps[1e-5][:, :]).then_inc(core.act_done[h], 1)
                    act.wait_ge(core.act_done[h], sact.value("log"))
                    nc.scalar.activation(core.sq[h], core.sq[h], ACT.Exp, scale=-0.5).then_inc(core.act_done[h], 1)

            @block.vector
            def _(dve):
                dve.wait_ge(landed, 16 * (1 + GH4))
                for h in BOTH:
                    dve.wait_ge(core.act_done[h], sact.value("rstd"))
                    nc.vector.scalar_tensor_tensor(out=core.cen[h], in0=o[h][:, :], scalar=gain[:, :], in1=core.sq[h],
                                                   op0=ALU.mult, op1=ALU.mult).then_inc(core.dve_done[h], 1)
                for h in BOTH:
                    dve.wait_ge(core.pe_done[h], spe.value("out"))
                    nc.vector.tensor_tensor(half(core.x, h), half(core.x, h), core.slot[h][1], ALU.add).then_inc(core.dve_done[h], 1)


NS, CONV = 16, 4
DD = 2
XR = 2 * NS + 1
C_PARTS = 3


def state_space(core, a, scratch):
    nc = core.nc
    sem = lambda n: core.sem(f"ss_{n}")
    xd_dram = scratch("xd_dram", (HALVES, XR, T))
    with ExitStack() as ctx:
        sb = lambda n, shape, ctx=ctx: core.sb(f"ss_{n}", shape, F32, ctx)
        w_in, w_x, w_dt, w_out = sb("w_in", [P, 4 * P]), sb("w_x", [P, DD, XR]), sb("w_dt", [P, DD * P]), sb("w_out", [P, DD, D])
        cols = sb("cols", [P, DD, CONV + 3])
        TAP, CB, BDT, DP = 0, CONV, CONV + 1, CONV + 2
        neg_a = sb("neg_a", [P, DD, NS])
        diag = sb("diag", [P, DD, P])
        pick = core.sb("ss_pick", [P, NS, P], BF16, ctx)
        c_parts = [core.sb(f"ss_c{h}", [P, T], BF16, ctx) for h in BOTH]
        xdbl = [sb(f"xdbl{h}", [P, T]) for h in BOTH]
        both = lambda n: [[sb(f"{n}{h}{d}", [P, T]) for d in range(DD)] for h in BOTH]
        xc, zs, dt, u = both("xc"), both("zs"), both("dt"), both("u")
        w_landed, built, xz_ready, xz_read, conv_done, silu_done, a_done, a_neg, diag_done = (sem(n) for n in (
            "w_landed", "built", "xz_ready", "xz_read", "conv_done", "silu_done", "a_done", "a_neg", "diag_done"))
        xd_ready, xd_copied, xd_stored, dt_ready, dt_lin, dt_abs, dt_exp, dt_ln, dt_done, u_done = (sem(n) for n in (
            "xd_ready", "xd_copied", "xd_stored", "dt_ready", "dt_lin", "dt_abs", "dt_exp", "dt_ln", "dt_done", "u_done"))
        every = [(h, d) for h in BOTH for d in range(DD)]
        split = sem("split")
        with ExitStack() as inner:
            left, second = sb("left", [NS, T], inner), core.sb("ss_second", [NS, T], BF16, inner)
            xpad = [[sb(f"xpad{h}{d}", [P, T + CONV - 1], inner) for d in range(DD)] for h in BOTH]
            with nc.Block() as block:
                @block.sync
                def _(sp):
                    sp.wait_ge(built, 1)
                    for t, n in ((w_in[:, :], "A2_in"), (w_x[:, :, :], "A2_x"), (w_dt[XR - 1:XR, :], "A2_dt"), (w_out[:, :, :], "A2_out"),
                                 (cols[:, :, :], "A2_cols"), (neg_a[:, :, :], "A2_A")):
                        sp.dma_start(t, a[n]).then_inc(w_landed, 16)
                    for h in BOTH:
                        sp.wait_ge(xd_copied, h + 1)
                        sp.dma_start(xd_dram[h], xdbl[h][0:XR, :]).then_inc(xd_stored, 16)
                    sp.wait_ge(xd_stored, 32)

                @block.gpsimd
                def _(pool):
                    link = chained(pool, built)
                    link(nc.gpsimd.memset(w_dt[:, :], 0.0))
                    for h in BOTH:
                        link(nc.gpsimd.memset(xdbl[h][:, :], 0.0))
                    for h in BOTH:
                        link(nc.gpsimd.memset(c_parts[h][:, :], 0.0))
                    for h, d in every:
                        link(nc.gpsimd.memset(xpad[h][d][:, 0:CONV - 1], 0.0))
                    link(nc.gpsimd.memset(pick[:, :, :], 0.0))
                    for i in range(C_PARTS):
                        link(nc.gpsimd.affine_select(out=pick[:, :, :], in_=pick[:, :, :], compare_op=ALU.not_equal, fill=1.0,
                                                     base=-32 * i, pattern=[[-1, NS], [0, P]], channel_multiplier=1))

                @block.tensor
                def _(pe):
                    pe.wait_ge(w_landed, 96)
                    n = 0
                    for i in range(4):
                        for h in BOTH:
                            if n >= 4:
                                pe.wait_ge(xz_read, n - 3)
                            product(nc, core.slot[n // 2 % 2][n % 2], [(w_in[:, i * P:(i + 1) * P], half(core.xn, h))]).then_inc(xz_ready, 1)
                            n += 1
                    for h in BOTH:
                        pe.wait_ge(xz_read, 7 + h)
                        pe.wait_ge(silu_done, 2 * h + 2)
                        product(nc, core.slot[1][h][0:XR, :], [(w_x[:, d, :], xc[h][d][:, :]) for d in range(DD)]).then_inc(xd_ready, 1)
                    pe.wait_ge(xz_read, 8)
                    for n, (h, d) in enumerate(every):
                        pe.wait_ge(xd_copied, h + 1)
                        if n >= 2:
                            pe.wait_ge(dt_lin, n - 1)
                        product(nc, core.slot[0][n % 2], [(w_dt[:, d * P:(d + 1) * P], xdbl[h][:, :])]).then_inc(dt_ready, 1)

                @block.scalar
                def _(act):
                    act.wait_ge(w_landed, 96)
                    n = 0
                    for i in range(4):
                        for h in BOTH:
                            act.wait_ge(xz_ready, n + 1)
                            slot = core.slot[n // 2 % 2][n % 2]
                            if i < DD:
                                nc.scalar.activation(xpad[h][i][:, CONV - 1:], slot, ACT.Identity).then_inc(xz_read, 1)
                            else:
                                nc.scalar.activation(zs[h][i - DD][:, :], slot, ACT.Silu).then_inc(xz_read, 1)
                            n += 1
                    for n, (h, d) in enumerate(every):
                        act.wait_ge(conv_done, CONV * n + CONV)
                        nc.scalar.activation(xc[h][d][:, :], xc[h][d][:, :], ACT.Silu).then_inc(silu_done, 1)
                    for h in BOTH:
                        act.wait_ge(xd_ready, h + 1)
                        act.wait_ge(built, 3)
                        nc.scalar.activation(xdbl[h][0:XR, :], core.slot[1][h][0:XR, :], ACT.Identity).then_inc(xd_copied, 1)
                    nc.scalar.activation(neg_a[:, :, :], neg_a[:, :, :], ACT.Exp).then_inc(a_done, 1)
                    for n, (h, d) in enumerate(every):
                        act.wait_ge(dt_ready, n + 1)
                        nc.scalar.activation(dt[h][d][:, :], core.slot[0][n % 2], ACT.Identity, bias=cols[:, d, BDT:BDT + 1]).then_inc(dt_lin, 1)
                    for n, (h, d) in enumerate(every):
                        act.wait_ge(dt_lin, n + 1)
                        nc.scalar.activation(u[h][d][:, :], dt[h][d][:, :], ACT.Abs).then_inc(dt_abs, 1)
                    for n, (h, d) in enumerate(every):
                        act.wait_ge(dt_abs, n + 1)
                        nc.scalar.activation(u[h][d][:, :], u[h][d][:, :], ACT.Exp, scale=-1.0).then_inc(dt_exp, 1)
                    for n, (h, d) in enumerate(every):
                        act.wait_ge(dt_exp, n + 1)
                        nc.scalar.activation(u[h][d][:, :], u[h][d][:, :], ACT.Ln, bias=core.one[:, :]).then_inc(dt_ln, 1)

                @block.vector
                def _(dve):
                    dve.wait_ge(w_landed, 96)
                    dve.wait_ge(built, 9)
                    for d in range(DD):
                        nc.vector.tensor_scalar(diag[:, d, :], core.ident[:, :], cols[:, d, DP:DP + 1], None, ALU.mult).then_inc(diag_done, 1)
                    for n, (h, d) in enumerate(every):
                        x = xpad[h][d]
                        dve.wait_ge(xz_read, 2 * d + h + 1)
                        nc.vector.tensor_scalar(xc[h][d][:, :], x[:, 0:T], cols[:, d, 0:1], cols[:, d, CB:CB + 1],
                                                ALU.mult, ALU.add).then_inc(conv_done, 1)
                        for k in range(1, CONV):
                            dve.wait_ge(conv_done, CONV * n + k)
                            nc.vector.scalar_tensor_tensor(out=xc[h][d][:, :], in0=x[:, k:k + T], scalar=cols[:, d, k:k + 1],
                                                           in1=xc[h][d][:, :], op0=ALU.mult, op1=ALU.add).then_inc(conv_done, 1)
                    dve.wait_ge(a_done, 1)
                    nc.vector.tensor_scalar(neg_a[:, :, :], neg_a[:, :, :], -1.0, None, ALU.mult).then_inc(a_neg, 1)
                    link = chained(dve, split)
                    for h in BOTH:
                        dve.wait_ge(xd_copied, h + 1)
                        link(nc.vector.tensor_copy(c_parts[h][0:NS, :], xdbl[h][0:NS, :]))
                        link(nc.vector.tensor_tensor(left[:, :], xdbl[h][0:NS, :], c_parts[h][0:NS, :], ALU.subtract))
                        link(nc.vector.tensor_copy(second[:, :], left[:, :]))
                        link(nc.vector.tensor_copy(c_parts[h][32:32 + NS, :], second[:, :]))
                        link(nc.vector.tensor_tensor(left[:, :], left[:, :], second[:, :], ALU.subtract))
                        link(nc.vector.tensor_copy(c_parts[h][64:64 + NS, :], left[:, :]))
                    for n, (h, d) in enumerate(every):
                        dve.wait_ge(dt_ln, n + 1)
                        nc.vector.scalar_tensor_tensor(out=dt[h][d][:, :], in0=dt[h][d][:, :], scalar=0.0, in1=u[h][d][:, :],
                                                       op0=ALU.max, op1=ALU.add).then_inc(dt_done, 1)
                        dve.wait_ge(dt_done, n + 1)
                        dve.wait_ge(silu_done, n + 1)
                        nc.vector.tensor_tensor(u[h][d][:, :], dt[h][d][:, :], xc[h][d][:, :], ALU.mult).then_inc(u_done, 1)

        RING = 4
        b_landed = [sem(f"b_landed{i}") for i in range(2)]
        da_ready, dbx_ready, scanned, c_ready, hc_ready, summed, y_gated, o_ready, joined = (sem(n) for n in (
            "da_ready", "dbx_ready", "scanned", "c_ready", "hc_ready", "summed", "y_gated", "o_ready", "joined"))
        turns = [(h, s, d) for h in BOTH for s in range(NS) for d in range(DD)]
        with ExitStack() as inner:
            bs = [sb(f"bs{i}", [P, T], inner) for i in range(2)]
            da = [sb(f"da{i}", [P, T], inner) for i in range(RING)]
            st = [sb(f"st{i}", [P, T], inner) for i in range(RING)]
            with nc.Block() as block:
                @block.sync
                def _(sp):
                    for n in range(HALVES * NS):
                        h, s = n // NS, n % NS
                        if n >= 2:
                            sp.wait_ge(dbx_ready, DD * (n - 1))
                        sp.dma_start(bs[n % 2][:, :], xd_dram[h, NS + s].partition_broadcast(P)).then_inc(b_landed[n % 2], 16)

                @block.scalar
                def _(act):
                    for n, (h, s, d) in enumerate(turns):
                        if n >= RING:
                            act.wait_ge(scanned, n - RING + 1)
                        nc.scalar.activation(da[n % RING][:, :], dt[h][d][:, :], ACT.Exp, scale=neg_a[:, d, s:s + 1]).then_inc(da_ready, 1)

                @block.gpsimd
                def _(pool):
                    for n, (h, s, d) in enumerate(turns):
                        pool.wait_ge(b_landed[n // DD % 2], 16 * (n // DD // 2 + 1))
                        if n >= RING:
                            pool.wait_ge(summed, n - RING + 1)
                        nc.gpsimd.tensor_tensor(st[n % RING][:, :], u[h][d][:, :], bs[n // DD % 2][:, :], ALU.mult).then_inc(dbx_ready, 1)

                @block.vector
                def _(dve):
                    def times_c(n):
                        h, s, d = turns[n]
                        dve.wait_ge(c_ready, n // DD + 1)
                        dve.wait_ge(scanned, n + 1)
                        nc.vector.tensor_tensor(st[n % RING][:, :], st[n % RING][:, :], core.slot[0][s % 2], ALU.mult).then_inc(hc_ready, 1)

                    def gate(h):
                        dve.wait_ge(summed, DD * NS * (h + 1))
                        for d in range(DD):
                            nc.vector.tensor_tensor(zs[h][d][:, :], zs[h][d][:, :], core.slot[1][d], ALU.mult).then_inc(y_gated, 1)

                    for n, (h, s, d) in enumerate(turns):
                        dve.wait_ge(da_ready, n + 1)
                        dve.wait_ge(dbx_ready, n + 1)
                        i = n % RING
                        nc.vector.tensor_tensor_scan(out=st[i][:, :], data0=da[i][:, :], data1=st[i][:, :], initial=0.0,
                                                     op0=ALU.mult, op1=ALU.add).then_inc(scanned, 1)
                        if n and n % (DD * NS):
                            times_c(n - 1)
                        if n % (DD * NS) == DD * NS - 1:
                            times_c(n)
                            gate(h)
                    for h in BOTH:
                        dve.wait_ge(o_ready, h + 1)
                        nc.vector.tensor_tensor(half(core.x, h), half(core.x, h), core.slot[0][h], ALU.add).then_inc(joined, 1)

                def add_state(pe, n):
                    h, s, d = turns[n]
                    pe.wait_ge(hc_ready, n + 1)
                    for c in range(0, T, BANK):
                        last = nc.tensor.matmul(core.slot[1][d][:, c:c + BANK], core.ident[:, :], st[n % RING][:, c:c + BANK],
                                                start=False, stop=(s == NS - 1), skip_group_check=True)
                    last.then_inc(summed, 1)

                @block.tensor
                def _(pe):
                    for n, (h, s, d) in enumerate(turns):
                        if s == 0 and d == 0:
                            if h:
                                pe.wait_ge(y_gated, DD)
                            for e in range(DD):
                                for c in range(0, T, BANK):
                                    nc.tensor.matmul(core.slot[1][e][:, c:c + BANK], diag[:, e, :], xc[h][e][:, c:c + BANK],
                                                     start=True, stop=False, skip_group_check=True)
                        if d == 0:
                            if n >= 2 * DD:
                                pe.wait_ge(hc_ready, n - DD)
                            product(nc, core.slot[0][s % 2], [(pick[:, s, :], c_parts[h])]).then_inc(c_ready, 1)
                        if n and n % (DD * NS):
                            add_state(pe, n - 1)
                        if n % (DD * NS) == DD * NS - 1:
                            add_state(pe, n)
                    for h in BOTH:
                        pe.wait_ge(y_gated, DD * (h + 1))
                        pe.wait_ge(hc_ready, len(turns))
                        product(nc, core.slot[0][h], [(w_out[:, d, :], zs[h][d][:, :]) for d in range(DD)]).then_inc(o_ready, 1)


def causal_attention(core, w_qkvo, cols, beside):
    nc = core.nc
    QT = T // P
    scale = float(D) ** -0.5
    S = spe, sact, sdve, spool = core.begin("q k v | scores turned mixed | out", "q k v | exp turned mixed |",
                                            "| max neg recip norm | join", "", QT)
    landed, built = core.sem("ca_landed"), core.sem("ca_built")
    with ExitStack() as ctx:
        sb = lambda n, shape: core.sb(f"ca_{n}", shape, F32, ctx)
        w, col = sb("w", [P, 4 * D]), sb("col", [P, 4])
        hide = sb("hide", [P, P])
        q, k, p, pt, mixed = ([sb(f"{n}{h}", [P, T]) for h in BOTH] for n in ("q", "k", "p", "pt", "mixed"))
        v = [sb(f"v{h}", [P, QT, D]) for h in BOTH]
        st = [sb(f"st{h}", [P, 4]) for h in BOTH]
        proj = {"q": 0, "k": 1}
        with nc.Block() as block:
            @block.sync
            def _(sp):
                sp.dma_start(w[:, :], w_qkvo).then_inc(landed, 16)
                sp.dma_start(col[:, :], cols).then_inc(landed, 16)

            @block.gpsimd
            def _(pool):
                link = chained(pool, built)
                link(nc.gpsimd.memset(hide[:, :], 0.0))
                link(nc.gpsimd.affine_select(out=hide[:, :], in_=hide[:, :], compare_op=ALU.is_ge, fill=-1e30,
                                             base=0, pattern=[[-1, P]], channel_multiplier=1))

            @block.tensor
            def _(pe):
                pe.wait_ge(landed, 32)
                for h in BOTH:
                    x = half(core.xn, h)
                    product(nc, core.slot[h][0], [(w[:, 0:D], x)]).then_inc(core.pe_done[h], 1)
                    product(nc, core.slot[h][1], [(w[:, D:2 * D], x)]).then_inc(core.pe_done[h], 1)
                for h in BOTH:
                    pe.wait_ge(core.act_done[h], sact.value("q"))
                    for t in range(QT):
                        last = nc.tensor.matmul(core.slot[h][0][:, t * D:(t + 1) * D], half(core.xn, h)[:, t * P:(t + 1) * P],
                                                w[:, 2 * D:3 * D], start=True, stop=True, skip_group_check=True)
                    last.then_inc(core.pe_done[h], 1)
                pe.wait_ge(built, 2)
                for t in range(QT):
                    tile = slice(t * P, (t + 1) * P)
                    for h in BOTH:
                        pe.wait_ge(core.act_done[h], sact.value("mixed", t - 1) if t else sact.value("v"))
                        for c in range(0, (t + 1) * P, BANK):
                            end = min(c + BANK, (t + 1) * P)
                            own = end == (t + 1) * P
                            last = nc.tensor.matmul(core.slot[h][0][:, c:end], q[h][:, tile], k[h][:, c:end],
                                                    start=True, stop=not own, skip_group_check=True)
                        last = nc.tensor.matmul(core.slot[h][0][:, tile], core.ident[:, :], hide[:, :],
                                                start=False, stop=True, skip_group_check=True)
                        last.then_inc(core.pe_done[h], 1)
                    for h in BOTH:
                        pe.wait_ge(core.dve_done[h], sdve.value("norm", t))
                        for j in range(t + 1):
                            last = nc.tensor.transpose(core.slot[h][1][:, j * P:(j + 1) * P], p[h][:, j * P:(j + 1) * P], core.ident[:, :])
                        last.then_inc(core.pe_done[h], 1)
                    for h in BOTH:
                        pe.wait_ge(core.act_done[h], sact.value("turned", t))
                        for j in range(t + 1):
                            last = nc.tensor.matmul(core.slot[h][0][:, 0:P], v[h][:, j, :], pt[h][:, j * P:(j + 1) * P],
                                                    start=(j == 0), stop=(j == t), skip_group_check=True)
                        last.then_inc(core.pe_done[h], 1)
                for h in BOTH:
                    pe.wait_ge(core.act_done[h], sact.value("mixed", QT - 1))
                    product(nc, core.slot[h][1], [(w[:, 3 * D:4 * D], mixed[h][:, :])]).then_inc(core.pe_done[h], 1)

            @block.scalar
            def _(act):
                act.wait_ge(landed, 32)
                for h in BOTH:
                    for n, dst in (("q", q[h]), ("k", k[h])):
                        i = proj[n]
                        act.wait_ge(core.pe_done[h], spe.value(n))
                        nc.scalar.activation(dst[:, :], core.slot[h][i], ACT.Identity, bias=col[:, i:i + 1]).then_inc(core.act_done[h], 1)
                for h in BOTH:
                    act.wait_ge(core.pe_done[h], spe.value("v"))
                    nc.scalar.activation(v[h][:, :, :].rearrange("p t d -> p (t d)"), core.slot[h][0], ACT.Identity).then_inc(core.act_done[h], 1)
                for t in range(QT):
                    keys = slice(0, (t + 1) * P)
                    for h in BOTH:
                        act.wait_ge(core.dve_done[h], sdve.value("neg", t))
                        nc.scalar.activation(p[h][:, keys], core.slot[h][0][:, keys], ACT.Exp, bias=st[h][:, 1:2], scale=scale,
                                             accum_out=st[h][:, 2:3]).then_inc(core.act_done[h], 1)
                    for h in BOTH:
                        act.wait_ge(core.pe_done[h], spe.value("turned", t))
                        nc.scalar.activation(pt[h][:, keys], core.slot[h][1][:, keys], ACT.Identity).then_inc(core.act_done[h], 1)
                    for h in BOTH:
                        act.wait_ge(core.pe_done[h], spe.value("mixed", t))
                        nc.scalar.activation(mixed[h][:, t * P:(t + 1) * P], core.slot[h][0][:, 0:P], ACT.Identity,
                                             bias=col[:, 2:3]).then_inc(core.act_done[h], 1)

            @block.vector
            def _(dve):
                for t in range(QT):
                    keys = slice(0, (t + 1) * P)
                    for h in BOTH:
                        done = core.dve_done[h]
                        dve.wait_ge(core.pe_done[h], spe.value("scores", t))
                        nc.vector.tensor_reduce(st[h][:, 0:1], core.slot[h][0][:, keys], AX.X, ALU.max).then_inc(done, 1)
                        dve.wait_ge(done, sdve.value("max", t))
                        nc.vector.tensor_scalar(st[h][:, 1:2], st[h][:, 0:1], -scale, None, ALU.mult).then_inc(done, 1)
                    for h in BOTH:
                        done = core.dve_done[h]
                        dve.wait_ge(core.act_done[h], sact.value("exp", t))
                        nc.vector.reciprocal(st[h][:, 3:4], st[h][:, 2:3]).then_inc(done, 1)
                        dve.wait_ge(done, sdve.value("recip", t))
                        nc.vector.tensor_scalar(p[h][:, keys], p[h][:, keys], st[h][:, 3:4], None, ALU.mult).then_inc(done, 1)
                    beside(dve, t)
                dve.wait_ge(landed, 32)
                for h in BOTH:
                    dve.wait_ge(core.pe_done[h], spe.value("out"))
                    nc.vector.scalar_tensor_tensor(out=half(core.x, h), in0=core.slot[h][1], scalar=col[:, 3:4], in1=half(core.x, h),
                                                   op0=ALU.add, op1=ALU.add).then_inc(core.dve_done[h], 1)


FB = 16
FI = 352
FT = T // P
FCH = [(c, min(P, FI - c)) for c in range(0, FI, P)]


FP4_SCALE_STEPS = 4


def fp4_scales(core, link, jobs):
    nc = core.nc
    for v, r, sign, stat in jobs:
        scale, inv = stat[:, 0, :], stat[:, 1, :]
        link(nc.vector.tensor_reduce(scale, blocks(r), AX.X, ALU.max))
        link(nc.vector.tensor_scalar(scale, scale, 1.0 / 6.0, 1e-12, ALU.mult, ALU.max))
        link(nc.vector.reciprocal(inv, scale))
        link(nc.vector.tensor_tensor(blocks(r), blocks(r), over_blocks(inv), ALU.mult))


FP4_STEPS = 10


def fp4_values(core, link, job, spare):
    v, r, sign, stat = job
    u, w = (b[:, 0:v.shape[-1]] for b in spare)
    link(core.nc.vector.tensor_scalar(u, r, 0.25, None, ALU.is_gt))
    for mid in (0.75, 1.25, 1.75):
        link(core.nc.vector.scalar_tensor_tensor(out=u, in0=r, scalar=mid, in1=u, op0=ALU.is_gt, op1=ALU.add))
    link(core.nc.vector.tensor_scalar(w, r, 5.0, 2.0, ALU.is_gt, ALU.mult))
    for mid in (2.5, 3.5):
        link(core.nc.vector.scalar_tensor_tensor(out=w, in0=r, scalar=mid, in1=w, op0=ALU.is_gt, op1=ALU.add))
    link(core.nc.vector.scalar_tensor_tensor(out=u, in0=u, scalar=0.5, in1=w, op0=ALU.mult, op1=ALU.add))
    link(core.nc.vector.tensor_tensor(u, u, sign, ALU.mult))
    link(core.nc.vector.tensor_tensor(blocks(v), blocks(u), over_blocks(stat[:, 0, :]), ALU.mult))


def blocks(v):
    return v.rearrange("p (b e) -> p b e", e=FB)


def over_blocks(s):
    return s.rearrange("p (b e) -> p b e", e=1).to_broadcast([P, s.shape[-1], FB])


def fp4_net(core, w_gate, w_up, w_down, attention_beside):
    nc = core.nc
    name = "fp"
    sem = lambda n: core.sem(f"fp_{n}")
    WN = 2 * len(FCH) * P + FI
    HN = FT * FI // 2
    with ExitStack() as ctx:
        sb = lambda n, shape, ctx=ctx: core.sb(f"fp_{n}", shape, F32, ctx)
        IN = N + WN
        bufs = [sb(f"buf{i}", [P, max(IN, 2 * HN)]) for i in range(6)]
        part = lambda i: bufs[i // 2][:, i % 2 * HN:(i % 2 + 1) * HN]
        stats = [sb(f"stats{i}", [P, 2, HN // FB]) for i in range(4)]
        in_stats = sb("in_stats", [P, 2, IN // FB])
        gu_t = [sb(f"w{n}_t", [P, FI]) for n in ("gate", "up")]
        down_t = sb("wdown_t", [P, len(FCH), D])

        def job(values, first, j):
            n = values.shape[-1]
            return values, part(first + 2 * j)[:, 0:n], part(first + 2 * j + 1)[:, 0:n], stats[j][:, :, 0:n // FB]

        landed, zeroed, turned, copied = sem("landed"), sem("zeroed"), sem("turned"), sem("copied")
        with ExitStack() as inner:
            raw = bufs[0][:, N:IN]
            x_tok = [half(bufs[0], h) for h in BOTH]
            SLICE = -(-IN // FB // FT) * FB

            def inputs(c, n):
                return (*(bufs[i][:, c:c + n] for i in range(3)), in_stats[:, :, c // FB:(c + n) // FB])
            thirds = [inputs(0, T), inputs(T, T), inputs(N, WN)]
            abs_done, signs_done, scaled, rounded = (sem(n) for n in ("in_abs", "in_sign", "in_scaled", "in_rounded"))
            with nc.Block() as block:
                @block.gpsimd
                def _(pool):
                    for i in range(2):
                        at = (i * len(FCH) + 2) * P
                        nc.gpsimd.memset(raw[FCH[2][1]:, at:at + P], 0.0).then_inc(zeroed, 1)
                    pool.wait_ge(zeroed, 2)

                @block.sync
                def _(sp):
                    for i, w in enumerate((w_gate, w_up)):
                        for n, (c, size) in enumerate(FCH):
                            at = (i * len(FCH) + n) * P
                            sp.dma_start(raw[0:size, at:at + P], w[c:c + size, :]).then_inc(landed, 16)
                    sp.dma_start(raw[:, 2 * len(FCH) * P:], w_down).then_inc(landed, 16)
                    sp.wait_ge(landed, 16 * (2 * len(FCH) + 1))

                @block.tensor
                def _(pe):
                    for h in BOTH:
                        for t in range(FT):
                            last = nc.tensor.transpose(core.slot[h][0][:, t * P:(t + 1) * P], half(core.xn, h)[:, t * P:(t + 1) * P], core.ident[:, :])
                        last.then_inc(turned, 1)

                @block.scalar
                def _(act):
                    for h in BOTH:
                        act.wait_ge(turned, h + 1)
                        nc.scalar.activation(x_tok[h], core.slot[h][0], ACT.Identity).then_inc(copied, 1)
                    for j, (v, r, sign, stat) in enumerate(thirds):
                        if j < 2:
                            act.wait_ge(copied, j + 1)
                        else:
                            act.wait_ge(landed, 16 * (2 * len(FCH) + 1))
                            act.wait_ge(zeroed, 2)
                        nc.scalar.activation(r, v, ACT.Abs).then_inc(abs_done, 1)
                        nc.scalar.activation(sign, v, ACT.Sign).then_inc(signs_done, 1)

                @block.vector
                def _(dve):
                    link = chained(dve, scaled)
                    for j, third in enumerate(thirds):
                        dve.wait_ge(abs_done, j + 1)
                        fp4_scales(core, link, [third])

            def round_inputs(dve, n):
                c = n * SLICE
                fp4_values(core, chained(dve, rounded, n * FP4_STEPS), inputs(c, min(SLICE, IN - c)), bufs[3:5])

            attention_beside(round_inputs)

            w_turned, w_copied, gu_ready, silu_done, h_done = (sem(n) for n in ("w_turned", "w_copied", "gu_ready", "silu", "h_done"))
            xq = bufs[5][:, 0:N]
            hidden = [sb(f"hidden{h}", [P, FT, FI]) for h in BOTH]
            gate = [sb(f"gate{i}", [P, 2, FI]) for i in range(2)]
            turned_h = [sb(f"turned_h{h}", [P, len(FCH), T]) for h in BOTH]
            group = [hidden[j // 2][:, j % 2 * FT // 2:(j % 2 + 1) * FT // 2, :].rearrange("p t e -> p (t e)") for j in range(4)]
            hids = [job(v, 0, j) for j, v in enumerate(group)]
            abs_done, signs_done, rounded = (sem(n) for n in ("h_abs", "h_sign", "h_rounded"))
            h_turned, h_copied, o_ready, joined = (sem(n) for n in ("h_turned", "h_copied", "o_ready", "joined"))
            units = [(h, n) for h in BOTH for n in range(len(FCH))]
            JOB_STEPS = FP4_STEPS + FP4_SCALE_STEPS
            with nc.Block() as block:
                @block.tensor
                def _(pe):
                    for i in range(2):
                        for n, (c, size) in enumerate(FCH):
                            at = (i * len(FCH) + n) * P
                            last = nc.tensor.transpose(core.slot[0][0][:, i * BANK + c:i * BANK + c + size], raw[0:size, at:at + P], core.ident[0:size, 0:size])
                    last.then_inc(w_turned, 1)
                    for n, (c, size) in enumerate(FCH):
                        at = 2 * len(FCH) * P + c
                        last = nc.tensor.transpose(core.slot[0][1][0:size, n * P:(n + 1) * P], raw[:, at:at + size], core.ident[:, :])
                    last.then_inc(w_turned, 1)
                    for h in BOTH:
                        for t in range(FT):
                            last = nc.tensor.transpose(core.slot[1][h][:, t * P:(t + 1) * P], x_tok[h][:, t * P:(t + 1) * P], core.ident[:, :])
                        last.then_inc(w_turned, 1)
                    pe.wait_ge(w_copied, 5 + len(FCH) - 1)
                    for u in range(HALVES * FT // 2):
                        if u >= 2:
                            pe.wait_ge(h_done, u - 1)
                        for t in range(2):
                            at = (2 * u + t) * P
                            for i in range(2):
                                last = nc.tensor.matmul(core.slot[u % 2][i][:, t * BANK:t * BANK + FI], xq[:, at:at + P], gu_t[i][:, :], start=True, stop=True)
                        last.then_inc(gu_ready, 1)
                    pe.wait_ge(h_done, HALVES * FT // 2)
                    for h in BOTH:
                        pe.wait_ge(rounded, JOB_STEPS * 2 * (h + 1))
                        for n, (c, size) in enumerate(FCH):
                            i = h * len(FCH) + n
                            if i >= 2:
                                pe.wait_ge(h_copied, i - 1)
                            for t in range(FT):
                                last = nc.tensor.transpose(core.slot[0][i % 2][0:size, t * P:(t + 1) * P], hidden[h][:, t, c:c + size], core.ident[:, :])
                            last.then_inc(h_turned, 1)
                        pe.wait_ge(h_copied, len(FCH) * (h + 1))
                        product(nc, core.slot[1][h], [(down_t[0:size, n, :], turned_h[h][0:size, n, :]) for n, (c, size) in enumerate(FCH)]
                                ).then_inc(o_ready, 1)

                @block.scalar
                def _(act):
                    act.wait_ge(w_turned, 1)
                    for i in range(2):
                        nc.scalar.activation(gu_t[i][:, :], core.slot[0][0][:, i * BANK:i * BANK + FI], ACT.Identity).then_inc(w_copied, 1)
                    act.wait_ge(w_turned, 2)
                    for n, (c, size) in enumerate(FCH):
                        nc.scalar.activation(down_t[0:size, n, :], core.slot[0][1][0:size, n * P:(n + 1) * P], ACT.Identity).then_inc(w_copied, 1)
                    for h in BOTH:
                        act.wait_ge(w_turned, 3 + h)
                        nc.scalar.activation(half(xq, h), core.slot[1][h], ACT.Identity).then_inc(w_copied, 1)
                    for u in range(HALVES * FT // 2):
                        act.wait_ge(gu_ready, u + 1)
                        if u >= 2:
                            act.wait_ge(h_done, u - 1)
                        nc.scalar.activation(gate[u % 2][:, :, :], core.slot[u % 2][0].rearrange("p (t e) -> p t e", t=2)[:, :, 0:FI], ACT.Silu).then_inc(silu_done, 1)
                        if u % 2:
                            v, r, sign, stat = hids[u // 2]
                            act.wait_ge(h_done, u + 1)
                            nc.scalar.activation(r, v, ACT.Abs).then_inc(abs_done, 1)
                            nc.scalar.activation(sign, v, ACT.Sign).then_inc(signs_done, 1)
                    for i, (h, n) in enumerate(units):
                        size = FCH[n][1]
                        act.wait_ge(h_turned, i + 1)
                        nc.scalar.activation(turned_h[h][0:size, n, :], core.slot[0][i % 2][0:size, :], ACT.Identity).then_inc(h_copied, 1)

                @block.vector
                def _(dve):
                    link = chained(dve, rounded)
                    for u in range(HALVES * FT // 2):
                        h, t = divmod(2 * u, FT)
                        dve.wait_ge(silu_done, u + 1)
                        nc.vector.tensor_tensor(hidden[h][:, t:t + 2, :], gate[u % 2][:, :, :],
                                                core.slot[u % 2][1].rearrange("p (t e) -> p t e", t=2)[:, :, 0:FI],
                                                ALU.mult).then_inc(h_done, 1)
                        if u % 2:
                            j = u // 2
                            dve.wait_ge(abs_done, j + 1)
                            fp4_scales(core, link, hids[j:j + 1])
                            dve.wait_ge(signs_done, j + 1)
                            fp4_values(core, link, hids[j], (part(8), part(9)))
                    for h in BOTH:
                        dve.wait_ge(o_ready, h + 1)
                        nc.vector.tensor_tensor(half(core.x, h), half(core.x, h), core.slot[1][h], ALU.add).then_inc(joined, 1)


def linear_branch_of_layer_0(core, a, scratch):
    with core.own_semaphores():
        linear_blocks(core, a["L0_att"], a["L0_f1"], a["L0_f2"], a["L0_cols"])


def routed_branch_of_layer_0(core, a, scratch):
    q_dram = scratch("q_dram", (HALVES, GROUPS, GH, ROWS, T), BF16)
    k_dram = scratch("k_dram", (HALVES, GROUPS, GH, ROWS, T), BF16)
    v_dram = scratch("v_dram", (HALVES, GROUPS, P, KT, GH * HD))
    with ExitStack() as ctx:
        x1 = core.sb("x1", [P, N], ctx=ctx)
        with ExitStack() as inner:
            stacks = attention_stacks(core, inner)
            attention_inputs(core, a["F0_qk"], a["F0_v"], a["F0_qk_cols"], a["F0_v_bias"], q_dram, k_dram, v_dram, stacks)
            mixed = [core.sb(f"mixed{h}", [P, GROUPS, T], ctx=inner) for h in BOTH]
            attention(core, q_dram, k_dram, v_dram, *stacks, mixed)
            attention_output(core, a["F0_out"], a["F0_out_cols"], mixed, x1)
        comb = scratch("comb0", (8, N))
        route(core, "r0", x1, a["F0_router"], a["F0_router_b"], "groups", 8, comb)
        experts(core, "e0", x1, a["F0_w1"], a["F0_w2"], a["F0_b2"], comb, ACT.Relu)
        layer_0_output(core, a["F0_ln2"], x1)


def add_experts(core, name, clip=None):
    nc = core.nc
    joined = core.sem(f"{name}_joined")
    with nc.Block() as block:
        @block.vector
        def _(dve):
            link = chained(dve, joined)
            for h in BOTH:
                if clip is None:
                    link(nc.vector.tensor_tensor(half(core.x, h), half(core.x, h), core.slot[1][h], ALU.add))
                else:
                    link(nc.vector.tensor_tensor(core.cen[h], half(core.xn, h), core.slot[1][h], ALU.add))
                    link(nc.vector.tensor_scalar(core.cen[h], core.cen[h], clip, -clip, ALU.min, ALU.max))
                    link(nc.vector.tensor_tensor(half(core.x, h), half(core.x, h), core.cen[h], ALU.add))


def layer_1_experts(core, a, scratch):
    comb = scratch("comb1", (8, N))
    choices_cap = int(1.25 * N / 8)
    route(core, "r1", core.xn, a["F1_router"], None, "capped", 8, comb, choices_cap)
    experts(core, "e1", core.xn, a["F1_w1"], a["F1_w2"], a["F1_b2"], comb, ACT.Relu)
    add_experts(core, "e1")


def layer_2_experts(core, a, scratch):
    comb = scratch("comb2", (16, N))
    route(core, "r2", core.xn, a["F2_router"], None, "pair", 14, comb)
    experts(core, "e2", core.xn, a["F2_w1"], a["F2_w2"], a["F2_b2"], comb, ACT.Gelu)
    add_experts(core, "e2", clip=100.0)


def program(nc, a, out, scratch):
    with ExitStack() as ctx:
        core = Core(nc, ctx)
        start(core, a["x"])
        linear_branch_of_layer_0(core, a, scratch)
        routed_branch_of_layer_0(core, a, scratch)
        residual_norm(core)
        with core.own_semaphores():
            slot_attention(core, a)
        layer_1_experts(core, a, scratch)
        residual_norm(core)
        with core.own_semaphores():
            state_space(core, a, scratch)
        layer_2_experts(core, a, scratch)
        residual_norm(core)
        fp4_net(core, a["F3_gate"], a["F3_up"], a["F3_down"],
                lambda beside: causal_attention(core, a["A3_w"], a["A3_cols"], beside))
        finish(core, out)


def finish(core, out):
    nc = core.nc
    stored = core.sem("stored")
    with nc.Block() as block:
        @block.sync
        def _(sp):
            sp.dma_start(out, core.x[:, :]).then_inc(stored, 16)
            sp.wait_ge(stored, 16)


def columns(np, v):
    v = np.asarray(v)
    v = v.reshape(*v.shape[:-1], v.shape[-1] // P, P)
    return np.ascontiguousarray(np.moveaxis(v, -1, 0))


def kernel(**inputs):
    import numpy as np
    import concourse.bacc as bacc
    from concourse.bass_utils import run_bass_kernel_spmd as run

    g = {n: np.asarray(v) for n, v in inputs.items()}
    lay = lambda v: np.ascontiguousarray(v)
    of = lambda prefix: lambda n: g[prefix + n]
    L0, F0, A1, F1, A2, F2, A3, F3 = (of(f"L{i}_{b}_") for i in range(4) for b in ("attn", "ffn"))
    B = L0("Wq").shape[0]
    w, b = F0("in_proj_w"), F0("in_proj_b")

    def expert_w1(w, b):
        b = b.reshape(b.shape[0], -1, P).transpose(0, 2, 1)
        return lay(np.concatenate([w, b], axis=2))

    def expert_w2(w):
        return lay(w.reshape(w.shape[0], -1, P, D).transpose(0, 2, 1, 3))

    a = {
        "x": lay(g["L0_attn_x"].reshape(N, D).T),
        "L0_att": lay(np.concatenate([L0("Wq"), L0("Wk"), L0("Wv"), L0("Wo")], axis=2)),
        "L0_f1": lay(L0("Wf1")),
        "L0_f2": expert_w2(L0("Wf2")),
        "L0_cols": lay(np.concatenate([columns(np, L0(n)) for n in
                                       ("bq", "bk", "bv", "bo", "ln1_s", "ln1_b", "ln2_s", "ln2_b", "bf2", "bf1")], axis=2)),
        "F0_qk": lay(w[:2 * D].T),
        "F0_v": lay(w[2 * D:].T),
        "F0_qk_cols": columns(np, b[:2 * D]),
        "F0_v_bias": lay(b[2 * D:]),
        "F0_out": lay(F0("out_proj_w").T.reshape(GROUPS, GH, HD, D).transpose(1, 2, 0, 3)),
        "F0_out_cols": lay(np.stack([F0("out_proj_b"), F0("ln1_g"), F0("ln1_b")], axis=1)),
        "F0_router": lay(np.concatenate([F0("w_group"), F0("w_expert").transpose(1, 0, 2).reshape(D, -1)], axis=1)),
        "F0_router_b": lay(np.concatenate([F0("b_group"), F0("b_expert").reshape(-1)])),
        "F0_w1": expert_w1(F0("w1"), F0("b1")), "F0_w2": expert_w2(F0("w2")), "F0_b2": lay(F0("b2")),
        "F0_ln2": lay(np.stack([F0("ln2_g"), F0("ln2_b")], axis=1)),
        "A1_tok": lay(np.concatenate([A1("Wk"), A1("Wv"), A1("Wf")], axis=1)),
        "A1_qk": lay(np.concatenate([A1("Wq"), A1("Wk")], axis=1)),
        "A1_gain": lay(A1("g_norm_w").reshape(-1, 1)),
        "A1_wo": lay(A1("Wo")),
        "F1_router": lay(F1("gate_w").T),
        "F1_w1": expert_w1(F1("W1"), F1("b1")), "F1_w2": expert_w2(F1("W2")), "F1_b2": lay(F1("b2")),
        "A2_in": lay(A2("W_in")),
        "A2_x": lay(np.concatenate([A2("W_x")[:, 1 + NS:], A2("W_x")[:, 1:1 + NS], A2("W_x")[:, :1]], axis=1).reshape(-1, P, XR).transpose(1, 0, 2)),
        "A2_dt": lay(A2("W_dt")),
        "A2_out": lay(A2("W_out").reshape(-1, P, D).transpose(1, 0, 2)),
        "A2_cols": lay(np.concatenate([A2("conv_w").reshape(-1, CONV)] + [A2(n).reshape(-1, 1) for n in ("conv_b", "b_dt", "D_param")],
                                      axis=1).reshape(-1, P, CONV + 3).transpose(1, 0, 2)),
        "A2_A": lay(A2("A_log").reshape(-1, P, NS).transpose(1, 0, 2)),
        "F2_router": lay(F2("gate_w").T),
        "F2_w1": expert_w1(F2("w1"), F2("b1")), "F2_w2": expert_w2(F2("w2")), "F2_b2": lay(F2("b2")),
        "A3_w": lay(np.concatenate([A3(n).T for n in ("Wq", "Wk", "Wv", "Wo")], axis=1)),
        "A3_cols": lay(np.stack([A3(n) for n in ("bq", "bk", "bv", "bo")], axis=1)),
        "F3_gate": lay(F3("w_gate")), "F3_up": lay(F3("w_up")), "F3_down": lay(F3("w_down")),
    }
    nc = bacc.Bacc("TRN2", target_bir_lowering=False, num_devices=1)
    aps = {n: nc.dram_tensor(f"in_{n}", v.shape, mybir.dt.from_np(v.dtype), kind="ExternalInput").ap() for n, v in a.items()}
    out = nc.dram_tensor("out", (D, N), F32, kind="ExternalOutput").ap()
    scratch = lambda name, shape, dt=F32: nc.dram_tensor(name, shape, dt, kind="Internal").ap()
    program(nc, aps, out, scratch)
    r = run(nc, [{f"in_{n}": v for n, v in a.items()}], core_ids=[0])
    return lay(r.results[0]["out"].T).reshape(g["L0_attn_x"].shape)
```
